# Optimizing a Trainium2 kernel written in Bass

```python
import numpy as np
import jax
import jax.numpy as jnp

def _softmax(x, axis=-1):
    return jax.nn.softmax(x, axis=axis)

def _gelu(x):
    return jax.nn.gelu(x, approximate=True)

def _silu(x):
    return jax.nn.silu(x)

def _sigmoid(x):
    return jax.nn.sigmoid(x)

def _layernorm(x, axis=-1, eps=1e-05):
    m = jnp.mean(x, axis=axis, keepdims=True)
    v = jnp.var(x, axis=axis, keepdims=True)
    return (x - m) / jnp.sqrt(v + eps)

def _scatter_add(tgt, idx, src, axis=0):
    return tgt.at[idx].add(src)

def _segment_sum(src, seg, n):
    return jax.ops.segment_sum(src, seg, n)
kernel_name = 'mk_hybrid_d1_jaxref_r8_8fe8f1'

def setup_inputs(seed: int=0):
    np.random.seed(seed)
    _w = jnp.asarray

    def _L0_attn_a_setup():
        import jax, jax.numpy as jnp
        import numpy as np
        D_MODEL = 128
        N_HEADS = 4
        KEY_DIM = 128
        VALUE_DIM = 256
        DK = KEY_DIM // N_HEADS
        DV = VALUE_DIM // N_HEADS
        LOW_RANK = 16
        GATE_NORM = 16.0
        EPS = 1e-05

        def _gla_scan(q, k, v, gk):
            B, H, L, dk = q.shape
            dv = v.shape[-1]
            qs = jnp.moveaxis(q, 2, 0)
            ks_ = jnp.moveaxis(k, 2, 0)
            vs = jnp.moveaxis(v, 2, 0)
            gs = jnp.moveaxis(gk, 2, 0)

            def step(S, inp):
                q_t, k_t, v_t, g_t = inp
                S = S * jnp.exp(g_t)[..., None] + k_t[..., None] * v_t[..., None, :]
                o_t = jnp.einsum('bhk,bhkv->bhv', q_t, S)
                return (S, o_t)
            S0 = jnp.zeros((B, H, dk, dv), q.dtype)
            _, os = jax.lax.scan(step, S0, (qs, ks_, vs, gs))
            return jnp.moveaxis(os, 0, 2)
        key = jax.random.key(seed)
        ks = jax.random.split(key, 10)
        B, L = (2, 256)
        gain = 2.0 ** (-2.5)

        def xavier(k, shape, g=gain):
            fan_in, fan_out = (shape[0], shape[1])
            a = g * np.sqrt(6.0 / (fan_in + fan_out))
            return jax.random.uniform(k, shape, jnp.float32, -a, a)
        return {'x': jax.random.normal(ks[0], (B, L, D_MODEL), jnp.float32), 'Wq': xavier(ks[1], (D_MODEL, KEY_DIM)), 'Wk': xavier(ks[2], (D_MODEL, KEY_DIM)), 'Wv': xavier(ks[3], (D_MODEL, VALUE_DIM)), 'Wg': xavier(ks[4], (D_MODEL, VALUE_DIM)), 'gk_w1': xavier(ks[5], (D_MODEL, LOW_RANK)), 'gk_w2': xavier(ks[6], (LOW_RANK, KEY_DIM)), 'gk_b2': jnp.zeros((KEY_DIM,), jnp.float32), 'g_norm_w': jnp.ones((DV,), jnp.float32), 'Wo': xavier(ks[7], (VALUE_DIM, D_MODEL))}
    _L0_attn_a_in = _L0_attn_a_setup()

    def _L0_attn_b_setup():
        import jax, jax.numpy as jnp
        import numpy as np
        LN_EPS = 1e-05
        NEG_INF = -1e+38

        def _layer_norm(x, g, b):
            mu = x.mean(-1, keepdims=True)
            var = ((x - mu) ** 2).mean(-1, keepdims=True)
            return (x - mu) * jax.lax.rsqrt(var + LN_EPS) * g + b

        def _wkv(w, u, k, v):
            B, T, C = k.shape
            kt = jnp.swapaxes(k, 0, 1)
            vt = jnp.swapaxes(v, 0, 1)
            aa0 = jnp.zeros((B, C), k.dtype)
            bb0 = jnp.zeros((B, C), k.dtype)
            pp0 = jnp.full((B, C), NEG_INF, k.dtype)

            def step(carry, inp):
                aa, bb, pp = carry
                kk, vv = inp
                p = jnp.maximum(pp, u + kk)
                e1 = jnp.exp(pp - p)
                e2 = jnp.exp(u + kk - p)
                y = (e1 * aa + e2 * vv) / (e1 + e2)
                p2 = jnp.maximum(pp + w, w + kk)
                e1u = jnp.exp(pp + w - p2)
                e2u = jnp.exp(w + kk - p2)
                aa2 = e1u * aa + e2u * vv
                bb2 = e1u + e2u
                pp2 = p2 + jnp.log(bb2)
                return ((aa2, bb2, pp2), y)
            _, ys = jax.lax.scan(step, (aa0, bb0, pp0), (kt, vt))
            return jnp.swapaxes(ys, 0, 1)

        def _shift(h):
            return jnp.pad(h[:, :-1, :], ((0, 0), (1, 0), (0, 0)))
        key = jax.random.key(seed)
        B, T, C = (8, 256, 128)
        ks = jax.random.split(key, 12)
        s = 0.02
        return {'x': jax.random.normal(ks[0], (B, T, C), jnp.float32), 'time_decay': jax.random.normal(ks[1], (C,), jnp.float32) * 0.01, 'time_first': jax.random.normal(ks[2], (C,), jnp.float32) * 0.01, 'w_tk': jax.random.normal(ks[3], (C, C), jnp.float32) * s, 'w_tv': jax.random.normal(ks[4], (C, C), jnp.float32) * s, 'w_tr': jax.random.normal(ks[5], (C, C), jnp.float32) * s, 'w_ck': jax.random.normal(ks[6], (C, 4 * C), jnp.float32) * s, 'w_cv': jax.random.normal(ks[7], (4 * C, C), jnp.float32) * s, 'w_cr': jax.random.normal(ks[8], (C, C), jnp.float32) * s, 'ln1_g': jnp.ones((C,), jnp.float32), 'ln1_b': jnp.zeros((C,), jnp.float32), 'ln2_g': jnp.ones((C,), jnp.float32), 'ln2_b': jnp.zeros((C,), jnp.float32), 'mix_k': jnp.ones((1, 1, C), jnp.float32), 'mix_v': jnp.ones((1, 1, C), jnp.float32), 'mix_r': jnp.ones((1, 1, C), jnp.float32), 'cmix_k': jnp.ones((1, 1, C), jnp.float32), 'cmix_r': jnp.ones((1, 1, C), jnp.float32)}
    _L0_attn_b_in = _L0_attn_b_setup()

    def _L0_ffn_setup():
        import jax, jax.numpy as jnp
        import numpy as np
        D = 128
        H = 4
        DF = 512
        E = 8
        EPS = 1e-05

        def _layer_norm(x, g, b):
            mu = jnp.mean(x, axis=-1, keepdims=True)
            var = jnp.mean(jnp.square(x - mu), axis=-1, keepdims=True)
            return (x - mu) * jax.lax.rsqrt(var + EPS) * g + b

        def _mha(x, Wqkv, bqkv, Wo, bo):
            S, B, _ = x.shape
            hd = D // H
            qkv = x @ Wqkv.T + bqkv
            q, k, v = jnp.split(qkv, 3, axis=-1)
            to_heads = lambda t: t.reshape(S, B, H, hd).transpose(1, 2, 0, 3)
            q, k, v = (to_heads(q), to_heads(k), to_heads(v))
            scores = jnp.einsum('bhqd,bhkd->bhqk', q, k) * (1.0 / np.sqrt(hd))
            att = jax.nn.softmax(scores, axis=-1)
            o = jnp.einsum('bhqk,bhkd->bhqd', att, v)
            o = o.transpose(2, 0, 1, 3).reshape(S, B, D)
            return o @ Wo.T + bo

        def _moe(x, Wg, W1, b1, W2, b2):
            S, B, _ = x.shape
            xf = x.reshape(S * B, D)
            logits = xf @ Wg.T
            idx = jnp.argmax(logits, axis=-1)
            out = jnp.zeros_like(xf)
            for e in range(E):
                m = (idx == e)[:, None].astype(xf.dtype)
                h = jax.nn.relu(xf @ W1[e] + b1[e])
                out = out + m * (h @ W2[e] + b2[e])
            return out.reshape(S, B, D)
        key = jax.random.key(seed)
        ks = jax.random.split(key, 16)
        S, B = (64, 8)
        s = lambda k, shape, fan: jax.random.normal(k, shape, jnp.float32) * (1.0 / np.sqrt(fan))
        return {'x': jax.random.normal(ks[0], (S, B, D), jnp.float32), 'Wqkv': s(ks[1], (3 * D, D), D), 'bqkv': jnp.zeros((3 * D,), jnp.float32), 'Wo': s(ks[2], (D, D), D), 'bo': jnp.zeros((D,), jnp.float32), 'g1': jnp.ones((D,), jnp.float32), 'be1': jnp.zeros((D,), jnp.float32), 'g2': jnp.ones((D,), jnp.float32), 'be2': jnp.zeros((D,), jnp.float32), 'Wg': s(ks[3], (E, D), D), 'W1': s(ks[4], (E, D, DF), D), 'b1': jnp.zeros((E, DF), jnp.float32), 'W2': s(ks[5], (E, DF, D), DF), 'b2': jnp.zeros((E, D), jnp.float32)}
    _L0_ffn_in = _L0_ffn_setup()
    _d = {'L0_attn_a_x': _L0_attn_a_in['x'], 'L0_attn_a_Wq': _L0_attn_a_in['Wq'], 'L0_attn_a_Wk': _L0_attn_a_in['Wk'], 'L0_attn_a_Wv': _L0_attn_a_in['Wv'], 'L0_attn_a_Wg': _L0_attn_a_in['Wg'], 'L0_attn_a_gk_w1': _L0_attn_a_in['gk_w1'], 'L0_attn_a_gk_w2': _L0_attn_a_in['gk_w2'], 'L0_attn_a_gk_b2': _L0_attn_a_in['gk_b2'], 'L0_attn_a_g_norm_w': _L0_attn_a_in['g_norm_w'], 'L0_attn_a_Wo': _L0_attn_a_in['Wo'], 'L0_attn_b_time_decay': _L0_attn_b_in['time_decay'], 'L0_attn_b_time_first': _L0_attn_b_in['time_first'], 'L0_attn_b_w_tk': _L0_attn_b_in['w_tk'], 'L0_attn_b_w_tv': _L0_attn_b_in['w_tv'], 'L0_attn_b_w_tr': _L0_attn_b_in['w_tr'], 'L0_attn_b_w_ck': _L0_attn_b_in['w_ck'], 'L0_attn_b_w_cv': _L0_attn_b_in['w_cv'], 'L0_attn_b_w_cr': _L0_attn_b_in['w_cr'], 'L0_attn_b_ln1_g': _L0_attn_b_in['ln1_g'], 'L0_attn_b_ln1_b': _L0_attn_b_in['ln1_b'], 'L0_attn_b_ln2_g': _L0_attn_b_in['ln2_g'], 'L0_attn_b_ln2_b': _L0_attn_b_in['ln2_b'], 'L0_attn_b_mix_k': _L0_attn_b_in['mix_k'], 'L0_attn_b_mix_v': _L0_attn_b_in['mix_v'], 'L0_attn_b_mix_r': _L0_attn_b_in['mix_r'], 'L0_attn_b_cmix_k': _L0_attn_b_in['cmix_k'], 'L0_attn_b_cmix_r': _L0_attn_b_in['cmix_r'], 'L0_ffn_Wqkv': _L0_ffn_in['Wqkv'], 'L0_ffn_bqkv': _L0_ffn_in['bqkv'], 'L0_ffn_Wo': _L0_ffn_in['Wo'], 'L0_ffn_bo': _L0_ffn_in['bo'], 'L0_ffn_g1': _L0_ffn_in['g1'], 'L0_ffn_be1': _L0_ffn_in['be1'], 'L0_ffn_g2': _L0_ffn_in['g2'], 'L0_ffn_be2': _L0_ffn_in['be2'], 'L0_ffn_Wg': _L0_ffn_in['Wg'], 'L0_ffn_W1': _L0_ffn_in['W1'], 'L0_ffn_b1': _L0_ffn_in['b1'], 'L0_ffn_W2': _L0_ffn_in['W2'], 'L0_ffn_b2': _L0_ffn_in['b2']}
    _x0 = _d['L0_attn_a_x']
    _d['L0_attn_a_x'] = jax.random.normal(jax.random.fold_in(jax.random.key(seed), 1), (16, 256, 128), dtype=_x0.dtype)
    del _x0
    return _d

def reference(L0_attn_a_x, L0_attn_a_Wq, L0_attn_a_Wk, L0_attn_a_Wv, L0_attn_a_Wg, L0_attn_a_gk_w1, L0_attn_a_gk_w2, L0_attn_a_gk_b2, L0_attn_a_g_norm_w, L0_attn_a_Wo, L0_attn_b_time_decay, L0_attn_b_time_first, L0_attn_b_w_tk, L0_attn_b_w_tv, L0_attn_b_w_tr, L0_attn_b_w_ck, L0_attn_b_w_cv, L0_attn_b_w_cr, L0_attn_b_ln1_g, L0_attn_b_ln1_b, L0_attn_b_ln2_g, L0_attn_b_ln2_b, L0_attn_b_mix_k, L0_attn_b_mix_v, L0_attn_b_mix_r, L0_attn_b_cmix_k, L0_attn_b_cmix_r, L0_ffn_Wqkv, L0_ffn_bqkv, L0_ffn_Wo, L0_ffn_bo, L0_ffn_g1, L0_ffn_be1, L0_ffn_g2, L0_ffn_be2, L0_ffn_Wg, L0_ffn_W1, L0_ffn_b1, L0_ffn_W2, L0_ffn_b2):

    def _L0_attn_a_ref(x, Wq, Wk, Wv, Wg, gk_w1, gk_w2, gk_b2, g_norm_w, Wo):
        import jax, jax.numpy as jnp
        import numpy as np
        D_MODEL = 128
        N_HEADS = 4
        KEY_DIM = 128
        VALUE_DIM = 256
        DK = KEY_DIM // N_HEADS
        DV = VALUE_DIM // N_HEADS
        LOW_RANK = 16
        GATE_NORM = 16.0
        EPS = 1e-05

        def _gla_scan(q, k, v, gk):
            B, H, L, dk = q.shape
            dv = v.shape[-1]
            qs = jnp.moveaxis(q, 2, 0)
            ks_ = jnp.moveaxis(k, 2, 0)
            vs = jnp.moveaxis(v, 2, 0)
            gs = jnp.moveaxis(gk, 2, 0)

            def step(S, inp):
                q_t, k_t, v_t, g_t = inp
                S = S * jnp.exp(g_t)[..., None] + k_t[..., None] * v_t[..., None, :]
                o_t = jnp.einsum('bhk,bhkv->bhv', q_t, S)
                return (S, o_t)
            S0 = jnp.zeros((B, H, dk, dv), q.dtype)
            _, os = jax.lax.scan(step, S0, (qs, ks_, vs, gs))
            return jnp.moveaxis(os, 0, 2)
        B, L, _ = x.shape
        scale = DK ** (-0.5)

        def heads(t, d):
            return t.reshape(B, L, N_HEADS, d).transpose(0, 2, 1, 3)
        q = heads(x @ Wq, DK) * scale
        k = heads(x @ Wk, DK)
        v = heads(x @ Wv, DV)
        gk = heads(jax.nn.log_sigmoid(x @ gk_w1 @ gk_w2 + gk_b2) / GATE_NORM, DK)
        o = _gla_scan(q, k, v, gk)
        o = o.transpose(0, 2, 1, 3)
        g = (x @ Wg).reshape(B, L, N_HEADS, DV)
        rms = o * jax.lax.rsqrt(jnp.mean(o * o, axis=-1, keepdims=True) + EPS)
        o = rms * g_norm_w * (g * jax.nn.sigmoid(g))
        o = o.reshape(B, L, VALUE_DIM)
        return o @ Wo

    def _L0_attn_b_ref(x, time_decay, time_first, w_tk, w_tv, w_tr, w_ck, w_cv, w_cr, ln1_g, ln1_b, ln2_g, ln2_b, mix_k, mix_v, mix_r, cmix_k, cmix_r):
        import jax, jax.numpy as jnp
        import numpy as np
        LN_EPS = 1e-05
        NEG_INF = -1e+38

        def _layer_norm(x, g, b):
            mu = x.mean(-1, keepdims=True)
            var = ((x - mu) ** 2).mean(-1, keepdims=True)
            return (x - mu) * jax.lax.rsqrt(var + LN_EPS) * g + b

        def _wkv(w, u, k, v):
            B, T, C = k.shape
            kt = jnp.swapaxes(k, 0, 1)
            vt = jnp.swapaxes(v, 0, 1)
            aa0 = jnp.zeros((B, C), k.dtype)
            bb0 = jnp.zeros((B, C), k.dtype)
            pp0 = jnp.full((B, C), NEG_INF, k.dtype)

            def step(carry, inp):
                aa, bb, pp = carry
                kk, vv = inp
                p = jnp.maximum(pp, u + kk)
                e1 = jnp.exp(pp - p)
                e2 = jnp.exp(u + kk - p)
                y = (e1 * aa + e2 * vv) / (e1 + e2)
                p2 = jnp.maximum(pp + w, w + kk)
                e1u = jnp.exp(pp + w - p2)
                e2u = jnp.exp(w + kk - p2)
                aa2 = e1u * aa + e2u * vv
                bb2 = e1u + e2u
                pp2 = p2 + jnp.log(bb2)
                return ((aa2, bb2, pp2), y)
            _, ys = jax.lax.scan(step, (aa0, bb0, pp0), (kt, vt))
            return jnp.swapaxes(ys, 0, 1)

        def _shift(h):
            return jnp.pad(h[:, :-1, :], ((0, 0), (1, 0), (0, 0)))
        h = _layer_norm(x, ln1_g, ln1_b)
        hp = _shift(h)
        xk = h * mix_k + hp * (1.0 - mix_k)
        xv = h * mix_v + hp * (1.0 - mix_v)
        xr = h * mix_r + hp * (1.0 - mix_r)
        k = xk @ w_tk
        v = xv @ w_tv
        r = jax.nn.sigmoid(xr @ w_tr)
        y = _wkv(time_decay, time_first, k, v)
        x = x + r * y
        h2 = _layer_norm(x, ln2_g, ln2_b)
        hp2 = _shift(h2)
        ck = h2 * cmix_k + hp2 * (1.0 - cmix_k)
        cr = h2 * cmix_r + hp2 * (1.0 - cmix_r)
        kk = jnp.square(jax.nn.relu(ck @ w_ck))
        x = x + jax.nn.sigmoid(cr @ w_cr) * (kk @ w_cv)
        return x

    def _L0_ffn_ref(x, Wqkv, bqkv, Wo, bo, g1, be1, g2, be2, Wg, W1, b1, W2, b2):
        import jax, jax.numpy as jnp
        import numpy as np
        D = 128
        H = 4
        DF = 512
        E = 8
        EPS = 1e-05

        def _layer_norm(x, g, b):
            mu = jnp.mean(x, axis=-1, keepdims=True)
            var = jnp.mean(jnp.square(x - mu), axis=-1, keepdims=True)
            return (x - mu) * jax.lax.rsqrt(var + EPS) * g + b

        def _mha(x, Wqkv, bqkv, Wo, bo):
            S, B, _ = x.shape
            hd = D // H
            qkv = x @ Wqkv.T + bqkv
            q, k, v = jnp.split(qkv, 3, axis=-1)
            to_heads = lambda t: t.reshape(S, B, H, hd).transpose(1, 2, 0, 3)
            q, k, v = (to_heads(q), to_heads(k), to_heads(v))
            scores = jnp.einsum('bhqd,bhkd->bhqk', q, k) * (1.0 / np.sqrt(hd))
            att = jax.nn.softmax(scores, axis=-1)
            o = jnp.einsum('bhqk,bhkd->bhqd', att, v)
            o = o.transpose(2, 0, 1, 3).reshape(S, B, D)
            return o @ Wo.T + bo

        def _moe(x, Wg, W1, b1, W2, b2):
            S, B, _ = x.shape
            xf = x.reshape(S * B, D)
            logits = xf @ Wg.T
            idx = jnp.argmax(logits, axis=-1)
            out = jnp.zeros_like(xf)
            for e in range(E):
                m = (idx == e)[:, None].astype(xf.dtype)
                h = jax.nn.relu(xf @ W1[e] + b1[e])
                out = out + m * (h @ W2[e] + b2[e])
            return out.reshape(S, B, D)
        y = _layer_norm(x + _mha(x, Wqkv, bqkv, Wo, bo), g1, be1)
        z = _layer_norm(y + _moe(y, Wg, W1, b1, W2, b2), g2, be2)
        return z
    x = L0_attn_a_x
    x = x + _L0_attn_a_ref(_layernorm(x, axis=-1), L0_attn_a_Wq, L0_attn_a_Wk, L0_attn_a_Wv, L0_attn_a_Wg, L0_attn_a_gk_w1, L0_attn_a_gk_w2, L0_attn_a_gk_b2, L0_attn_a_g_norm_w, L0_attn_a_Wo)
    x = x + _L0_ffn_ref(_layernorm(x, axis=-1), L0_ffn_Wqkv, L0_ffn_bqkv, L0_ffn_Wo, L0_ffn_bo, L0_ffn_g1, L0_ffn_be1, L0_ffn_g2, L0_ffn_be2, L0_ffn_Wg, L0_ffn_W1, L0_ffn_b1, L0_ffn_W2, L0_ffn_b2)
    x = x + _L0_attn_b_ref(_layernorm(x, axis=-1), L0_attn_b_time_decay, L0_attn_b_time_first, L0_attn_b_w_tk, L0_attn_b_w_tv, L0_attn_b_w_tr, L0_attn_b_w_ck, L0_attn_b_w_cv, L0_attn_b_w_cr, L0_attn_b_ln1_g, L0_attn_b_ln1_b, L0_attn_b_ln2_g, L0_attn_b_ln2_b, L0_attn_b_mix_k, L0_attn_b_mix_v, L0_attn_b_mix_r, L0_attn_b_cmix_k, L0_attn_b_cmix_r)
    x = x + _L0_ffn_ref(_layernorm(x, axis=-1), L0_ffn_Wqkv, L0_ffn_bqkv, L0_ffn_Wo, L0_ffn_bo, L0_ffn_g1, L0_ffn_be1, L0_ffn_g2, L0_ffn_be2, L0_ffn_Wg, L0_ffn_W1, L0_ffn_b1, L0_ffn_W2, L0_ffn_b2)
    return x

_drawn_inputs = setup_inputs


def setup_inputs(seed=0):
    import zlib

    import numpy as np

    out = dict(_drawn_inputs(seed))
    spreads = {'L0_attn_a_gk_b2': (0.0, 0.72),
     'L0_attn_a_g_norm_w': (1.0, 0.6),
     'L0_attn_b_ln1_g': (1.0, 0.6),
     'L0_attn_b_ln1_b': (0.0, 0.1),
     'L0_attn_b_ln2_g': (1.0, 0.6),
     'L0_attn_b_ln2_b': (0.0, 0.8),
     'L0_attn_b_mix_k': (1.0, 0.6),
     'L0_attn_b_mix_v': (1.0, 0.6),
     'L0_attn_b_mix_r': (1.0, 0.6),
     'L0_attn_b_cmix_k': (1.0, 0.6),
     'L0_attn_b_cmix_r': (1.0, 0.6),
     'L0_ffn_bqkv': (0.0, 0.1),
     'L0_ffn_bo': (0.0, 0.1),
     'L0_ffn_g1': (1.0, 0.2),
     'L0_ffn_be1': (0.0, 0.1),
     'L0_ffn_g2': (1.0, 0.2),
     'L0_ffn_be2': (0.0, 0.1),
     'L0_ffn_b1': (0.0, 0.1),
     'L0_ffn_b2': (0.0, 0.1)}
    factors = {'L0_attn_a_gk_w1': 8.0,
     'L0_attn_a_gk_w2': 23.785,
     'L0_attn_b_time_decay': 4.851,
     'L0_attn_b_time_first': 64.0,
     'L0_attn_b_w_tk': 2.675,
     'L0_attn_b_w_tr': 3.652,
     'L0_attn_b_w_ck': 4.673,
     'L0_attn_b_w_cv': 4.598,
     'L0_attn_b_w_cr': 8.0}
    for name, (base, spread) in spreads.items():
        noise = np.random.default_rng([zlib.crc32(name.encode()), seed]).standard_normal(out[name].shape)
        drawn = base * np.exp(spread * noise) if base else spread * noise
        out[name] = jnp.asarray(drawn.astype(out[name].dtype))
    for name, factor in factors.items():
        out[name] = (out[name] * factor).astype(out[name].dtype)
    return out
```

```python
from contextlib import ExitStack
import numpy as np
import concourse.bass as bass
import concourse.mybir as mybir

F32, I32, BF16 = mybir.dt.float32, mybir.dt.int32, mybir.dt.bfloat16
ALU, ACT, AX = mybir.AluOpType, mybir.ActivationFunctionType, mybir.AxisListType
P, D, SEQ, L = 128, 128, 16, 256
EPS = 1e-5
EXP_LN = "natural_log_exp_and_others"
SIG_CLAMP = 40.0

class PhaseSemaphores:
    def __init__(self, nc, ctx, tag):
        self.nc, self.tag, self.sems = nc, tag, []
        ctx.callback(self.clear)

    def __call__(self, name):
        self.sems.append(self.nc.alloc_semaphore(name=self.tag + name))
        return self.sems[-1]

    def clear(self):
        self.nc.clear_and_free_semaphores(self.sems)
        self.nc.all_engine_barrier()


def wait_apart(eng, apart, sem, value):
    eng.wait_ge(sem, value)
    if apart is not None and not isinstance(value, int):
        eng.sem_inc(apart, 1)


class Chain:
    def __init__(self, eng, sem, apart=None):
        self.eng, self.sem, self.apart, self.base, self.n = eng, sem, apart, 0, 0

    def enter(self, base):
        self.base, self.n = base, 0

    def mark(self, ins):
        self.n += 1
        ins.then_inc(self.sem, 1)
        return self.n

    def need(self, n, apart=None):
        wait_apart(self.eng, apart or self.apart, self.sem, self.base + n)

    def link(self, ins, apart=None):
        self.need(self.mark(ins), apart)

    def leave(self, steps):
        assert self.n == steps, (self.n, steps)


def pipelined(eng, chain, turns, front_steps, turn_steps, front, turn):
    front(0)
    chain.leave(front_steps)
    with eng.Fori(0, turns - 1) as i:
        chain.enter(i * turn_steps + front_steps)
        turn(i, True)
        chain.leave(turn_steps)
    chain.enter((turns - 1) * turn_steps + front_steps)
    turn(turns - 1, False)


STAT_STEPS = 5


def stats_to_mean_var(nc, dve, sem, st, mv, var_eps, base=0):
    def step(n, ins):
        ins.then_inc(sem, 1)
        dve.wait_ge(sem, base + n)
    step(1, nc.vector.tensor_tensor(mv[:, :, 0], st[:, :, 1], st[:, :, 4], ALU.subtract))
    step(2, nc.vector.scalar_tensor_tensor(mv[:, :, 1], mv[:, :, 0], 0.25, mv[:, :, 0], ALU.mult, ALU.mult))
    step(3, nc.vector.scalar_tensor_tensor(var_eps, st[:, :, 2], 1.0 / 128, mv[:, :, 1], ALU.mult, ALU.add))
    step(4, nc.vector.scalar_tensor_tensor(mv[:, :, 1], st[:, :, 5], 1.0 / 128, var_eps, ALU.mult, ALU.add))
    nc.vector.tensor_scalar(var_eps, mv[:, :, 1], EPS, None, ALU.add)
    nc.vector.scalar_tensor_tensor(mv[:, :, 0], mv[:, :, 0], 0.5, st[:, :, 4], ALU.mult, ALU.add).then_inc(sem, 1)


CONST_COLS = {}
EXPERTS, DF = 8, 512
REGION = SEQ * L + P
BLOCKS = SEQ * L // P + EXPERTS
ROWS = EXPERTS * REGION + EXPERTS * P


def const_array():
    p = np.arange(P)
    e = np.arange(EXPERTS)
    cols = []
    CONST_COLS.clear()

    def put(name, a):
        CONST_COLS[name] = (sum(c.shape[1] for c in cols), a.shape[1])
        cols.append(a.astype(np.float32))

    row = lambda v: np.broadcast_to(np.asarray(v)[None, :], (P, len(v)))
    put("ident", np.eye(P))
    put("causal", p[:, None] <= p[None, :])
    put("strict", p[:, None] < p[None, :])
    put("ones", np.ones((P, 256)))
    put("headmask", (p[:, None] // 32) == (np.arange(256)[None, :] // 64))
    put("pairmask", np.where((p[:, None] // 64) == (np.arange(32)[None, :] // 16), 0.0, -1e30))
    put("neg_half", np.full((P, 32), -0.5))
    put("expert_less_8", row(e - EXPERTS))
    put("region_start", row(e * REGION))
    put("region_end", row((e + 1) * REGION))
    put("block", row(np.arange(BLOCKS)))
    return np.concatenate(cols, 1)


def load_consts(nc, ctx, io):
    const_array()
    t = ctx.enter_context(nc.sbuf_tensor("consts", list(io["consts"].shape), F32))
    s = ctx.enter_context(nc.semaphore("consts_loaded"))
    C = {k: t[:, a:a + n] for k, (a, n) in CONST_COLS.items()}
    C["ones_row"] = C["ones"]
    C["causal4"] = C["causal"].unsqueeze(1).to_broadcast([P, 4, P])
    C["loaded"], C["loads"], C["tensor"] = s, 16, t
    return C


def gla_phase(nc, io, C, x_dram, x1_dram):
    UNITS, PAIR, CH = 16, 2, 2
    GATE, SCALE, CLAMP = 1.0 / 16.0, 32.0 ** -0.5, 16.0 * 80.0
    DVE_FRONT, DVE_TURN, ACT_FRONT, ACT_TURN, POOL_TURN = 10, 12, 4, 8, 10
    with ExitStack() as ctx:
        sb = lambda name, shape: ctx.enter_context(nc.sbuf_tensor("gla_" + name, shape, F32))
        sem = lambda name: ctx.enter_context(nc.semaphore("gla_" + name))
        x = sb("x", [P, UNITS * CH, D])
        wqk, wvg, w1t, w2, w12 = sb("wqk", [P, 256]), sb("wvg", [P, 512]), sb("w1t", [16, P]), sb("w2", [16, P]), sb("w12", [P, P])
        wo, wn, b2 = sb("wo", [P, 2, D]), sb("wn", [P, 1]), sb("b2", [P, 1])
        won = sb("won", [P, 2, D])
        two = range(PAIR)
        h = [sb(f"h{j}", [P, CH, D]) for j in two]
        hT = [sb(f"hT{j}", [P, L]) for j in two]
        za = [sb(f"za{j}", [P, L]) for j in two]
        ze = [sb(f"ze{j}", [P, L]) for j in two]
        zl = [sb(f"zl{j}", [P, L]) for j in two]
        zm = [sb(f"zm{j}", [P, L]) for j in two]
        zg = [sb(f"zg{j}", [P, L]) for j in two]
        cum = [sb(f"cum{j}", [P, L]) for j in two]
        dl = [sb(f"dl{j}", [P, L]) for j in two]
        dc = [sb(f"dc{j}", [P, L]) for j in two]
        dm = [sb(f"dm{j}", [P, 1]) for j in two]
        dS = [sb(f"dS{j}", [P, 1]) for j in two]
        eq = [sb(f"eq{j}", [P, L]) for j in two]
        ek = [sb(f"ek{j}", [P, L]) for j in two]
        qt = [sb(f"qt{j}", [P, L]) for j in two]
        kt = [sb(f"kt{j}", [P, L]) for j in two]
        ktok = [sb(f"ktok{j}", [P, P]) for j in two]
        v = [sb(f"v{j}", [P, CH, 256]) for j in two]
        gc = [sb(f"gc{j}", [P, CH, 256]) for j in two]
        ge = [sb(f"ge{j}", [P, CH, 256]) for j in two]
        gl = [sb(f"gl{j}", [P, CH, 256]) for j in two]
        gs = [sb(f"gs{j}", [P, CH, 256]) for j in two]
        gg = [sb(f"gg{j}", [P, CH, 256]) for j in two]
        am = [sb(f"am{j}", [P, CH, 4, P]) for j in two]
        S = [sb(f"S{j}", [P, 256]) for j in two]
        sq = [sb(f"sq{j}", [P, CH * 256]) for j in two]
        ss = [sb(f"ss{j}", [P, 8]) for j in two]
        sv = [sb(f"sv{j}", [P, 8]) for j in two]
        rr = [sb(f"rr{j}", [P, 8]) for j in two]
        og = [sb(f"og{j}", [P, CH, 256]) for j in two]
        on = [sb(f"on{j}", [P, CH, 256]) for j in two]
        oT = [sb(f"oT{j}", [P, 4, P]) for j in two]
        mvs, ves, rstd = sb("mvs", [P, UNITS * CH, 2]), sb("ves", [P, UNITS * CH]), sb("rstd", [P, UNITS * CH])
        sts = sb("sts", [P, UNITS * CH, 6])
        qx = [sb(f"qx{j}", [P, CH, 4, P]) for j in two]
        ps = ctx.enter_context(nc.psum_tensor("gla_ps", [P, 8, 512], F32))
        bank = lambda j, b: ps[:, 4 * j + b, :]
        hT_ps = [bank(j, 0)[:, 0:256] for j in two]
        z_ps = [bank(j, 0)[:, 256:512] for j in two]
        q_ps = [bank(j, 1)[:, 0:256] for j in two]
        k_ps = [bank(j, 1)[:, 256:512] for j in two]
        a_ps = lambda j, c: bank(j, 1 - c)
        vg_ps = [ps[:, 4 * j + 2:4 * j + 4, :] for j in two]
        kt_ps = [bank(j, 2)[:, 0:P] for j in two]
        u_ps = [bank(j, 2)[:, 256:512] for j in two]
        oT_ps = [bank(j, 2) for j in two]
        o_ps = [bank(j, 3) for j in two]
        out_ps = [bank(j, 3)[:, 0:256] for j in two]

        s_x, s_w = [sem(f"x_loaded{k}") for k in range(4)], sem("weights_loaded")
        s_w12, s_w12c, s_won = sem("w12_product"), sem("w12_copied"), sem("wo_scaled")
        s_stat, s_ve, s_rstd, s_h = sem("stats"), sem("var_eps"), sem("rstd"), sem("normed")
        s_hTp, s_hT, s_z, s_qk, s_vg = (sem("hT_psum"), sem("hT_copied"), sem("gate_product"), sem("qk_product"),
                                        sem("vg_product"))
        s_v, s_gc, s_zl, s_dec, s_e, s_gs, s_gg = (sem("v_copied"), sem("g_clamped"), sem("softplus"), sem("decay_ready"),
                                                   sem("decay_exp"), sem("g_sigmoid"), sem("g_silu"))
        s_qt, s_ktp, s_ktok, s_a, s_am, s_u, s_S = (sem("qk_decayed"), sem("k_transposed"), sem("k_copied"), sem("scores"),
                                                    sem("scores_masked"), sem("state_product"), sem("state_ready"))
        s_qz, s_qx, s_bn, s_aggr = sem("qx_zeroed"), sem("qx_ready"), sem("bn_stats"), sem("bn_aggr")
        s_o, s_sq, s_ss, s_rr, s_on = sem("o_product"), sem("o_squared"), sem("o_sums"), sem("o_rstd"), sem("o_gated")
        s_oTp, s_oT, s_out, s_x1, s_st = (sem("oT_psum"), sem("oT_copied"), sem("out_product"), sem("x1_ready"),
                                          sem("x1_stored"))
        c_dve, c_act, c_pool = sem("dve_steps"), sem("act_steps"), sem("pool_steps")
        apart = sem("apart")
        block = ctx.enter_context(nc.Block())

        @block.sync
        def _(sp):
            for dst, src in ((wqk[:, 0:P], io["Wq"]), (wqk[:, P:256], io["Wk"]), (wvg[:, 0:256], io["Wv"]),
                             (wvg[:, 256:512], io["Wg"]), (w1t[:, :], io["gk_w1T"]), (w2[:, :], io["gk_w2"]),
                             (wo[:, :, :], io["Wo_a"].rearrange("(c p) d -> p c d", p=P)),
                             (wn[:, :], io["g_norm_col"]), (b2[:, :], io["gk_b2_col"])):
                sp.dma_start(dst, src).then_inc(s_w, 16)
            for k in range(4):
                sp.dma_start(x[:, 8 * k:8 * k + 8, :],
                             x_dram[4 * k:4 * k + 4].rearrange("s (c p) d -> p (s c) d", p=P)).then_inc(s_x[k], 16)
            with sp.Fori(0, UNITS) as n:
                sp.wait_ge(s_x1, n + 1)
                sp.dma_start(x1_dram[bass.ts(n, 1)].rearrange("s (c p) d -> p (s c) d", p=P),
                             x[:, bass.ts(n, CH), :]).then_inc(s_st, 16)
            sp.wait_ge(s_st, 16 * UNITS)

        units = lambda i: [(j, i * PAIR + j) for j in two]
        TURNS = UNITS // PAIR

        @block.tensor
        def _(pe):
            def to_hT(i):
                for j, n in units(i):
                    pe.wait_ge(s_h, n + 1)
                    for c in range(CH):
                        last = nc.tensor.transpose(hT_ps[j][:, P * c:P * c + P], h[j][:, c, :], C["ident"])
                    last.then_inc(s_hTp, 1)

            def to_zqk(i):
                for j, n in units(i):
                    pe.wait_ge(s_hT, n + 1)
                    nc.tensor.matmul(z_ps[j], w12[:, :], hT[j][:, :], start=True, stop=True).then_inc(s_z, 1)
                    nc.tensor.matmul(q_ps[j], wqk[:, 0:P], hT[j][:, :], start=True, stop=True)
                    nc.tensor.matmul(k_ps[j], wqk[:, P:256], hT[j][:, :], start=True, stop=True).then_inc(s_qk, 1)

            def to_vg(i):
                for j, n in units(i):
                    for c in range(CH):
                        last = nc.tensor.matmul(vg_ps[j][:, c, :], hT[j][:, P * c:P * c + P], wvg[:, :],
                                                start=True, stop=True)
                    last.then_inc(s_vg, 1)

            def front(i):
                to_hT(i)
                to_zqk(i)
                to_vg(i)

            def turn(i, more):
                for j, n in units(i):
                    pe.wait_ge(s_qt, n + 1)
                    pe.wait_ge(s_gc, n + 1)
                    nc.tensor.transpose(kt_ps[j], kt[j][:, 0:P], C["ident"]).then_inc(s_ktp, 1)
                for j, n in units(i):
                    pe.wait_ge(s_qx, n + 1)
                    for c in range(CH):
                        nc.tensor.matmul(a_ps(j, c), kt[j][:, P * c:P * c + P], qx[j][:, c, :, :], start=True,
                                         stop=True).then_inc(s_a, 1)
                for j, n in units(i):
                    pe.wait_ge(s_ktok, n + 1)
                    nc.tensor.matmul(u_ps[j], ktok[j][:, :], v[j][:, 0, :], start=True, stop=True).then_inc(s_u, 1)
                for j, n in units(i):
                    for c in range(CH):
                        pe.wait_ge(s_am, n * CH + c + 1)
                        for hd in range(4):
                            nc.tensor.matmul(o_ps[j][:, 256 * c + 64 * hd:256 * c + 64 * hd + 64], am[j][:, c, hd, :],
                                             v[j][:, c, 64 * hd:64 * hd + 64], start=(c == 0 and hd == 0), stop=False,
                                             skip_group_check=True)
                    pe.wait_ge(s_S, n + 1)
                    nc.tensor.matmul(o_ps[j][:, 256:512], qt[j][:, P:256], S[j][:, :], start=False, stop=True,
                                     skip_group_check=True).then_inc(s_o, 1)
                if more:
                    to_hT(i + 1)
                    to_zqk(i + 1)
                for j, n in units(i):
                    pe.wait_ge(s_on, n + 1)
                    for c in range(CH):
                        for b in range(2):
                            last = nc.tensor.transpose(oT_ps[j][:, P * (2 * c + b):P * (2 * c + b) + P],
                                                       on[j][:, c, P * b:P * b + P], C["ident"])
                    last.then_inc(s_oTp, 1)
                for j, n in units(i):
                    pe.wait_ge(s_oT, n + 1)
                    for c in range(CH):
                        for b in range(2):
                            last = nc.tensor.matmul(out_ps[j][:, P * c:P * c + P], oT[j][:, 2 * c + b, :], won[:, b, :],
                                                    start=(b == 0), stop=(b == 1))
                    last.then_inc(s_out, 1)
                if more:
                    for j, n in units(i):
                        pe.wait_ge(s_x1, n + 1)
                    to_vg(i + 1)

            pe.wait_ge(C["loaded"], C["loads"])
            pe.wait_ge(s_w, 16 * 9)
            nc.tensor.matmul(bank(0, 0)[:, 0:P], w1t[:, :], w2[:, :], start=True, stop=True).then_inc(s_w12, 1)
            pe.wait_ge(s_w12c, 1)
            pipelined(pe, Chain(pe, None), TURNS, 0, 0, front, turn)

        @block.scalar
        def _(act):
            chain = Chain(act, c_act)

            def copy_hT(i):
                for j, n in units(i):
                    act.wait_ge(s_hTp, n + 1)
                    nc.scalar.activation(hT[j][:, :], hT_ps[j], ACT.Copy).then_inc(s_hT, 1)

            def softplus(i):
                for j, n in units(i):
                    act.wait_ge(s_z, n + 1)
                    chain.link(nc.scalar.activation(za[j][:, :], z_ps[j], ACT.Abs, bias=b2[:, :]))
                    chain.link(nc.scalar.activation(ze[j][:, :], za[j][:, :], ACT.Exp, scale=-1.0))
                    nc.scalar.activation(zl[j][:, :], ze[j][:, :], ACT.Ln, bias=1.0).then_inc(s_zl, 1)

            def rest(i):
                for j, n in units(i):
                    act.wait_ge(s_vg, n + 1)
                    nc.scalar.activation(v[j][:, :, :], vg_ps[j][:, :, 0:256], ACT.Copy).then_inc(s_v, 1)
                for j, n in units(i):
                    act.wait_ge(s_dec, n + 1)
                    nc.scalar.activation(eq[j][:, :], dc[j][:, :], ACT.Exp, scale=GATE)
                    nc.scalar.activation(ek[j][:, :], dc[j][:, :], ACT.Exp, scale=-GATE)
                    nc.scalar.activation(dS[j][:, :], dm[j][:, :], ACT.Exp, scale=GATE).then_inc(s_e, 1)

            def front(i):
                copy_hT(i)
                softplus(i)
                rest(i)

            def turn(i, more):
                for j, n in units(i):
                    act.wait_ge(s_ktp, n + 1)
                    nc.scalar.activation(ktok[j][:, :], kt_ps[j], ACT.Copy).then_inc(s_ktok, 1)
                for j, n in units(i):
                    act.wait_ge(s_gc, n + 1)
                    chain.link(nc.scalar.activation(ge[j][:, :, :], gc[j][:, :, :], ACT.Exp, scale=-1.0))
                    chain.link(nc.scalar.activation(gl[j][:, :, :], ge[j][:, :, :], ACT.Ln, bias=1.0))
                    nc.scalar.activation(gs[j][:, :, :], gl[j][:, :, :], ACT.Exp, scale=-1.0).then_inc(s_gs, 1)
                for j, n in units(i):
                    act.wait_ge(s_o, n + 1)
                    nc.scalar.activation(sq[j][:, :], o_ps[j], ACT.Square).then_inc(s_sq, 1)
                if more:
                    copy_hT(i + 1)
                    softplus(i + 1)
                for j, n in units(i):
                    act.wait_ge(s_oTp, n + 1)
                    nc.scalar.activation(oT[j][:, :, :], oT_ps[j], ACT.Copy).then_inc(s_oT, 1)
                if more:
                    rest(i + 1)

            act.preload_act_table_set(EXP_LN)
            act.wait_ge(s_w, 16 * 9)
            pipelined(act, chain, TURNS, ACT_FRONT, ACT_TURN, front, turn)

        @block.gpsimd
        def _(pool):

            chain = Chain(pool, c_pool, apart)
            for j in two:
                nc.gpsimd.memset(qx[j][:, :, :, :], 0.0).then_inc(s_qz, 1)
            wait_apart(pool, apart, s_stat, 1)
            nc.gpsimd.tensor_tensor(rstd[:, :], ves[:, :], C["neg_half"][:, 0:UNITS * CH], ALU.pow).then_inc(s_rstd, 1)
            pool.wait_ge(s_qz, PAIR)
            with pool.Fori(0, TURNS) as i:
                chain.enter(i * POOL_TURN)
                for j, n in units(i):
                    wait_apart(pool, apart, s_qt, n + 1)
                    for hd in range(4):
                        rows = slice(32 * hd, 32 * hd + 32)
                        chain.link(nc.gpsimd.tensor_copy(qx[j][rows, :, hd, :],
                                                         qt[j][rows, :].rearrange("p (c t) -> p c t", c=CH)))
                    pool.sem_inc(s_qx, 1)
                for j, n in units(i):
                    pool.wait_ge(s_gs, n + 1)
                    nc.gpsimd.tensor_tensor(gg[j][:, :, :], gc[j][:, :, :], gs[j][:, :, :], ALU.mult).then_inc(s_gg, 1)
                for j, n in units(i):
                    wait_apart(pool, apart, s_ss, n + 1)
                    chain.link(nc.gpsimd.tensor_scalar(sv[j][:, :], ss[j][:, :], 1.0 / 64, EPS, ALU.mult, ALU.add))
                    nc.gpsimd.tensor_tensor(rr[j][:, :], sv[j][:, :], C["neg_half"][:, 0:8], ALU.pow).then_inc(s_rr, 1)
                chain.leave(POOL_TURN)

        @block.vector
        def _(dve):
            chain = Chain(dve, c_dve)


            def norm(i):
                for j, n in units(i):
                    for c in range(CH):
                        last = nc.vector.tensor_scalar(h[j][:, c, :], x[:, n * CH + c, :], mvs[:, n * CH + c, 0:1],
                                                       rstd[:, bass.ts(n * CH + c, 1)], ALU.subtract, ALU.mult)
                    last.then_inc(s_h, 1)

            def gate(i):
                for j, n in units(i):
                    dve.wait_ge(s_zl, n + 1)
                    chain.link(nc.vector.tensor_scalar(zm[j][:, :], z_ps[j], b2[:, 0:1], 0.0, ALU.add, ALU.min))
                    chain.link(nc.vector.tensor_tensor(zg[j][:, :], zm[j][:, :], zl[j][:, :], ALU.subtract))
                    chain.link(nc.vector.tensor_tensor_scan(cum[j][:, :], C["ones_row"], zg[j][:, :], 0.0, ALU.mult,
                                                            ALU.add))
                    for c in range(CH):
                        mid = cum[j][:, P * c + P // 2 - 1:P * c + P // 2]
                        last = chain.mark(nc.vector.tensor_scalar(dl[j][:, P * c:P * c + P], cum[j][:, P * c:P * c + P],
                                                                  mid, -CLAMP, ALU.subtract, ALU.max))
                    nc.vector.tensor_tensor(dm[j][:, :], cum[j][:, P + P // 2 - 1:P + P // 2],
                                            cum[j][:, P // 2 - 1:P // 2], ALU.subtract)
                    chain.need(last)
                    nc.vector.tensor_scalar(dc[j][:, :], dl[j][:, :], CLAMP, None, ALU.min).then_inc(s_dec, 1)

            def rest(i):
                for j, n in units(i):
                    dve.wait_ge(s_v, n + 1)
                    nc.vector.tensor_scalar(gc[j][:, :, :], vg_ps[j][:, :, 256:512], -SIG_CLAMP, None,
                                            ALU.max).then_inc(s_gc, 1)
                for j, n in units(i):
                    dve.wait_ge(s_e, n + 1)
                    dve.wait_ge(s_qk, n + 1)
                    nc.vector.scalar_tensor_tensor(qt[j][:, :], q_ps[j], SCALE, eq[j][:, :], ALU.mult, ALU.mult)
                    nc.vector.tensor_tensor(kt[j][:, :], k_ps[j], ek[j][:, :], ALU.mult).then_inc(s_qt, 1)

            def front(i):
                norm(i)
                gate(i)
                rest(i)

            def turn(i, more):
                if more:
                    norm(i + 1)
                for j, n in units(i):
                    for c in range(CH):
                        dve.wait_ge(s_a, n * CH + c + 1)
                        nc.vector.tensor_tensor(am[j][:, c, :, :], a_ps(j, c).rearrange("p (g t) -> p g t", g=4),
                                                C["causal4"], ALU.mult).then_inc(s_am, 1)
                    dve.wait_ge(s_u, n + 1)
                    nc.vector.scalar_tensor_tensor(S[j][:, :], u_ps[j], dS[j][:, 0:1], C["headmask"], ALU.mult,
                                                   ALU.mult).then_inc(s_S, 1)
                for j, n in units(i):
                    dve.wait_ge(s_sq, n + 1)
                    nc.vector.tensor_reduce(ss[j][:, :], sq[j][:, :].rearrange("p (g e) -> p g e", e=64), AX.X,
                                            ALU.add).then_inc(s_ss, 1)
                    dve.wait_ge(s_gg, n + 1)
                    m_og = chain.mark(nc.vector.tensor_tensor(og[j][:, :, :], o_ps[j].rearrange("p (c e) -> p c e", c=CH),
                                                              gg[j][:, :, :], ALU.mult))
                    dve.wait_ge(s_rr, n + 1)
                    chain.need(m_og)
                    nc.vector.tensor_tensor(on[j][:, :, :].rearrange("p c (g e) -> p (c g) e", e=64),
                                            og[j][:, :, :].rearrange("p c (g e) -> p (c g) e", e=64),
                                            rr[j][:, :].unsqueeze(2).to_broadcast([P, 8, 64]), ALU.mult).then_inc(s_on, 1)
                if more:
                    gate(i + 1)
                for j, n in units(i):
                    dve.wait_ge(s_out, n + 1)
                    xs = x[:, bass.ts(n, CH), :]
                    nc.vector.tensor_tensor(xs, xs, out_ps[j].rearrange("p (c e) -> p c e", c=CH), ALU.add).then_inc(s_x1, 1)
                if more:
                    rest(i + 1)

            dve.wait_ge(C["loaded"], C["loads"])
            dve.wait_ge(s_w, 16 * 9)
            nc.vector.tensor_scalar(won[:, :, :], wo[:, :, :], wn[:, 0:1], None, ALU.mult).then_inc(s_won, 1)
            dve.wait_ge(s_w12, 1)
            nc.vector.tensor_copy(w12[:, :], bank(0, 0)[:, 0:P]).then_inc(s_w12c, 1)
            for k in range(4):
                dve.wait_ge(s_x[k], 16)
                with dve.Fori(8 * k, 8 * k + 8) as c:
                    nc.vector.bn_stats(sts[:, c, :], x[:, c, :]).then_inc(s_bn, 1)
            dve.wait_ge(s_bn, UNITS * CH)
            stats_to_mean_var(nc, dve, s_aggr, sts[:, :, :], mvs[:, :, :], var_eps=ves[:, :])
            dve.wait_ge(s_aggr, STAT_STEPS)
            dve.sem_inc(s_stat, 1)
            dve.wait_ge(s_rstd, 1)
            pipelined(dve, chain, TURNS, DVE_FRONT, DVE_TURN, front, turn)


def ffn_attention(nc, io, C, F, x_dram, tag):
    UNITS, PAIR, CT = 16, 2, 2
    TURNS = UNITS // PAIR
    DVE_FRONT, DVE_TURN, ACT_FRONT, ACT_TURN, POOL_TURN = 0, 30, 0, 0, 6
    SCALE = 32.0 ** -0.5
    with ExitStack() as ctx:
        sb = lambda name, shape, dt=F32: ctx.enter_context(nc.sbuf_tensor(tag + name, shape, dt))
        sem = PhaseSemaphores(nc, ctx, tag)
        two = range(PAIR)
        x = F["x"]
        wq, wk, wv, wo = sb("wq", [P, P]), sb("wk", [P, P]), sb("wv", [P, P]), sb("wo", [P, P])
        wg = sb("wg", [P, EXPERTS])
        bq, bk = sb("bq", [P, 1]), sb("bk", [P, 1])
        bv, bo, g1, be1 = sb("bv", [P, P]), sb("bo", [P, P]), sb("g1", [P, P]), sb("be1", [P, P])
        strict16, ones16 = sb("strict16", [P, P], BF16), sb("ones16", [P, P], BF16)
        zeros = sb("zeros", [P, P])
        sts, mvs = sb("sts", [P, UNITS * CT, 6]), sb("mvs", [P, UNITS * CT, 2])
        ves, rstd = sb("ves", [P, UNITS * CT]), sb("rstd", [P, UNITS * CT])
        each = lambda name, shape, dt=F32: [sb(f"{name}{j}", shape, dt) for j in two]
        h, hb, hT = each("h", [P, CT, D]), each("hb", [P, CT, D]), each("hT", [P, 256])
        qx, kT, v = each("qx", [P, 16, 4, 16]), each("kT", [P, 256]), each("v", [P, CT, P])
        sm, mx, sd, ex = each("sm", [P, 8, 32]), each("mx", [P, 8]), each("sd", [P, 8, 32]), each("ex", [P, 8, 32])
        su, rs, pr = each("su", [P, 8]), each("rs", [P, 8]), each("pr", [P, 8, 32])
        ptx, oT = each("ptx", [P, CT, 4, P]), each("oT", [P, CT, P])
        r, st, mv, ve, rst = (each("r", [P, CT, D]), each("st", [P, CT, 6]), each("mv", [P, CT, 2]), each("ve", [P, CT]),
                              each("rst", [P, CT]))
        yn, yg, y, yT = each("yn", [P, CT, D]), each("yg", [P, CT, D]), each("y", [P, CT, D]), each("yT", [P, 256])
        lmx, eq, ei, em, oh = (each("lmx", [P, CT]), each("eq", [P, CT, EXPERTS]), each("ei", [P, CT, EXPERTS]),
                               each("em", [P, CT]), each("oh", [P, CT, EXPERTS]))
        oh16 = each("oh16", [P, CT, EXPERTS], BF16)
        rk, rsel, dest, base = (each("rk", [P, CT, EXPERTS]), each("rsel", [P, CT, EXPERTS]), each("dest", [P, CT], I32),
                                each("base", [P, EXPERTS]))
        ps = ctx.enter_context(nc.psum_tensor(tag + "ps", [P, 8, 512], F32))
        bank = lambda j, b: ps[:, 4 * j + b, :]
        hT_ps = [bank(j, 0)[:, 0:256] for j in two]
        s_ps = [bank(j, 0)[:, 256:512] for j in two]
        mha_ps = [bank(j, 0)[:, 0:256] for j in two]
        q_ps = [bank(j, 1)[:, 0:256] for j in two]
        pt_ps = [bank(j, 1)[:, 256:512] for j in two]
        k_ps = [bank(j, 2)[:, 0:256] for j in two]
        v_ps = [bank(j, 2)[:, 256:512] for j in two]
        pv_ps = [ps[:, 4 * j + 2:4 * j + 4, :] for j in two]
        yT_ps = [bank(j, 1)[:, 0:256] for j in two]
        lg_ps = [bank(j, 3)[:, 0:16] for j in two]
        rank_ps = [bank(j, 3)[:, 32:56] for j in two]

        (s_w, s_bn, s_aggr, s_rstd, s_h, s_hb, s_hTp, s_hT, s_q, s_kv, s_qx, s_kvc, s_s, s_sd, s_ex, s_pr, s_pt, s_pxa,
         s_pxd, s_pv, s_oa, s_od, s_mha, s_st, s_rst, s_yn, s_y, s_yTp, s_yT, s_lg, s_oh, s_rank, s_dest, s_scat, s_zero,
         s_c16, s_tab) = (sem(k) for k in (
             "weights_loaded", "bn_stats", "mean_var", "rstd", "normed", "h_plus_bo", "hT_psum", "hT_copied", "q_product",
             "kv_product", "q_spread", "kv_copied", "scores", "scores_less_max", "scores_exp", "probs", "probsT_psum",
             "probsT_spread_by_act", "probsT_spread_by_dve", "pv_product", "oT_by_act", "oT_by_dve", "mha_product",
             "r_stats", "r_rstd", "r_normed", "y_ready", "yT_psum", "yT_copied", "logits", "one_hot", "ranks", "dest_ready",
             "scattered", "spreads_zeroed", "masks16", "tables_ready"))
        c_dve, c_pool = sem("dve_steps"), sem("pool_steps")
        units = lambda i: [(j, i * PAIR + j) for j in two]
        WEIGHTS = 13
        apart = sem("apart")
        block = ctx.enter_context(nc.Block())

        @block.sync
        def _(sp):
            for k in range(4):
                for lp in range(8):
                    sp.dma_start(x[16 * lp:16 * lp + 16, 8 * k:8 * k + 8, :],
                                 x_dram.rearrange("s (g l) d -> l s g d", l=8)[lp, :, 8 * k:8 * k + 8, :]
                                 ).then_inc(F["s_x"][k], 16)

        def row(a, lo=0, hi=P):
            return a[lo:hi].unsqueeze(0).to_broadcast([P, hi - lo])

        @block.tensor
        def _(pe):
            def front(i):
                for j, n in units(i):
                    pe.wait_ge(s_h, n + 1)
                    for c in range(CT):
                        last = nc.tensor.transpose(hT_ps[j][:, P * c:P * c + P], h[j][:, c, :], C["ident"])
                    last.then_inc(s_hTp, 1)
                for j, n in units(i):
                    pe.wait_ge(s_hT, n + 1)
                    nc.tensor.matmul(q_ps[j], wq[:, :], hT[j][:, :], start=True, stop=True).then_inc(s_q, 1)
                    nc.tensor.matmul(k_ps[j], wk[:, :], hT[j][:, :], start=True, stop=True)
                    for c in range(CT):
                        last = nc.tensor.matmul(v_ps[j][:, P * c:P * c + P], hT[j][:, P * c:P * c + P], wv[:, :],
                                                start=True, stop=True)
                    last.then_inc(s_kv, 1)

            def turn(i, more):
                for j, n in units(i):
                    pe.wait_ge(s_qx, n + 1)
                    pe.wait_ge(s_kvc, n + 1)
                    for pair in range(8):
                        last = nc.tensor.matmul(s_ps[j][:, 32 * pair:32 * pair + 32], qx[j][:, 2 * pair:2 * pair + 2, :, :],
                                                kT[j][:, 32 * pair:32 * pair + 32], start=True, stop=True)
                    last.then_inc(s_s, 1)
                for j, n in units(i):
                    pe.wait_ge(s_pr, n + 1)
                    for c in range(CT):
                        last = nc.tensor.transpose(pt_ps[j][:, P * c:P * c + P], pr[j][:, 4 * c:4 * c + 4, :], C["ident"])
                    last.then_inc(s_pt, 1)
                for j, n in units(i):
                    pe.wait_ge(s_pxa, n + 1)
                    pe.wait_ge(s_pxd, n + 1)
                    for c in range(CT):
                        last = nc.tensor.matmul(pv_ps[j][:, c, :], v[j][:, c, :], ptx[j][:, c, :, :], start=True, stop=True)
                    last.then_inc(s_pv, 1)
                for j, n in units(i):
                    pe.wait_ge(s_oa, n + 1)
                    pe.wait_ge(s_od, n + 1)
                    for c in range(CT):
                        last = nc.tensor.matmul(mha_ps[j][:, P * c:P * c + P], oT[j][:, c, :], wo[:, :], start=True,
                                                stop=True)
                    last.then_inc(s_mha, 1)
                for j, n in units(i):
                    pe.wait_ge(s_y, n + 1)
                    for c in range(CT):
                        last = nc.tensor.transpose(yT_ps[j][:, P * c:P * c + P], y[j][:, c, :], C["ident"])
                    last.then_inc(s_yTp, 1)
                for j, n in units(i):
                    pe.wait_ge(s_yT, n + 1)
                    for c in range(CT):
                        last = nc.tensor.matmul(lg_ps[j][:, 8 * c:8 * c + 8], yT[j][:, P * c:P * c + P], wg[:, :],
                                                start=True, stop=True)
                    last.then_inc(s_lg, 1)
                if more:
                    front(i + 1)
                for j, n in units(i):
                    pe.wait_ge(s_oh, n + 1)
                    nc.tensor.matmul(rank_ps[j][:, 0:16], strict16[:, :], oh16[j][:, :, :], start=True, stop=False,
                                     skip_group_check=True)
                    nc.tensor.matmul(rank_ps[j][:, 8:16], ones16[:, :], oh16[j][:, 0, :], start=False, stop=False,
                                     skip_group_check=True)
                    nc.tensor.matmul(rank_ps[j][:, 16:24], ones16[:, :], oh16[j][:, 0, :], start=False, stop=False,
                                     skip_group_check=True)
                    nc.tensor.matmul(rank_ps[j][:, 16:24], ones16[:, :], oh16[j][:, 1, :], start=False, stop=True,
                                     skip_group_check=True).then_inc(s_rank, 1)

            pe.wait_ge(s_w, 16 * WEIGHTS)
            pe.wait_ge(s_c16, 1)
            pipelined(pe, Chain(pe, None), TURNS, 0, 0, front, turn)

        @block.scalar
        def _(act):
            def front(i):
                for j, n in units(i):
                    act.wait_ge(s_hTp, n + 1)
                    nc.scalar.activation(hT[j][:, :], hT_ps[j], ACT.Copy).then_inc(s_hT, 1)
                for j, n in units(i):
                    act.wait_ge(s_q, n + 1)
                    for hd in range(4):
                        rows = slice(32 * hd, 32 * hd + 32)
                        last = nc.scalar.activation(qx[j][rows, :, hd, :], q_ps[j][rows, :].rearrange("p (l s) -> p l s", s=16),
                                                    ACT.Identity, bias=bq[rows, :])
                    last.then_inc(s_qx, 1)

            def turn(i, more):
                for j, n in units(i):
                    act.wait_ge(s_sd, n + 1)
                    nc.scalar.activation(ex[j][:, :, :], sd[j][:, :, :], ACT.Exp, scale=SCALE).then_inc(s_ex, 1)
                for j, n in units(i):
                    act.wait_ge(s_pt, n + 1)
                    for k in range(2):
                        rows = slice(32 * k, 32 * k + 32)
                        last = nc.scalar.activation(ptx[j][rows, :, k, :], pt_ps[j][rows, :].rearrange("p (c e) -> p c e", c=CT),
                                                    ACT.Copy)
                    last.then_inc(s_pxa, 1)
                for j, n in units(i):
                    act.wait_ge(s_pv, n + 1)
                    for hd in range(2):
                        rows = slice(32 * hd, 32 * hd + 32)
                        last = nc.scalar.activation(
                            oT[j][rows, :, :].rearrange("p c (l s) -> p c l s", s=16),
                            pv_ps[j][rows, :, :].rearrange("p c (l h s) -> p c l h s", h=4, s=16)[:, :, :, hd, :], ACT.Copy)
                    last.then_inc(s_oa, 1)
                for j, n in units(i):
                    act.wait_ge(s_yTp, n + 1)
                    nc.scalar.activation(yT[j][:, :], yT_ps[j], ACT.Copy).then_inc(s_yT, 1)
                if more:
                    front(i + 1)

            for dst, src in ((wq, io["WqT"]), (wk, io["WkT"]), (wv, io["WvT"]), (wo, io["WoT"]), (wg, io["WgT"]),
                             (bq, io["bq_col"]), (bk, io["bk_col"]), (zeros, io["zeros"])):
                act.dma_start(dst[:, :], src).then_inc(s_w, 16)
            for dst, src in ((bv, io["bv"]), (bo, io["bo"]), (g1, io["g1"]), (be1, io["be1"])):
                act.dma_start(dst[:, :], row(src)).then_inc(s_w, 16)
            act.dma_start(F["scratch_rows"][EXPERTS * REGION:ROWS, :].rearrange("(b p) d -> p b d", p=P),
                          io["zeros8"]).then_inc(s_w, 16)
            act.wait_ge(s_w, 16 * WEIGHTS)
            pipelined(act, Chain(act, None), TURNS, 0, 0, front, turn)

        @block.gpsimd
        def _(pool):

            chain = Chain(pool, c_pool, apart)
            for j in two:
                nc.gpsimd.memset(qx[j][:, :, :, :], 0.0)
                last = nc.gpsimd.memset(ptx[j][:, :, :, :], 0.0)
            last.then_inc(s_zero, 1)
            pool.wait_ge(s_w, 16 * WEIGHTS)
            pool.wait_ge(s_aggr, STAT_STEPS)
            nc.gpsimd.tensor_tensor(rstd[:, :], ves[:, :], C["neg_half"][:, 0:UNITS * CT], ALU.pow).then_inc(s_rstd, 1)
            wide = lambda a: a[:, :].unsqueeze(1).to_broadcast([P, CT, P])
            with pool.Fori(0, TURNS) as i:
                chain.enter(i * POOL_TURN)
                for j, n in units(i):
                    pool.wait_ge(s_h, n + 1)
                    nc.gpsimd.tensor_tensor(hb[j][:, :, :], h[j][:, :, :], wide(bo), ALU.add).then_inc(s_hb, 1)
                for j, n in units(i):
                    wait_apart(pool, apart, s_st, n + 1)
                    chain.link(nc.gpsimd.tensor_scalar(ve[j][:, :], mv[j][:, :, 1], EPS, None, ALU.add))
                    nc.gpsimd.tensor_tensor(rst[j][:, :], ve[j][:, :], C["neg_half"][:, 0:CT], ALU.pow).then_inc(s_rst, 1)
                pool.wait_ge(s_scat, i * 32 * PAIR)
                for j, n in units(i):
                    pool.wait_ge(s_yn, n + 1)
                    chain.link(nc.gpsimd.tensor_tensor(yg[j][:, :, :], yn[j][:, :, :], wide(g1), ALU.mult))
                    chain.link(nc.gpsimd.tensor_tensor(y[j][:, :, :], yg[j][:, :, :], wide(be1), ALU.add))
                    pool.sem_inc(s_y, 1)
                for j, n in units(i):
                    wait_apart(pool, apart, s_dest, n + 1)
                    for c in range(CT):
                        nc.gpsimd.indirect_dma_start(
                            F["scratch_rows"], bass.IndirectOffsetOnAxis(ap=dest[j][:, c:c + 1], axis=0),
                            y[j][:, c, :], None).then_inc(s_scat, 16)
                chain.leave(POOL_TURN)
            pool.wait_ge(s_scat, 32 * UNITS)
            pool.wait_ge(s_tab, 1)
            for e in range(EXPERTS):
                start = nc.gpsimd.value_load(F["tables"][0:1, 2 * BLOCKS + e:2 * BLOCKS + e + 1], min_val=0,
                                             max_val=ROWS - P)
                nc.gpsimd.dma_start(F["scratch_rows"][bass.ds(start, P), :], zeros[:, :]).then_inc(s_scat, 16)
            pool.wait_ge(s_scat, 32 * UNITS + 16 * EXPERTS)

        @block.vector
        def _(dve):
            chain = Chain(dve, c_dve)


            def front(i):
                for j, n in units(i):
                    for c in range(CT):
                        last = nc.vector.tensor_scalar(h[j][:, c, :], x[:, n * CT + c, :], mvs[:, n * CT + c, 0:1],
                                                       rstd[:, bass.ts(n * CT + c, 1)], ALU.subtract, ALU.mult)
                    last.then_inc(s_h, 1)
                for j, n in units(i):
                    dve.wait_ge(s_kv, n + 1)
                    nc.vector.tensor_scalar(kT[j][:, :], k_ps[j], bk[:, 0:1], None, ALU.add)
                    nc.vector.tensor_tensor(v[j][:, :, :], v_ps[j].rearrange("p (c e) -> p c e", c=CT),
                                            bv[:, :].unsqueeze(1).to_broadcast([P, CT, P]), ALU.add).then_inc(s_kvc, 1)

            def turn(i, more):
                for j, n in units(i):
                    dve.wait_ge(s_s, n + 1)
                    chain.link(nc.vector.tensor_tensor(sm[j][:, :, :], s_ps[j].rearrange("p (g k) -> p g k", k=32),
                                                       C["pairmask"].unsqueeze(1).to_broadcast([P, 8, 32]), ALU.add))
                    chain.link(nc.vector.tensor_reduce(mx[j][:, :], sm[j][:, :, :], AX.X, ALU.max))
                    nc.vector.tensor_tensor(sd[j][:, :, :], sm[j][:, :, :],
                                            mx[j][:, :].unsqueeze(2).to_broadcast([P, 8, 32]), ALU.subtract).then_inc(s_sd, 1)
                for j, n in units(i):
                    dve.wait_ge(s_ex, n + 1)
                    chain.link(nc.vector.tensor_reduce(su[j][:, :], ex[j][:, :, :], AX.X, ALU.add))
                    chain.link(nc.vector.reciprocal(rs[j][:, :], su[j][:, :]))
                    nc.vector.tensor_tensor(pr[j][:, :, :], ex[j][:, :, :],
                                            rs[j][:, :].unsqueeze(2).to_broadcast([P, 8, 32]), ALU.mult).then_inc(s_pr, 1)
                for j, n in units(i):
                    dve.wait_ge(s_pt, n + 1)
                    for k in range(2, 4):
                        rows = slice(32 * k, 32 * k + 32)
                        last = nc.vector.tensor_copy(ptx[j][rows, :, k, :], pt_ps[j][rows, :].rearrange("p (c e) -> p c e", c=CT))
                    last.then_inc(s_pxd, 1)
                for j, n in units(i):
                    dve.wait_ge(s_pv, n + 1)
                    for hd in range(2, 4):
                        rows = slice(32 * hd, 32 * hd + 32)
                        last = nc.vector.tensor_copy(
                            oT[j][rows, :, :].rearrange("p c (l s) -> p c l s", s=16),
                            pv_ps[j][rows, :, :].rearrange("p c (l h s) -> p c l h s", h=4, s=16)[:, :, :, hd, :])
                    last.then_inc(s_od, 1)
                for j, n in units(i):
                    dve.wait_ge(s_mha, n + 1)
                    dve.wait_ge(s_hb, n + 1)
                    chain.link(nc.vector.tensor_tensor(r[j][:, :, :], mha_ps[j].rearrange("p (c e) -> p c e", c=CT),
                                                       hb[j][:, :, :], ALU.add))
                    for c in range(CT):
                        last = chain.mark(nc.vector.bn_stats(st[j][:, c, :], r[j][:, c, :]))
                    chain.need(last, apart)
                    for c in range(CT):
                        last = nc.vector.bn_aggr(mv[j][:, c, :], st[j][:, c, :])
                    last.then_inc(s_st, 1)
                for j, n in units(i):
                    dve.wait_ge(s_rst, n + 1)
                    for c in range(CT):
                        last = nc.vector.tensor_scalar(yn[j][:, c, :], r[j][:, c, :], mv[j][:, c, 0:1], rst[j][:, c:c + 1],
                                                       ALU.subtract, ALU.mult)
                    last.then_inc(s_yn, 1)
                for j, n in units(i):
                    dve.wait_ge(s_lg, n + 1)
                    lg = lg_ps[j].rearrange("p (c e) -> p c e", c=CT)
                    spread = lambda a: a[:, :].unsqueeze(2).to_broadcast([P, CT, EXPERTS])
                    index = C["expert_less_8"].unsqueeze(1).to_broadcast([P, CT, EXPERTS])
                    chain.link(nc.vector.tensor_reduce(lmx[j][:, :], lg, AX.X, ALU.max))
                    chain.link(nc.vector.tensor_tensor(eq[j][:, :, :], lg, spread(lmx[j]), ALU.is_ge))
                    chain.link(nc.vector.tensor_tensor(ei[j][:, :, :], eq[j][:, :, :], index, ALU.mult))
                    chain.link(nc.vector.tensor_reduce(em[j][:, :], ei[j][:, :, :], AX.X, ALU.min))
                    nc.vector.tensor_tensor(oh[j][:, :, :], index, spread(em[j]), ALU.is_equal)
                    nc.vector.tensor_tensor(oh16[j][:, :, :], index, spread(em[j]), ALU.is_equal).then_inc(s_oh, 1)
                if more:
                    front(i + 1)
                for j, n in units(i):
                    dve.wait_ge(s_rank, n + 1)
                    chain.link(nc.vector.tensor_tensor(rk[j][:, :, :], rank_ps[j][:, 0:16].rearrange("p (c e) -> p c e", c=CT),
                                                       base[j][:, :].unsqueeze(1).to_broadcast([P, CT, EXPERTS]), ALU.add))
                    chain.link(nc.vector.tensor_tensor(rsel[j][:, :, :], rk[j][:, :, :], oh[j][:, :, :], ALU.mult))
                    chain.link(nc.vector.tensor_tensor(base[1 - j][:, :], rank_ps[j][:, 16:24], base[j][:, :], ALU.add))
                    with nc.allow_low_precision(reason="whole numbers below 2**24"):
                        chain.link(nc.vector.tensor_reduce(dest[j][:, :], rsel[j][:, :, :], AX.X, ALU.add))
                    nc.vector.tensor_copy(F["dest"][:, bass.ts(n, CT)], dest[j][:, :]).then_inc(s_dest, 1)

            dve.wait_ge(C["loaded"], C["loads"])
            dve.wait_ge(s_zero, 1)
            nc.vector.tensor_copy(strict16[:, :], C["strict"])
            nc.vector.tensor_copy(base[0][:, :], C["region_start"])
            nc.vector.tensor_copy(ones16[:, :], C["ones"][:, 0:P]).then_inc(s_c16, 1)
            for k in range(4):
                dve.wait_ge(F["s_x"][k], 16 * 8 * F["use"])
                with dve.Fori(8 * k, 8 * k + 8) as c:
                    nc.vector.bn_stats(sts[:, c, :], x[:, c, :]).then_inc(s_bn, 1)
            dve.wait_ge(s_bn, UNITS * CT)
            stats_to_mean_var(nc, dve, s_aggr, sts[:, :, :], mvs[:, :, :], var_eps=ves[:, :])
            dve.wait_ge(s_rstd, 1)
            dve.wait_ge(s_w, 16 * WEIGHTS)
            pipelined(dve, chain, TURNS, DVE_FRONT, DVE_TURN, front, turn)
            routing_tables(nc, dve, C, F, base[0], sb, sem, s_tab)


def routing_tables(nc, dve, C, F, base, sb, sem, s_tab):
    s = sem("table_steps")
    count = [0]

    def link(ins):
        count[0] += 1
        ins.then_inc(s, 1)
        dve.wait_ge(s, count[0])

    n_f, n_i, nb_i, nb, cum = (sb("t_n", [P, EXPERTS]), sb("t_ni", [P, EXPERTS], I32), sb("t_nbi", [P, EXPERTS], I32),
                               sb("t_nb", [P, EXPERTS]), sb("t_cum", [P, EXPERTS]))
    skip, past, pskip = sb("t_skip", [P, EXPERTS]), sb("t_past", [P, BLOCKS, EXPERTS]), sb("t_ps", [P, BLOCKS, EXPERTS])
    expert, rows = sb("t_e", [P, BLOCKS]), sb("t_r", [P, BLOCKS])
    link(nc.vector.tensor_tensor(n_f[:, :], base[:, :], C["region_start"], ALU.subtract))
    link(nc.vector.tensor_scalar(n_i[:, :], n_f[:, :], float(P - 1), None, ALU.add))
    link(nc.vector.tensor_scalar(nb_i[:, :], n_i[:, :], 7, None, ALU.logical_shift_right))
    link(nc.vector.tensor_copy(nb[:, :], nb_i[:, :]))
    link(nc.vector.tensor_tensor_scan(cum[:, :], C["ones"][:, 0:EXPERTS], nb[:, :], 0.0, ALU.mult, ALU.add))
    link(nc.vector.tensor_scalar(skip[:, :], nb[:, :], -float(P), float(REGION), ALU.mult, ALU.add))
    shape = [P, BLOCKS, EXPERTS]
    block = C["block"].unsqueeze(2).to_broadcast(shape)
    link(nc.vector.tensor_tensor(past[:, :, :], block, cum[:, :].unsqueeze(1).to_broadcast(shape), ALU.is_ge))
    link(nc.vector.tensor_tensor(pskip[:, :, :], past[:, :, :], skip[:, :].unsqueeze(1).to_broadcast(shape), ALU.mult))
    link(nc.vector.tensor_reduce(expert[:, :], past[:, :, :], AX.X, ALU.add))
    link(nc.vector.tensor_reduce(rows[:, :], pskip[:, :, :], AX.X, ALU.add))
    link(nc.vector.tensor_scalar(F["tables"][0:1, 0:BLOCKS], expert[0:1, :], float(EXPERTS - 1), None, ALU.min))
    link(nc.vector.scalar_tensor_tensor(F["tables"][0:1, BLOCKS:2 * BLOCKS], C["block"][0:1, :], float(P), rows[0:1, :],
                                        ALU.mult, ALU.add))
    link(nc.vector.tensor_copy(F["tables"][0:1, 2 * BLOCKS:2 * BLOCKS + EXPERTS], base[0:1, :]))
    tiles = SEQ * L // P
    behind, unused, less = sb("t_bh", [P, tiles, EXPERTS]), sb("t_un", [P, tiles, EXPERTS]), sb("t_ls", [P, tiles])
    shape = [P, tiles, EXPERTS]
    link(nc.vector.tensor_tensor(behind[:, :, :], F["dest"][:, :].unsqueeze(2).to_broadcast(shape),
                                 C["region_end"].unsqueeze(1).to_broadcast(shape), ALU.is_ge))
    link(nc.vector.tensor_tensor(unused[:, :, :], behind[:, :, :], skip[:, :].unsqueeze(1).to_broadcast(shape), ALU.mult))
    link(nc.vector.tensor_reduce(less[:, :], unused[:, :, :], AX.X, ALU.add))
    link(nc.vector.tensor_tensor(F["place"][:, :], F["dest"][:, :], less[:, :], ALU.subtract))
    dve.sem_inc(s_tab, 1)


def ffn_experts(nc, io, C, F, tag):
    LANES = 4
    TURNS = BLOCKS // LANES
    assert TURNS * LANES == BLOCKS
    FC = DF // P
    WCOLS = DF + FC + P
    with ExitStack() as ctx:
        sb = lambda name, shape, dt=F32: ctx.enter_context(nc.sbuf_tensor(tag + name, shape, dt))
        sem = PhaseSemaphores(nc, ctx, tag)
        lanes = range(LANES)
        each = lambda name, shape, dt=F32: [sb(f"{name}{j}", shape, dt) for j in lanes]
        w2 = F["w2"]
        g2, be2 = sb("g2", [P, P]), sb("be2", [P, P])
        y, yT, wst = each("y", [P, D]), each("yT", [P, P]), each("wst", [P, WCOLS])
        hh, r, st, mv, ve, rst = (each("hh", [P, FC, P]), each("r", [P, D]), each("st", [P, 6]), each("mv", [P, 2]),
                                  each("ve", [P, 1]), each("rst", [P, 1]))
        yb, rg, z = each("yb", [P, D]), each("rg", [P, D]), each("z", [P, D])
        ps = ctx.enter_context(nc.psum_tensor(tag + "ps", [P, 8, 512], F32))
        hh_ps = [ps[:, 2 * j, :] for j in lanes]
        yT_ps = [ps[:, 2 * j + 1, 0:P] for j in lanes]
        out_ps = [ps[:, 2 * j + 1, 256:256 + D] for j in lanes]
        (s_w, s_yTp, s_yT, s_h, s_hr, s_yb, s_out, s_st, s_rst, s_z) = (sem(k) for k in (
            "affine_loaded", "yT_psum", "yT_copied", "hidden_product", "hidden_ready", "y_plus_bias", "out_product",
            "r_stats", "r_rstd", "z_ready"))
        s_store = [sem(f"z_stored{j}") for j in lanes]
        s_wst = [sem(f"weights_staged{j}") for j in lanes]
        s_load = [sem(f"y_loaded{j}") for j in lanes]
        c_dve, c_pool, apart = sem("dve_steps"), sem("pool_steps"), sem("apart")
        DVE_TURN, POOL_TURN = 3 * LANES, LANES
        units = lambda i: [(j, i * LANES + j) for j in lanes]
        expert = lambda eng, b: eng.value_load(F["tables"][0:1, bass.ds(b, 1)], min_val=0, max_val=EXPERTS - 1)
        first_row = lambda eng, b: eng.value_load(F["tables"][0:1, bass.ds(b + BLOCKS, 1)], min_val=0, max_val=ROWS - P)
        block = ctx.enter_context(nc.Block())

        @block.sync
        def _(sp):
            def load(j, b):
                sp.dma_start(y[j][:, :], F["scratch_rows"][bass.ds(first_row(sp, b), P), :]).then_inc(s_load[j], 16)

            def turn(i, more):
                for j, b in units(i):
                    if more:
                        sp.wait_ge(s_hr, b + 1)
                        stage(j, b + LANES)
                if more == 2:
                    for j, b in units(i + 1):
                        sp.wait_ge(s_yTp, b + 1)
                        sp.wait_ge(s_yb, b + 1)
                        load(j, b + LANES)
                for j, b in units(i):
                    sp.wait_ge(s_z, b + 1)
                    sp.dma_start(F["result_rows"][bass.ts(b, P), :], z[j][:, :]).then_inc(s_store[j], 16)

            def stage(j, b):
                sp.dma_start(wst[j][:, :], io["w1b"][bass.ds(expert(sp, b), 1)].rearrange("e p w -> p (e w)")
                             ).then_inc(s_wst[j], 16)

            sp.dma_start(g2[:, :], io["g2"].unsqueeze(0).to_broadcast([P, P])).then_inc(s_w, 16)
            sp.dma_start(be2[:, :], io["be2"].unsqueeze(0).to_broadcast([P, P])).then_inc(s_w, 16)
            for j, b in units(0):
                load(j, b)
            for j, b in units(0):
                stage(j, b)
            for j, b in units(0):
                sp.wait_ge(s_yTp, b + 1)
                sp.wait_ge(s_yb, b + 1)
                load(j, b + LANES)
            with sp.Fori(0, TURNS - 2) as i:
                turn(i, 2)
            turn(TURNS - 2, 1)
            turn(TURNS - 1, 0)
            for j in lanes:
                sp.wait_ge(s_store[j], 16 * TURNS)

        @block.gpsimd
        def _(pool):
            chain = Chain(pool, c_pool, apart)

            def add_bias(i):
                for j, b in units(i):
                    pool.wait_ge(s_load[j], 16 * i + 16)
                    wait_apart(pool, apart, s_wst[j], 16 * i + 16)
                    nc.gpsimd.tensor_tensor(yb[j][:, :], y[j][:, :], wst[j][:, DF + FC:WCOLS], ALU.add).then_inc(s_yb, 1)

            def turn(i, more):
                for j, b in units(i):
                    wait_apart(pool, apart, s_st, b + 1)
                    chain.link(nc.gpsimd.tensor_scalar(ve[j][:, :], mv[j][:, 1:2], EPS, None, ALU.add))
                    nc.gpsimd.tensor_tensor(rst[j][:, :], ve[j][:, :], C["neg_half"][:, 0:1], ALU.pow).then_inc(s_rst, 1)
                if more:
                    add_bias(i + 1)

            add_bias(0)
            with pool.Fori(0, TURNS - 1) as i:
                chain.enter(i * POOL_TURN)
                turn(i, True)
                chain.leave(POOL_TURN)
            chain.enter((TURNS - 1) * POOL_TURN)
            turn(TURNS - 1, False)

        @block.tensor
        def _(pe):
            def to_yT(i):
                for j, b in units(i):
                    pe.wait_ge(s_load[j], 16 * i + 16)
                    nc.tensor.transpose(yT_ps[j], y[j][:, :], C["ident"]).then_inc(s_yTp, 1)

            def turn(i, more):
                for j, b in units(i):
                    pe.wait_ge(s_yT, b + 1)
                    pe.wait_ge(s_wst[j], 16 * i + 16)
                    for f in range(FC):
                        last = nc.tensor.matmul(hh_ps[j][:, P * f:P * f + P], wst[j][:, P * f:P * f + P], yT[j][:, :],
                                                start=True, stop=True)
                    last.then_inc(s_h, 1)
                for j, b in units(i):
                    e = expert(pe, b)
                    pe.wait_ge(s_hr, b + 1)
                    for f in range(FC):
                        last = nc.tensor.matmul(out_ps[j], hh[j][:, f, :], w2[:, bass.ds(e * (FC * D) + f * D, D)],
                                                start=(f == 0), stop=(f == FC - 1))
                    last.then_inc(s_out, 1)
                if more:
                    pe.wait_ge(s_st, (i + 1) * LANES)
                    to_yT(i + 1)

            to_yT(0)
            with pe.Fori(0, TURNS - 1) as i:
                turn(i, True)
            turn(TURNS - 1, False)

        @block.scalar
        def _(act):
            def copy_yT(i):
                for j, b in units(i):
                    act.wait_ge(s_yTp, b + 1)
                    nc.scalar.activation(yT[j][:, :], yT_ps[j], ACT.Copy).then_inc(s_yT, 1)

            def turn(i, more):
                for j, b in units(i):
                    act.wait_ge(s_h, b + 1)
                    for f in range(FC):
                        last = nc.scalar.activation(hh[j][:, f, :], hh_ps[j][:, P * f:P * f + P], ACT.Relu,
                                                    bias=wst[j][:, DF + f:DF + f + 1])
                    last.then_inc(s_hr, 1)
                if more:
                    copy_yT(i + 1)

            act.preload_act_table_set(EXP_LN)
            copy_yT(0)
            with act.Fori(0, TURNS - 1) as i:
                turn(i, True)
            turn(TURNS - 1, False)

        @block.vector
        def _(dve):
            chain = Chain(dve, c_dve)

            def turn(i, first):
                for j, b in units(i):
                    dve.wait_ge(s_out, b + 1)
                    dve.wait_ge(s_yb, b + 1)
                    chain.link(nc.vector.tensor_tensor(r[j][:, :], out_ps[j], yb[j][:, :], ALU.add))
                    chain.link(nc.vector.bn_stats(st[j][:, :], r[j][:, :]), apart)
                    nc.vector.bn_aggr(mv[j][:, :], st[j][:, :]).then_inc(s_st, 1)
                for j, b in units(i):
                    if not first:
                        dve.wait_ge(s_store[j], 16 * i)
                    dve.wait_ge(s_rst, b + 1)
                    chain.link(nc.vector.scalar_tensor_tensor(rg[j][:, :], r[j][:, :], mv[j][:, 0:1], g2[:, :],
                                                              ALU.subtract, ALU.mult))
                    nc.vector.scalar_tensor_tensor(z[j][:, :], rg[j][:, :], rst[j][:, 0:1], be2[:, :], ALU.mult,
                                                   ALU.add).then_inc(s_z, 1)

            dve.wait_ge(s_w, 32)
            turn(0, True)
            chain.leave(DVE_TURN)
            with dve.Fori(1, TURNS) as i:
                chain.enter(i * DVE_TURN)
                turn(i, False)
                chain.leave(DVE_TURN)


def ffn_gather(nc, io, C, F, out_dram, tag):
    TILES, GROUP = SEQ * L // P, 4
    TURNS = TILES // GROUP
    with ExitStack() as ctx:
        sb = lambda name, shape, dt=F32: ctx.enter_context(nc.sbuf_tensor(tag + name, shape, dt))
        sem = PhaseSemaphores(nc, ctx, tag)
        x = F["x"]
        z = [sb(f"z{k}", [P, D]) for k in range(2 * GROUP)]
        at = sb("at", [P, 2, GROUP], I32)
        s_at, s_z, s_sum, s_out = sem("places_copied"), [sem("gathered0"), sem("gathered1")], sem("summed"), sem("stored")
        apart = sem("apart")
        block = ctx.enter_context(nc.Block())

        @block.gpsimd
        def _(pool):

            with pool.Fori(0, TURNS // 2) as i:
                for k in range(2):
                    wait_apart(pool, apart, s_at, 2 * i + k + 1)
                    for g in range(GROUP):
                        nc.gpsimd.indirect_dma_start(z[GROUP * k + g][:, :], None, F["result_rows"],
                                                     bass.IndirectOffsetOnAxis(ap=at[:, k, g:g + 1], axis=0)
                                                     ).then_inc(s_z[k], 16)

        @block.vector
        def _(dve):
            def place(i, k):
                nc.vector.tensor_copy(at[:, k, :], F["place"][:, bass.ts(2 * i + k, GROUP)]).then_inc(s_at, 1)

            def add(i, k):
                dve.wait_ge(s_z[k], 16 * GROUP * (i + 1))
                for g in range(GROUP):
                    xs = x[:, (2 * i + k) * GROUP + g, :]
                    last = nc.vector.tensor_tensor(xs, xs, z[GROUP * k + g][:, :], ALU.add)
                last.then_inc(s_sum, 1)

            for k in range(2):
                place(0, k)
            with dve.Fori(0, TURNS // 2 - 1) as i:
                for k in range(2):
                    add(i, k)
                    place(i + 1, k)
            for k in range(2):
                add(TURNS // 2 - 1, k)

        @block.sync
        def _(sp):
            for k in range(TURNS // 2):
                sp.wait_ge(s_sum, 2 * k + 2)
                for lp in range(8):
                    sp.dma_start(out_dram.rearrange("s (g l) d -> l s g d", l=8)[lp, :, 8 * k:8 * k + 8, :],
                                 x[16 * lp:16 * lp + 16, 8 * k:8 * k + 8, :]).then_inc(s_out, 16)
            sp.wait_ge(s_out, 16 * 8 * (TURNS // 2))


def rwkv_phase(nc, io, C, x_dram, out_dram, tag="rk_"):
    UNITS, PAIR, CT = SEQ, 2, 2
    TURNS = UNITS // PAIR
    FC = DF // P
    LIM = 30.0
    DVE_FRONT, DVE_TURN, ACT_FRONT, ACT_TURN, POOL_TURN = 22, 32, 8, 12, 4
    with ExitStack() as ctx:
        sb = lambda name, shape, dt=F32: ctx.enter_context(nc.sbuf_tensor(tag + name, shape, dt))
        sem = PhaseSemaphores(nc, ctx, tag)
        two = range(PAIR)
        each = lambda name, shape, dt=F32: [sb(f"{name}{j}", shape, dt) for j in two]
        x = sb("x", [P, UNITS * CT, D])
        wk, wv, wr, wcr = sb("wk", [P, P]), sb("wv", [P, P]), sb("wr", [P, P]), sb("wcr", [P, P])
        wck, wcv = sb("wck", [P, DF]), sb("wcv", [P, FC, D])
        cols = sb("cols", [P, 11])
        ln1g, ln1b, ln2g, ln2b, mixk, mixv, mixr, cmixk, cmixr, decay, first = (cols[:, k:k + 1] for k in range(11))
        U = sb("U", [P, 1])
        sts, mvs = sb("sts", [P, UNITS * CT, 6]), sb("mvs", [P, UNITS * CT, 2])
        ves, rs1, t1, t2, rs2, rs12 = (sb(k, [P, UNITS * CT]) for k in ("ves", "rs1", "t1", "t2", "rs2", "rs12"))
        u, hn, hT, dh = each("u", [P, CT, D]), each("hn", [P, CT, D]), each("hT", [P, L + 1]), each("dh", [P, L])
        xk, xv, xr = each("xk", [P, L]), each("xv", [P, L]), each("xr", [P, L])
        m, mu, muc, X, Xi = each("m", [P, L + 1]), each("mu", [P, L]), each("muc", [P, L]), each("X", [P, L]), each("Xi", [P, L])
        e1, e2, Q, lnQ, lam = each("e1", [P, L]), each("e2", [P, L]), each("Q", [P, L + 1]), each("lnQ", [P, L]), each("lam", [P, L])
        G, Gi, al, bv, a = each("G", [P, L]), each("Gi", [P, L]), each("al", [P, L]), each("bv", [P, L]), each("a", [P, L + 1])
        lw, sw, rc, re, rl, sr = (each("lw", [P, L]), each("sw", [P, L]), each("rc", [P, L]), each("re", [P, L]),
                                  each("rl", [P, L]), each("sr", [P, L]))
        d1, d2, yv, ry = each("d1", [P, L]), each("d2", [P, L]), each("yv", [P, L]), each("ry", [P, L])
        xp, st, mv, ve, rst = (each("xp", [P, CT, D]), each("st", [P, CT, 6]), each("mv", [P, CT, 2]), each("ve", [P, CT]),
                               each("rst", [P, CT]))
        h2, h2T, dh2, ck, cr = each("h2", [P, CT, D]), each("h2T", [P, L + 1]), each("dh2", [P, L]), each("ck", [P, L]), each("cr", [P, L])
        rk, kk = each("rk", [P, FC, L]), each("kk", [P, FC, L])
        cc, ce, cl, sc, o, xs = (each("cc", [P, L]), each("ce", [P, L]), each("cl", [P, L]), each("sc", [P, L]),
                                 each("o", [P, CT, D]), each("xs", [P, CT, D]))
        ps = ctx.enter_context(nc.psum_tensor(tag + "ps", [P, 8, 512], F32))
        bank = lambda j, b: ps[:, 4 * j + b, :]
        hT_ps = [bank(j, 0)[:, 0:256] for j in two]
        r_ps = [bank(j, 0)[:, 256:512] for j in two]
        k_ps = [bank(j, 1)[:, 0:256] for j in two]
        v_ps = [bank(j, 1)[:, 256:512] for j in two]
        w_ps = [bank(j, 2)[:, 0:256] for j in two]
        h2T_ps = [bank(j, 3)[:, 0:256] for j in two]
        kk_ps = [ps[:, 4 * j + 2:4 * j + 4, :] for j in two]
        kv_ps = [bank(j, 2)[:, 0:256] for j in two]
        cr_ps = [bank(j, 2)[:, 256:512] for j in two]
        names = ("weights_loaded bn_stats mean_var rstd1 var2 rstd2 rstd12 first_exp normed hT_psum hT_copied mixed kvr_product "
                 "shift_ready shift_exp Q_ready Q_ln lam_ready lam_exp r_clamped r_sigmoid y_sigmoid ry_ready w_psum "
                 "xp_stats xp_rstd h2_ready h2T_psum h2T_copied cmixed kk_product relu_ready kk_ready ckv_product cr_clamped "
                 "cr_sigmoid x_plus_xp x_out stored bounds_set").split()
        (s_w, s_bn, s_mv, s_rs1, s_var2, s_rs2, s_rs12, s_U, s_h, s_hTp, s_hT, s_mix, s_kvr, s_mu, s_X, s_Q, s_lnQ, s_lam, s_G,
         s_rc, s_sr, s_sw, s_ry, s_wp, s_st, s_rst, s_h2, s_h2Tp, s_h2T, s_cmix, s_kk, s_relu, s_kk2, s_kv, s_cc, s_sc,
         s_xs, s_out, s_store, s_set) = (sem(k) for k in names)
        s_x = [sem(f"x_loaded{k}") for k in range(4)]
        c_dve, c_act, c_pool, apart = sem("dve_steps"), sem("act_steps"), sem("pool_steps"), sem("apart")
        units = lambda i: [(j, i * PAIR + j) for j in two]
        tiles = lambda t: t.rearrange("p (c e) -> p c e", c=CT)
        WEIGHTS = 7
        block = ctx.enter_context(nc.Block())

        @block.sync
        def _(sp):
            for k in range(4):
                sp.dma_start(x[:, 8 * k:8 * k + 8, :],
                             x_dram[4 * k:4 * k + 4].rearrange("s (c p) d -> p (s c) d", p=P)).then_inc(s_x[k], 16)
            with sp.Fori(0, UNITS) as n:
                sp.wait_ge(s_out, n + 1)
                sp.dma_start(out_dram[bass.ts(n, 1)].rearrange("s (c p) d -> p (s c) d", p=P),
                             x[:, bass.ts(n, CT), :]).then_inc(s_store, 16)
            sp.wait_ge(s_store, 16 * UNITS)

        @block.tensor
        def _(pe):
            def to_hT(i):
                for j, n in units(i):
                    pe.wait_ge(s_h, n + 1)
                    for c in range(CT):
                        last = nc.tensor.transpose(hT_ps[j][:, P * c:P * c + P], hn[j][:, c, :], C["ident"])
                    last.then_inc(s_hTp, 1)

            def to_kvr(i):
                for j, n in units(i):
                    pe.wait_ge(s_mix, n + 1)
                    nc.tensor.matmul(k_ps[j], wk[:, :], xk[j][:, :], start=True, stop=True)
                    nc.tensor.matmul(v_ps[j], wv[:, :], xv[j][:, :], start=True, stop=True)
                    nc.tensor.matmul(r_ps[j], wr[:, :], xr[j][:, :], start=True, stop=True).then_inc(s_kvr, 1)

            def front(i):
                to_hT(i)
                to_kvr(i)

            def turn(i, more):
                pe.wait_ge(s_out, i * PAIR)
                for j, n in units(i):
                    pe.wait_ge(s_ry, n + 1)
                    for c in range(CT):
                        last = nc.tensor.transpose(w_ps[j][:, P * c:P * c + P], ry[j][:, P * c:P * c + P], C["ident"])
                    last.then_inc(s_wp, 1)
                if more:
                    to_hT(i + 1)
                for j, n in units(i):
                    pe.wait_ge(s_h2, n + 1)
                    for c in range(CT):
                        last = nc.tensor.transpose(h2T_ps[j][:, P * c:P * c + P], h2[j][:, c, :], C["ident"])
                    last.then_inc(s_h2Tp, 1)
                if more:
                    to_kvr(i + 1)
                for j, n in units(i):
                    pe.wait_ge(s_cmix, n + 1)
                    for f in range(FC):
                        last = nc.tensor.matmul(kk_ps[j][:, f // 2, 256 * (f % 2):256 * (f % 2) + 256],
                                                wck[:, P * f:P * f + P], ck[j][:, :], start=True, stop=True)
                    last.then_inc(s_kk, 1)
                for j, n in units(i):
                    pe.wait_ge(s_relu, n + 1)
                    pe.wait_ge(s_kk2, n + 1)
                    for c in range(CT):
                        nc.tensor.matmul(cr_ps[j][:, P * c:P * c + P], cr[j][:, P * c:P * c + P], wcr[:, :], start=True,
                                         stop=True)
                    for c in range(CT):
                        for f in range(FC):
                            last = nc.tensor.matmul(kv_ps[j][:, P * c:P * c + P], kk[j][:, f, P * c:P * c + P], wcv[:, f, :],
                                                    start=(f == 0), stop=(f == FC - 1))
                    last.then_inc(s_kv, 1)

            pe.wait_ge(C["loaded"], C["loads"])
            pe.wait_ge(s_w, 16 * WEIGHTS)
            pipelined(pe, Chain(pe, None), TURNS, 0, 0, front, turn)

        @block.scalar
        def _(act):
            chain = Chain(act, c_act)

            def sigmoid(out, l, e, src):
                chain.link(nc.scalar.activation(e, src, ACT.Exp, scale=-1.0))
                chain.link(nc.scalar.activation(l, e, ACT.Ln, bias=1.0))
                return nc.scalar.activation(out, l, ACT.Exp, scale=-1.0)

            def copy_hT(i):
                for j, n in units(i):
                    act.wait_ge(s_hTp, n + 1)
                    nc.scalar.activation(hT[j][:, 1:L + 1], hT_ps[j], ACT.Identity, bias=ln1b, scale=ln1g).then_inc(s_hT, 1)

            def exps(i):
                for j, n in units(i):
                    act.wait_ge(s_mu, n + 1)
                    nc.scalar.activation(X[j][:, :], muc[j][:, :], ACT.Exp)
                    nc.scalar.activation(Xi[j][:, :], muc[j][:, :], ACT.Exp, scale=-1.0).then_inc(s_X, 1)
                for j, n in units(i):
                    act.wait_ge(s_rc, n + 1)
                    sigmoid(sr[j][:, :], rl[j][:, :], re[j][:, :], rc[j][:, :]).then_inc(s_sr, 1)
                for j, n in units(i):
                    act.wait_ge(s_Q, n + 1)
                    nc.scalar.activation(lnQ[j][:, :], Q[j][:, 0:L], ACT.Ln).then_inc(s_lnQ, 1)
                for j, n in units(i):
                    act.wait_ge(s_lam, n + 1)
                    chain.link(nc.scalar.activation(Gi[j][:, :], lam[j][:, :], ACT.Exp, scale=-1.0))
                    nc.scalar.activation(G[j][:, :], lam[j][:, :], ACT.Exp).then_inc(s_G, 1)
                    chain.link(nc.scalar.activation(lw[j][:, :], Gi[j][:, :], ACT.Ln, bias=1.0, scale=U[:, :]))
                    nc.scalar.activation(sw[j][:, :], lw[j][:, :], ACT.Exp, scale=-1.0).then_inc(s_sw, 1)

            def front(i):
                copy_hT(i)
                exps(i)

            def turn(i, more):
                if more:
                    copy_hT(i + 1)
                for j, n in units(i):
                    act.wait_ge(s_h2Tp, n + 1)
                    nc.scalar.activation(h2T[j][:, 1:L + 1], h2T_ps[j], ACT.Identity, bias=ln2b, scale=ln2g).then_inc(s_h2T, 1)
                for j, n in units(i):
                    act.wait_ge(s_kk, n + 1)
                    nc.scalar.activation(rk[j][:, :, :].rearrange("p f t -> p (f t)"), kk_ps[j].rearrange("p b t -> p (b t)"),
                                         ACT.Relu).then_inc(s_relu, 1)
                if more:
                    exps(i + 1)
                for j, n in units(i):
                    act.wait_ge(s_cc, n + 1)
                    sigmoid(sc[j][:, :], cl[j][:, :], ce[j][:, :], cc[j][:, :]).then_inc(s_sc, 1)

            for dst, src in ((wk[:, :], io["w_tk"]), (wv[:, :], io["w_tv"]), (wr[:, :], io["w_tr"]), (wcr[:, :], io["w_cr"]),
                             (wck[:, :], io["w_ck"]), (wcv[:, :, :], io["w_cv"].rearrange("(f p) d -> p f d", p=P)),
                             (cols[:, :], io["rwkv_cols"])):
                act.dma_start(dst, src).then_inc(s_w, 16)
            act.preload_act_table_set(EXP_LN)
            act.wait_ge(s_w, 16 * WEIGHTS)
            nc.scalar.activation(U[:, :], first, ACT.Exp).then_inc(s_U, 1)
            act.wait_ge(s_U, 1)
            pipelined(act, chain, TURNS, ACT_FRONT, ACT_TURN, front, turn)

        @block.gpsimd
        def _(pool):
            chain = Chain(pool, c_pool, apart)
            for j in two:
                nc.gpsimd.memset(hT[j][:, 0:1], 0.0)
                nc.gpsimd.memset(h2T[j][:, 0:1], 0.0)
                nc.gpsimd.memset(m[j][:, 0:1], -1e38)
                nc.gpsimd.memset(Q[j][:, 0:1], 1.0)
                last = nc.gpsimd.memset(a[j][:, 0:1], 0.0)
            last.then_inc(s_set, 1)
            pool.wait_ge(C["loaded"], C["loads"])
            pool.wait_ge(s_mv, STAT_STEPS)
            nc.gpsimd.tensor_tensor(rs1[:, :], ves[:, :], C["neg_half"][:, 0:UNITS * CT], ALU.pow).then_inc(s_rs1, 1)
            pool.wait_ge(s_var2, 3)
            nc.gpsimd.tensor_tensor(rs2[:, :], t1[:, :], C["neg_half"][:, 0:UNITS * CT], ALU.pow).then_inc(s_rs2, 1)
            with pool.Fori(0, TURNS) as i:
                chain.enter(i * POOL_TURN)
                for j, n in units(i):
                    wait_apart(pool, apart, s_st, n + 1)
                    chain.link(nc.gpsimd.tensor_scalar(ve[j][:, :], mv[j][:, :, 1], EPS, None, ALU.add))
                    nc.gpsimd.tensor_tensor(rst[j][:, :], ve[j][:, :], C["neg_half"][:, 0:CT], ALU.pow).then_inc(s_rst, 1)
                for j, n in units(i):
                    pool.wait_ge(s_relu, n + 1)
                    chain.mark(nc.gpsimd.tensor_tensor(kk[j][:, :, :], rk[j][:, :, :], rk[j][:, :, :], ALU.mult))
                    pool.wait_ge(c_pool, i * POOL_TURN + 3 + j)
                    pool.sem_inc(s_kk2, 1)
                for j, n in units(i):
                    nc.gpsimd.tensor_tensor(xs[j][:, :, :], xp[j][:, :, :], x[:, bass.ts(n, CT), :], ALU.add).then_inc(s_xs, 1)
                chain.leave(POOL_TURN)

        @block.vector
        def _(dve):
            chain = Chain(dve, c_dve)
            V = nc.vector

            def norm(i):
                for j, n in units(i):
                    for c in range(CT):
                        at = bass.ts(n * CT + c, 1)
                        V.tensor_scalar(u[j][:, c, :], x[:, n * CT + c, :], mvs[:, n * CT + c, 0:1], rs1[:, at], ALU.subtract,
                                        ALU.mult)
                        last = V.tensor_scalar(hn[j][:, c, :], x[:, n * CT + c, :], mvs[:, n * CT + c, 0:1], rs12[:, at],
                                               ALU.subtract, ALU.mult)
                    last.then_inc(s_h, 1)

            def mixed(i):
                for j, n in units(i):
                    dve.wait_ge(s_hT, n + 1)
                    now, before = hT[j][:, 1:L + 1], hT[j][:, 0:L]
                    chain.link(V.tensor_tensor(dh[j][:, :], now, before, ALU.subtract))
                    V.scalar_tensor_tensor(xk[j][:, :], dh[j][:, :], mixk, before, ALU.mult, ALU.add)
                    V.scalar_tensor_tensor(xv[j][:, :], dh[j][:, :], mixv, before, ALU.mult, ALU.add)
                    V.scalar_tensor_tensor(xr[j][:, :], dh[j][:, :], mixr, before, ALU.mult, ALU.add).then_inc(s_mix, 1)

            def maxima(i):
                for j, n in units(i):
                    dve.wait_ge(s_kvr, n + 1)
                    chain.link(V.tensor_tensor_scan(m[j][:, 1:L + 1], k_ps[j], decay.to_broadcast([P, L]), -1e38, ALU.max,
                                                    ALU.add))
                    chain.link(V.tensor_tensor(mu[j][:, :], m[j][:, 0:L], k_ps[j], ALU.subtract))
                    V.tensor_scalar(muc[j][:, :], mu[j][:, :], LIM, -LIM, ALU.min, ALU.max).then_inc(s_mu, 1)
                    V.tensor_scalar(rc[j][:, :], r_ps[j], -SIG_CLAMP, None, ALU.max).then_inc(s_rc, 1)

            def denominators(i):
                for j, n in units(i):
                    dve.wait_ge(s_X, n + 1)
                    chain.mark(V.tensor_scalar(e1[j][:, :], X[j][:, :], 1.0, None, ALU.min))
                    chain.link(V.tensor_scalar(e2[j][:, :], Xi[j][:, :], 1.0, None, ALU.min))
                    V.tensor_tensor_scan(Q[j][:, 1:L + 1], e1[j][:, :], e2[j][:, :], 1.0, ALU.mult, ALU.add).then_inc(s_Q, 1)

            def ratios(i):
                for j, n in units(i):
                    dve.wait_ge(s_lnQ, n + 1)
                    V.tensor_tensor(lam[j][:, :], muc[j][:, :], lnQ[j][:, :], ALU.add).then_inc(s_lam, 1)

            def outputs(i):
                for j, n in units(i):
                    dve.wait_ge(s_G, n + 1)
                    chain.mark(V.tensor_scalar(al[j][:, :], G[j][:, :], 1.0, None, ALU.min))
                    chain.link(V.scalar_tensor_tensor(bv[j][:, :], Gi[j][:, :], 1.0, v_ps[j], ALU.min, ALU.mult))
                    chain.link(V.tensor_tensor_scan(a[j][:, 1:L + 1], al[j][:, :], bv[j][:, :], 0.0, ALU.mult, ALU.add))
                for j, n in units(i):
                    chain.link(V.tensor_tensor(d1[j][:, :], a[j][:, 0:L], v_ps[j], ALU.subtract))
                    dve.wait_ge(s_sw, n + 1)
                    chain.link(V.tensor_tensor(d2[j][:, :], d1[j][:, :], sw[j][:, :], ALU.mult))
                    chain.link(V.tensor_tensor(yv[j][:, :], d2[j][:, :], v_ps[j], ALU.add))
                    dve.wait_ge(s_sr, n + 1)
                    V.tensor_tensor(ry[j][:, :], yv[j][:, :], sr[j][:, :], ALU.mult).then_inc(s_ry, 1)

            def front(i):
                norm(i)
                mixed(i)
                maxima(i)
                denominators(i)
                ratios(i)
                outputs(i)

            def turn(i, more):
                for j, n in units(i):
                    dve.wait_ge(s_wp, n + 1)
                    chain.link(V.tensor_tensor(xp[j][:, :, :], tiles(w_ps[j]), u[j][:, :, :], ALU.add))
                    for c in range(CT):
                        last = chain.mark(V.bn_stats(st[j][:, c, :], xp[j][:, c, :]))
                    chain.need(last, apart)
                    for c in range(CT):
                        last = V.bn_aggr(mv[j][:, c, :], st[j][:, c, :])
                    last.then_inc(s_st, 1)
                if more:
                    norm(i + 1)
                for j, n in units(i):
                    dve.wait_ge(s_rst, n + 1)
                    for c in range(CT):
                        last = V.tensor_scalar(h2[j][:, c, :], xp[j][:, c, :], mv[j][:, c, 0:1], rst[j][:, c:c + 1],
                                               ALU.subtract, ALU.mult)
                    last.then_inc(s_h2, 1)
                if more:
                    mixed(i + 1)
                for j, n in units(i):
                    dve.wait_ge(s_h2T, n + 1)
                    now, before = h2T[j][:, 1:L + 1], h2T[j][:, 0:L]
                    chain.link(V.tensor_tensor(dh2[j][:, :], now, before, ALU.subtract))
                    V.scalar_tensor_tensor(ck[j][:, :], dh2[j][:, :], cmixk, before, ALU.mult, ALU.add)
                    V.scalar_tensor_tensor(cr[j][:, :], dh2[j][:, :], cmixr, before, ALU.mult, ALU.add).then_inc(s_cmix, 1)
                if more:
                    maxima(i + 1)
                    denominators(i + 1)
                    ratios(i + 1)
                    outputs(i + 1)
                for j, n in units(i):
                    dve.wait_ge(s_kv, n + 1)
                    V.tensor_scalar(cc[j][:, :], cr_ps[j], -SIG_CLAMP, None, ALU.max).then_inc(s_cc, 1)
                for j, n in units(i):
                    dve.wait_ge(s_sc, n + 1)
                    chain.link(V.tensor_tensor(o[j][:, :, :], tiles(kv_ps[j]), tiles(sc[j][:, :]), ALU.mult))
                    dve.wait_ge(s_xs, n + 1)
                    V.tensor_tensor(x[:, bass.ts(n, CT), :], o[j][:, :, :], xs[j][:, :, :], ALU.add).then_inc(s_out, 1)

            dve.wait_ge(C["loaded"], C["loads"])
            dve.wait_ge(s_w, 16 * WEIGHTS)
            dve.wait_ge(s_set, 1)
            for k in range(4):
                dve.wait_ge(s_x[k], 16)
                with dve.Fori(8 * k, 8 * k + 8) as c:
                    V.bn_stats(sts[:, c, :], x[:, c, :]).then_inc(s_bn, 1)
            dve.wait_ge(s_bn, UNITS * CT)
            stats_to_mean_var(nc, dve, s_mv, sts[:, :, :], mvs[:, :, :], var_eps=ves[:, :])
            dve.wait_ge(s_rs1, 1)
            for step, (dst, p, q) in enumerate(((t1, mvs[:, :, 1], rs1[:, :]), (t2, t1[:, :], rs1[:, :]))):
                V.tensor_tensor(dst[:, :], p, q, ALU.mult).then_inc(s_var2, 1)
                dve.wait_ge(s_var2, step + 1)
            V.tensor_scalar(t1[:, :], t2[:, :], EPS, None, ALU.add).then_inc(s_var2, 1)
            dve.wait_ge(s_rs2, 1)
            V.tensor_tensor(rs12[:, :], rs1[:, :], rs2[:, :], ALU.mult).then_inc(s_rs12, 1)
            dve.wait_ge(s_rs12, 1)
            pipelined(dve, chain, TURNS, DVE_FRONT, DVE_TURN, front, turn)


def ffn_state(nc, ctx):
    t = lambda name, shape, dt=F32: ctx.enter_context(nc.sbuf_tensor("ffn_" + name, shape, dt))
    dram = lambda name, rows: nc.dram_tensor(name, [rows, D], F32, kind="Internal").ap()
    tiles = SEQ * L // P
    return dict(x=t("x", [P, tiles, D]), dest=t("dest", [P, tiles], I32), place=t("place", [P, tiles], I32),
                tables=t("tables", [1, 2 * BLOCKS + EXPERTS], I32),
                w2=t("w2", [P, EXPERTS * DF // P * D]),
                s_x=[ctx.enter_context(nc.semaphore(f"ffn_x_loaded{k}")) for k in range(4)],
                scratch_rows=dram("scratch_rows", ROWS), result_rows=dram("result_rows", BLOCKS * P))


def hybrid_layers(nc, io, out):
    with ExitStack() as ctx:
        C = load_consts(nc, ctx, io)
        F = ffn_state(nc, ctx)
        x1, x2, x3 = (nc.dram_tensor(name, [SEQ, L, D], F32, kind="Internal").ap() for name in ("x1", "x2", "x3"))
        loaded = ctx.enter_context(nc.semaphore("expert_weights_loaded"))
        with nc.Block() as block:
            @block.sync
            def _(sp):
                sp.dma_start(C["tensor"][:, :], io["consts"]).then_inc(C["loaded"], C["loads"])
                sp.dma_start(F["w2"][:, :], io["w2"]).then_inc(loaded, 16)
        gla_phase(nc, io, C, io["x"], x1)
        with nc.Block() as block:
            @block.sync
            def _(sp):
                sp.wait_ge(loaded, 16)
        for use, (source, result) in enumerate(((x1, x2), (x3, out))):
            F["use"] = use + 1
            ffn_attention(nc, io, C, F, source, f"att{use}_")
            ffn_experts(nc, io, C, F, f"experts{use}_")
            ffn_gather(nc, io, C, F, result, f"gather{use}_")
            if use == 0:
                rwkv_phase(nc, io, C, x2, x3)


def laid_out(inputs):
    a = {k[len("L0_attn_a_"):]: v for k, v in inputs.items() if k.startswith("L0_attn_a_")}
    b = {k[len("L0_attn_b_"):]: v for k, v in inputs.items() if k.startswith("L0_attn_b_")}
    f = {k[len("L0_ffn_"):]: v for k, v in inputs.items() if k.startswith("L0_ffn_")}
    fc = DF // P
    w1b = np.concatenate([f["W1"].transpose(1, 0, 2), f["b1"].reshape(EXPERTS, fc, P).transpose(2, 0, 1),
                          np.broadcast_to(f["b2"][None], (P, EXPERTS, D))], 2).transpose(1, 0, 2)
    rows = ("ln1_g", "ln1_b", "ln2_g", "ln2_b", "mix_k", "mix_v", "mix_r", "cmix_k", "cmix_r", "time_decay",
            "time_first")
    io = {
        "x": a["x"], "consts": const_array(),
        "Wq": a["Wq"], "Wk": a["Wk"], "Wv": a["Wv"], "Wg": a["Wg"], "gk_w1T": a["gk_w1"].T, "gk_w2": a["gk_w2"],
        "Wo_a": a["Wo"], "g_norm_col": np.tile(a["g_norm_w"], 2)[:, None], "gk_b2_col": a["gk_b2"][:, None],
        "WqT": f["Wqkv"][0:P].T, "WkT": f["Wqkv"][P:2 * P].T, "WvT": f["Wqkv"][2 * P:3 * P].T, "WoT": f["Wo"].T,
        "WgT": f["Wg"].T, "bq_col": f["bqkv"][0:P, None], "bk_col": f["bqkv"][P:2 * P, None],
        "bv": f["bqkv"][2 * P:3 * P], "bo": f["bo"], "g1": f["g1"], "be1": f["be1"], "g2": f["g2"], "be2": f["be2"],
        "w1b": w1b, "w2": f["W2"].reshape(EXPERTS, fc, P, D).transpose(2, 0, 1, 3).reshape(P, -1),
        "zeros": np.zeros((P, P), np.float32), "zeros8": np.zeros((P, EXPERTS, P), np.float32),
        "w_tk": b["w_tk"], "w_tv": b["w_tv"], "w_tr": b["w_tr"], "w_cr": b["w_cr"], "w_ck": b["w_ck"],
        "w_cv": b["w_cv"], "rwkv_cols": np.stack([b[k].reshape(-1) for k in rows], 1),
    }
    return {k: np.ascontiguousarray(v) for k, v in io.items()}


def kernel(**inputs):
    import concourse.bacc as bacc
    from concourse.bass_utils import run_bass_kernel_spmd

    nc = bacc.Bacc("TRN2", target_bir_lowering=False, num_devices=1)
    arrays, io = {}, {}
    for name, array in laid_out({k: np.asarray(v) for k, v in inputs.items()}).items():
        arrays[f"in_{name}_dram"] = array
        io[name] = nc.dram_tensor(f"in_{name}_dram", array.shape, mybir.dt.from_np(array.dtype),
                                  kind="ExternalInput").ap()
    out = nc.dram_tensor("out_0_dram", [SEQ, L, D], F32, kind="ExternalOutput").ap()
    hybrid_layers(nc, io, out)
    result = run_bass_kernel_spmd(nc, [arrays], core_ids=[0])
    return result.results[0]["out_0_dram"]
```

```python
from contextlib import ExitStack
import numpy as np
import concourse.bass as bass
import concourse.mybir as mybir

F32, I32, BF16 = mybir.dt.float32, mybir.dt.int32, mybir.dt.bfloat16
ALU, ACT, AX = mybir.AluOpType, mybir.ActivationFunctionType, mybir.AxisListType
P, D, SEQ, L = 128, 128, 16, 256
EPS = 1e-5
EXP_LN = "natural_log_exp_and_others"
SIG_CLAMP = 40.0

class PhaseSemaphores:
    def __init__(self, nc, ctx, tag):
        self.nc, self.tag, self.sems = nc, tag, []
        ctx.callback(self.clear)

    def __call__(self, name):
        self.sems.append(self.nc.alloc_semaphore(name=self.tag + name))
        return self.sems[-1]

    def clear(self):
        self.nc.clear_and_free_semaphores(self.sems)
        self.nc.all_engine_barrier()


def wait_apart(eng, apart, sem, value):
    eng.wait_ge(sem, value)
    if apart is not None and not isinstance(value, int):
        eng.sem_inc(apart, 1)


class Chain:
    def __init__(self, eng, sem, apart=None):
        self.eng, self.sem, self.apart, self.base, self.n = eng, sem, apart, 0, 0

    def enter(self, base):
        self.base, self.n = base, 0

    def mark(self, ins):
        self.n += 1
        ins.then_inc(self.sem, 1)
        return self.n

    def need(self, n, apart=None):
        wait_apart(self.eng, apart or self.apart, self.sem, self.base + n)

    def link(self, ins, apart=None):
        self.need(self.mark(ins), apart)

    def leave(self, steps):
        assert self.n == steps, (self.n, steps)


def pipelined(eng, chain, turns, front_steps, turn_steps, front, turn):
    front(0)
    chain.leave(front_steps)
    with eng.Fori(0, turns - 1) as i:
        chain.enter(i * turn_steps + front_steps)
        turn(i, True)
        chain.leave(turn_steps)
    chain.enter((turns - 1) * turn_steps + front_steps)
    turn(turns - 1, False)


STAT_STEPS = 5


def stats_to_mean_var(nc, dve, sem, st, mv, var_eps, base=0):
    def step(n, ins):
        ins.then_inc(sem, 1)
        dve.wait_ge(sem, base + n)
    step(1, nc.vector.tensor_tensor(mv[:, :, 0], st[:, :, 1], st[:, :, 4], ALU.subtract))
    step(2, nc.vector.scalar_tensor_tensor(mv[:, :, 1], mv[:, :, 0], 0.25, mv[:, :, 0], ALU.mult, ALU.mult))
    step(3, nc.vector.scalar_tensor_tensor(var_eps, st[:, :, 2], 1.0 / 128, mv[:, :, 1], ALU.mult, ALU.add))
    step(4, nc.vector.scalar_tensor_tensor(mv[:, :, 1], st[:, :, 5], 1.0 / 128, var_eps, ALU.mult, ALU.add))
    nc.vector.tensor_scalar(var_eps, mv[:, :, 1], EPS, None, ALU.add)
    nc.vector.scalar_tensor_tensor(mv[:, :, 0], mv[:, :, 0], 0.5, st[:, :, 4], ALU.mult, ALU.add).then_inc(sem, 1)


CONST_COLS = {}
EXPERTS, DF = 8, 512
REGION = SEQ * L + P
BLOCKS = SEQ * L // P + EXPERTS
ROWS = EXPERTS * REGION + EXPERTS * P


def const_array():
    p = np.arange(P)
    e = np.arange(EXPERTS)
    cols = []
    CONST_COLS.clear()

    def put(name, a):
        CONST_COLS[name] = (sum(c.shape[1] for c in cols), a.shape[1])
        cols.append(a.astype(np.float32))

    row = lambda v: np.broadcast_to(np.asarray(v)[None, :], (P, len(v)))
    put("ident", np.eye(P))
    put("causal", p[:, None] <= p[None, :])
    put("strict", p[:, None] < p[None, :])
    put("ones", np.ones((P, 256)))
    put("headmask", (p[:, None] // 32) == (np.arange(256)[None, :] // 64))
    put("pairmask", np.where((p[:, None] // 64) == (np.arange(32)[None, :] // 16), 0.0, -1e30))
    put("neg_half", np.full((P, 32), -0.5))
    put("expert_less_8", row(e - EXPERTS))
    put("region_start", row(e * REGION))
    put("region_end", row((e + 1) * REGION))
    put("block", row(np.arange(BLOCKS)))
    return np.concatenate(cols, 1)


def load_consts(nc, ctx, io):
    const_array()
    t = ctx.enter_context(nc.sbuf_tensor("consts", list(io["consts"].shape), F32))
    s = ctx.enter_context(nc.semaphore("consts_loaded"))
    C = {k: t[:, a:a + n] for k, (a, n) in CONST_COLS.items()}
    C["ones_row"] = C["ones"]
    C["causal4"] = C["causal"].unsqueeze(1).to_broadcast([P, 4, P])
    C["loaded"], C["loads"], C["tensor"] = s, 16, t
    return C


def gla_phase(nc, io, C, x_dram, x1_dram):
    UNITS, CH = 16, 2
    GATE, SCALE, CLAMP = 1.0 / 16.0, 32.0 ** -0.5, 16.0 * 80.0
    WEIGHTS = 9
    with ExitStack() as ctx:
        sb = lambda name, shape: ctx.enter_context(nc.sbuf_tensor("gla_" + name, shape, F32))
        sem = PhaseSemaphores(nc, ctx, "gla_")
        each = lambda name, shape: [sb(f"{name}{j}", shape) for j in range(2)]
        x = sb("x", [P, UNITS * CH, D])
        wqk, wvg, w1t, w2, w12 = sb("wqk", [P, 256]), sb("wvg", [P, 512]), sb("w1t", [16, P]), sb("w2", [16, P]), sb("w12", [P, P])
        wo, won, wn, b2 = sb("wo", [P, 2, D]), sb("won", [P, 2, D]), sb("wn", [P, 1]), sb("b2", [P, 1])
        st, mv, ve, rs = each("st", [P, CH, 6]), each("mv", [P, CH, 2]), each("ve", [P, CH]), each("rs", [P, CH])
        h, hT = each("h", [P, CH, D]), each("hT", [P, L])
        za, ze, zl, zm, zg = (each(k, [P, L]) for k in ("za", "ze", "zl", "zm", "zg"))
        cum, dl, dc, eq, ek, qt, kt = (each(k, [P, L]) for k in ("cum", "dl", "dc", "eq", "ek", "qt", "kt"))
        dm, dS = each("dm", [P, 1]), each("dS", [P, 1])
        v, gc, qx = each("v", [P, CH, 256]), each("gc", [P, CH, 256]), each("qx", [P, CH, 4, P])
        ktok, S, am = each("ktok", [P, P]), each("S", [P, 256]), each("am", [P, CH, 4, P])
        ge, gl, gs, gg = (each(k, [P, CH, 256]) for k in ("ge", "gl", "gs", "gg"))
        sq, ss, sv, rr = each("sq", [P, CH * 256]), each("ss", [P, 8]), each("sv", [P, 8]), each("rr", [P, 8])
        og, on, oT = each("og", [P, CH, 256]), each("on", [P, CH, 256]), each("oT", [P, 4, P])
        ps = ctx.enter_context(nc.psum_tensor("gla_ps", [P, 8, 512], F32))
        hT_ps = z_ps = ps[:, 0, 0:256]
        q_ps, k_ps = ps[:, 1, 0:256], ps[:, 1, 256:512]
        kt_ps, u_ps = ps[:, 1, 0:P], ps[:, 1, 256:512]
        v_ps, g_ps = ps[:, 2, :], ps[:, 3, :]
        a_ps = lambda c: ps[:, 4 + c, :]
        o_ps = ps[:, 6, :]
        oT_ps, out_ps = ps[:, 7, :], ps[:, 7, 0:256]
        two_chunks = lambda a: a.rearrange("p (c e) -> p c e", c=CH)

        s_w, s_w12, s_w12c, s_won, s_qz = (sem(k) for k in (
            "weights_loaded", "w12_product", "w12_copied", "won_ready", "qx_zeroed"))
        s_x = [sem(f"x_loaded{j}") for j in range(2)]
        s_mv, s_rs, s_h, s_hTp, s_hT, s_z, s_zl, s_dec, s_e = (sem(k) for k in (
            "x_stats", "x_rstd", "normed", "hT_psum", "hT_copied", "gate_product", "softplus", "decay_ready", "decay_exp"))
        s_qk, s_vp, s_gp, s_v, s_gc, s_qt, s_qx = (sem(k) for k in (
            "qk_product", "v_product", "g_product", "v_copied", "g_clamped", "qk_decayed", "qx_ready"))
        s_ktp, s_ktok, s_u, s_S, s_a, s_am, s_o, s_gs, s_gg = (sem(k) for k in (
            "k_transposed", "k_copied", "state_product", "state_ready", "scores", "scores_masked", "o_product",
            "g_sigmoid", "g_silu"))
        s_sq, s_ss, s_rr, s_og, s_on, s_oTp, s_oT, s_out, s_x1, s_st = (sem(k) for k in (
            "o_squared", "o_sums", "o_rstd", "o_gated", "o_normed", "oT_psum", "oT_copied", "out_product", "x1_ready",
            "x1_stored"))
        c_dve_s, c_dve_a, c_act_a, c_act_b, c_pool_s, c_pool_c, apart = (sem(k) for k in (
            "dve_steps_statistics", "dve_steps_projections", "act_steps_projections", "act_steps_attention",
            "pool_steps_statistics", "pool_steps_output", "apart"))

        def bodies(eng, body):
            for n in range(-3, 1):
                body(n, n % 2, [n + k >= 0 for k in range(-1, 4)])
            with eng.Fori(0, (UNITS - 4) // 2) as i:
                for k in range(2):
                    body(2 * i + k + 1, (k + 1) % 2, [True] * 5)
            for n in range(UNITS - 3, UNITS + 1):
                body(n, n % 2, [n + k < UNITS for k in range(-1, 4)])

        def q_of_head(j, hd):
            rows = slice(32 * hd, 32 * hd + 32)
            return qx[j][rows, :, hd, :], qt[j][rows, :].rearrange("p (c t) -> p c t", c=CH)

        block = ctx.enter_context(nc.Block())

        @block.sync
        def _(sp):
            def load(n, j):
                sp.dma_start(x[:, bass.ds(n * CH, CH), :], x_dram[bass.ds(n, 1)].rearrange("s (c p) d -> p (s c) d", p=P)
                             ).then_inc(s_x[j], 16)
            for j in range(2):
                load(j, j)
            with sp.Fori(0, UNITS // 2 - 1) as i:
                for j in range(2):
                    sp.wait_ge(s_x[j], 16 * i + 16)
                    load(2 * i + 2 + j, j)
            with sp.Fori(0, UNITS) as n:
                sp.wait_ge(s_x1, n + 1)
                sp.dma_start(x1_dram[bass.ts(n, 1)].rearrange("s (c p) d -> p (s c) d", p=P),
                             x[:, bass.ts(n, CH), :]).then_inc(s_st, 16)
            sp.wait_ge(s_st, 16 * UNITS)

        @block.tensor
        def _(pe):
            def body(n, j, has):
                d, c, b, a = n - 1, n, n + 1, n + 2
                bj, dj, has_d, has_c, has_b, has_a = 1 - j, 1 - j, *has[0:4]
                if has_b:
                    pe.wait_ge(s_qt, b + 1)
                    nc.tensor.transpose(kt_ps, kt[bj][:, 0:P], C["ident"]).then_inc(s_ktp, 1)
                if has_a:
                    pe.wait_ge(s_h, a + 1)
                    for ch in range(CH):
                        last = nc.tensor.transpose(hT_ps[:, P * ch:P * ch + P], h[j][:, ch, :], C["ident"])
                    last.then_inc(s_hTp, 1)
                if has_b:
                    pe.wait_ge(s_qx, b + 1)
                    nc.tensor.matmul(a_ps(0), kt[bj][:, 0:P], qx[bj][:, 0, :, :], start=True, stop=True).then_inc(s_a, 1)
                if has_d:
                    pe.wait_ge(s_on, d + 1)
                    if not isinstance(n, int) or n > 1:
                        pe.wait_ge(s_x1, d)
                    for ch in range(CH):
                        for half in range(2):
                            last = nc.tensor.transpose(oT_ps[:, P * (2 * ch + half):P * (2 * ch + half) + P],
                                                       on[dj][:, ch, P * half:P * half + P], C["ident"])
                    last.then_inc(s_oTp, 1)
                if has_a:
                    pe.wait_ge(s_hT, a + 1)
                    nc.tensor.matmul(z_ps, w12[:, :], hT[j][:, :], start=True, stop=True).then_inc(s_z, 1)
                if has_b:
                    nc.tensor.matmul(a_ps(1), kt[bj][:, P:256], qx[bj][:, 1, :, :], start=True, stop=True).then_inc(s_a, 1)
                    pe.wait_ge(s_ktok, b + 1)
                    pe.wait_ge(s_v, b + 1)
                    nc.tensor.matmul(u_ps, ktok[bj][:, :], v[bj][:, 0, :], start=True, stop=True).then_inc(s_u, 1)
                if has_a:
                    for ch in range(CH):
                        last = nc.tensor.matmul(v_ps[:, 256 * ch:256 * ch + 256], hT[j][:, P * ch:P * ch + P],
                                                wvg[:, 0:256], start=True, stop=True)
                    last.then_inc(s_vp, 1)
                    if has_b:
                        pe.wait_ge(s_gc, b + 1)
                    for ch in range(CH):
                        last = nc.tensor.matmul(g_ps[:, 256 * ch:256 * ch + 256], hT[j][:, P * ch:P * ch + P],
                                                wvg[:, 256:512], start=True, stop=True)
                    last.then_inc(s_gp, 1)
                    if has_b:
                        pe.wait_ge(s_S, b + 1)
                    nc.tensor.matmul(q_ps, wqk[:, 0:P], hT[j][:, :], start=True, stop=True)
                    nc.tensor.matmul(k_ps, wqk[:, P:256], hT[j][:, :], start=True, stop=True).then_inc(s_qk, 1)
                if has_d:
                    pe.wait_ge(s_oT, d + 1)
                    for ch in range(CH):
                        for half in range(2):
                            last = nc.tensor.matmul(out_ps[:, P * ch:P * ch + P], oT[dj][:, 2 * ch + half, :],
                                                    won[:, half, :], start=(half == 0), stop=(half == 1))
                    last.then_inc(s_out, 1)
                if has_b:
                    if has_c:
                        pe.wait_ge(s_og, c + 1)
                    pe.wait_ge(s_am, (b + 1) * CH)
                    for ch in range(CH):
                        for hd in range(4):
                            nc.tensor.matmul(o_ps[:, 256 * ch + 64 * hd:256 * ch + 64 * hd + 64], am[bj][:, ch, hd, :],
                                             v[bj][:, ch, 64 * hd:64 * hd + 64], start=(ch == 0 and hd == 0), stop=False,
                                             skip_group_check=True)
                    pe.wait_ge(s_S, b + 1)
                    nc.tensor.matmul(o_ps[:, 256:512], qt[bj][:, P:256], S[bj][:, :], start=False, stop=True,
                                     skip_group_check=True).then_inc(s_o, 1)

            pe.wait_ge(C["loaded"], C["loads"])
            pe.wait_ge(s_w, 16 * WEIGHTS)
            nc.tensor.matmul(ps[:, 0, 0:P], w1t[:, :], w2[:, :], start=True, stop=True).then_inc(s_w12, 1)
            pe.wait_ge(s_w12c, 1)
            pe.wait_ge(s_won, 1)
            bodies(pe, body)

        @block.scalar
        def _(act):
            in_a, in_b = Chain(act, c_act_a), Chain(act, c_act_b)

            def body(n, j, has):
                d, c, b, a = n - 1, n, n + 1, n + 2
                bj, dj, has_d, has_c, has_b, has_a = 1 - j, 1 - j, *has[0:4]
                in_a.enter(a * 2)
                in_b.enter(b * 2)
                if has_c:
                    act.wait_ge(s_o, c + 1)
                    nc.scalar.activation(sq[j][:, :], o_ps, ACT.Square).then_inc(s_sq, 1)
                if has_b:
                    act.wait_ge(s_ktp, b + 1)
                    nc.scalar.activation(ktok[bj][:, :], kt_ps, ACT.Copy).then_inc(s_ktok, 1)
                if has_a:
                    act.wait_ge(s_hTp, a + 1)
                    nc.scalar.activation(hT[j][:, :], hT_ps, ACT.Copy).then_inc(s_hT, 1)
                if has_d:
                    act.wait_ge(s_oTp, d + 1)
                    nc.scalar.activation(oT[dj][:, :, :], oT_ps, ACT.Copy).then_inc(s_oT, 1)
                if has_b:
                    act.wait_ge(s_gc, b + 1)
                    in_b.link(nc.scalar.activation(ge[bj][:, :, :], gc[bj][:, :, :], ACT.Exp, scale=-1.0))
                    in_b.mark(nc.scalar.activation(gl[bj][:, :, :], ge[bj][:, :, :], ACT.Ln, bias=1.0))
                if has_a:
                    act.wait_ge(s_z, a + 1)
                    in_a.link(nc.scalar.activation(za[j][:, :], z_ps, ACT.Abs, bias=b2[:, :]))
                    in_a.link(nc.scalar.activation(ze[j][:, :], za[j][:, :], ACT.Exp, scale=-1.0))
                    nc.scalar.activation(zl[j][:, :], ze[j][:, :], ACT.Ln, bias=1.0).then_inc(s_zl, 1)
                if has_b:
                    in_b.need(2)
                    nc.scalar.activation(gs[bj][:, :, :], gl[bj][:, :, :], ACT.Exp, scale=-1.0).then_inc(s_gs, 1)
                if has_a:
                    act.wait_ge(s_vp, a + 1)
                    nc.scalar.activation(v[j][:, :, :], two_chunks(v_ps), ACT.Copy).then_inc(s_v, 1)
                    act.wait_ge(s_dec, a + 1)
                    nc.scalar.activation(eq[j][:, :], dc[j][:, :], ACT.Exp, scale=GATE)
                    nc.scalar.activation(ek[j][:, :], dc[j][:, :], ACT.Exp, scale=-GATE)
                    nc.scalar.activation(dS[j][:, :], dm[j][:, :], ACT.Exp, scale=GATE).then_inc(s_e, 1)
                if has_a:
                    act.wait_ge(s_qt, a + 1)
                    for hd in range(4):
                        last = nc.scalar.activation(*q_of_head(j, hd), ACT.Copy)
                    last.then_inc(s_qx, 1)

            for dst, src in ((wqk[:, 0:P], io["Wq"]), (wqk[:, P:256], io["Wk"]), (wvg[:, 0:256], io["Wv"]),
                             (wvg[:, 256:512], io["Wg"]), (w1t[:, :], io["gk_w1T"]), (w2[:, :], io["gk_w2"]),
                             (wo[:, :, :], io["Wo_a"].rearrange("(c p) d -> p c d", p=P)),
                             (wn[:, :], io["g_norm_col"]), (b2[:, :], io["gk_b2_col"])):
                act.dma_start(dst, src).then_inc(s_w, 16)
            act.preload_act_table_set(EXP_LN)
            act.wait_ge(s_w, 16 * WEIGHTS)
            act.wait_ge(s_qz, 2)
            bodies(act, body)

        @block.gpsimd
        def _(pool):
            in_s, in_c = Chain(pool, c_pool_s, apart), Chain(pool, c_pool_c, apart)

            def body(n, j, has):
                d, c, b, a, s = n - 1, n, n + 1, n + 2, n + 3
                dj, bj, sj, has_d, has_c, has_b, has_a, has_s = 1 - j, 1 - j, 1 - j, *has
                in_s.enter(s)
                in_c.enter(c)
                if has_s:
                    wait_apart(pool, apart, s_mv, s + 1)
                    in_s.link(nc.gpsimd.tensor_scalar(ve[sj][:, :], mv[sj][:, :, 1], EPS, None, ALU.add))
                    nc.gpsimd.tensor_tensor(rs[sj][:, :], ve[sj][:, :], C["neg_half"][:, 0:CH], ALU.pow).then_inc(s_rs, 1)
                if has_c:
                    wait_apart(pool, apart, s_ss, c + 1)
                    in_c.link(nc.gpsimd.tensor_scalar(sv[j][:, :], ss[j][:, :], 1.0 / 64, EPS, ALU.mult, ALU.add))
                    nc.gpsimd.tensor_tensor(rr[j][:, :], sv[j][:, :], C["neg_half"][:, 0:8], ALU.pow).then_inc(s_rr, 1)
                    pool.wait_ge(s_rr, c + 1)
                    wait_apart(pool, apart, s_og, c + 1)
                    nc.gpsimd.tensor_tensor(on[j][:, :, :].rearrange("p c (g e) -> p (c g) e", e=64),
                                            og[j][:, :, :].rearrange("p c (g e) -> p (c g) e", e=64),
                                            rr[j][:, :].unsqueeze(2).to_broadcast([P, 8, 64]), ALU.mult).then_inc(s_on, 1)
                if has_b:
                    pool.wait_ge(s_gs, b + 1)
                    nc.gpsimd.tensor_tensor(gg[bj][:, :, :], gc[bj][:, :, :], gs[bj][:, :, :], ALU.mult).then_inc(s_gg, 1)

            for j in range(2):
                nc.gpsimd.memset(qx[j][:, :, :, :], 0.0).then_inc(s_qz, 1)
            pool.wait_ge(s_qz, 2)
            pool.wait_ge(C["loaded"], C["loads"])
            bodies(pool, body)

        @block.vector
        def _(dve):
            in_s, in_a = Chain(dve, c_dve_s, apart), Chain(dve, c_dve_a)
            V = nc.vector

            def body(n, j, has):
                d, c, b, a, s = n - 1, n, n + 1, n + 2, n + 3
                dj, bj, sj, has_d, has_c, has_b, has_a, has_s = 1 - j, 1 - j, 1 - j, *has
                in_s.enter(s * CH)
                in_a.enter(a * 5)
                if has_c:
                    dve.wait_ge(s_sq, c + 1)
                    V.tensor_reduce(ss[j][:, :], sq[j][:, :].rearrange("p (g e) -> p g e", e=64), AX.X, ALU.add
                                    ).then_inc(s_ss, 1)
                    dve.wait_ge(s_gg, c + 1)
                    V.tensor_tensor(og[j][:, :, :], two_chunks(o_ps), gg[j][:, :, :], ALU.mult).then_inc(s_og, 1)
                if has_b:
                    for ch in range(CH):
                        dve.wait_ge(s_a, b * CH + ch + 1)
                        V.tensor_tensor(am[bj][:, ch, :, :], a_ps(ch).rearrange("p (g t) -> p g t", g=4),
                                        C["causal4"], ALU.mult).then_inc(s_am, 1)
                    dve.wait_ge(s_u, b + 1)
                    V.scalar_tensor_tensor(S[bj][:, :], u_ps, dS[bj][:, 0:1], C["headmask"], ALU.mult, ALU.mult
                                           ).then_inc(s_S, 1)
                if has_s:
                    dve.wait_ge(s_x[sj], s // 2 * 16 + 16 if isinstance(s, int) else s * 8 + (16 - 8 * sj))
                    for ch in range(CH):
                        last = in_s.mark(V.bn_stats(st[sj][:, ch, :], x[:, s * CH + ch, :]))
                    in_s.need(last)
                    for ch in range(CH):
                        last = V.bn_aggr(mv[sj][:, ch, :], st[sj][:, ch, :])
                    last.then_inc(s_mv, 1)
                if has_a:
                    dve.wait_ge(s_zl, a + 1)
                    in_a.link(V.tensor_scalar(zm[j][:, :], z_ps, b2[:, 0:1], 0.0, ALU.add, ALU.min))
                    in_a.link(V.tensor_tensor(zg[j][:, :], zm[j][:, :], zl[j][:, :], ALU.subtract))
                    in_a.link(V.tensor_tensor_scan(cum[j][:, :], C["ones_row"], zg[j][:, :], 0.0, ALU.mult, ALU.add))
                    for ch in range(CH):
                        mid = cum[j][:, P * ch + P // 2 - 1:P * ch + P // 2]
                        last = in_a.mark(V.tensor_scalar(dl[j][:, P * ch:P * ch + P], cum[j][:, P * ch:P * ch + P],
                                                         mid, -CLAMP, ALU.subtract, ALU.max))
                    V.tensor_tensor(dm[j][:, :], cum[j][:, P + P // 2 - 1:P + P // 2], cum[j][:, P // 2 - 1:P // 2],
                                    ALU.subtract)
                    in_a.need(last)
                    V.tensor_scalar(dc[j][:, :], dl[j][:, :], CLAMP, None, ALU.min).then_inc(s_dec, 1)
                if has_d:
                    dve.wait_ge(s_out, d + 1)
                    xs = x[:, bass.ds(d * CH, CH), :]
                    V.tensor_tensor(xs, xs, two_chunks(out_ps), ALU.add).then_inc(s_x1, 1)
                if has_a:
                    dve.wait_ge(s_gp, a + 1)
                    V.tensor_scalar(gc[j][:, :, :], two_chunks(g_ps), -SIG_CLAMP, None, ALU.max).then_inc(s_gc, 1)
                    dve.wait_ge(s_e, a + 1)
                    dve.wait_ge(s_qk, a + 1)
                    V.scalar_tensor_tensor(qt[j][:, :], q_ps, SCALE, eq[j][:, :], ALU.mult, ALU.mult)
                    V.tensor_tensor(kt[j][:, :], k_ps, ek[j][:, :], ALU.mult).then_inc(s_qt, 1)
                if has_s:
                    dve.wait_ge(s_rs, s + 1)
                    for ch in range(CH):
                        last = V.tensor_scalar(h[sj][:, ch, :], x[:, s * CH + ch, :], mv[sj][:, ch, 0:1],
                                               rs[sj][:, ch:ch + 1], ALU.subtract, ALU.mult)
                    last.then_inc(s_h, 1)

            dve.wait_ge(C["loaded"], C["loads"])
            dve.wait_ge(s_w, 16 * WEIGHTS)
            V.tensor_scalar(won[:, :, :], wo[:, :, :], wn[:, 0:1], None, ALU.mult).then_inc(s_won, 1)
            dve.wait_ge(s_w12, 1)
            V.tensor_copy(w12[:, :], ps[:, 0, 0:P]).then_inc(s_w12c, 1)
            bodies(dve, body)


def ffn_attention(nc, io, C, F, x_dram, tag):
    UNITS, PAIR, CT = 16, 2, 2
    TURNS = UNITS // PAIR
    TILES = UNITS * CT
    DVE_FRONT, DVE_TURN, POOL_TURN = 6, 32, 2
    SCALE = 32.0 ** -0.5
    with ExitStack() as ctx:
        sb = lambda name, shape, dt=F32: ctx.enter_context(nc.sbuf_tensor(tag + name, shape, dt))
        sem = PhaseSemaphores(nc, ctx, tag)
        two = range(PAIR)
        x = F["x"]
        wq, wk, wv, wo = sb("wq", [P, P]), sb("wk", [P, P]), sb("wv", [P, P]), sb("wo", [P, P])
        wg = sb("wg", [P, EXPERTS])
        bq, bk, bv = sb("bq", [P, 1]), sb("bk", [P, 1]), sb("bv", [P, 1])
        bo, g1, be1 = sb("bo", [P, P]), sb("g1", [P, P]), sb("be1", [P, P])
        strict16, ones16 = sb("strict16", [P, P], BF16), sb("ones16", [P, P], BF16)
        mask = sb("mask", [P, 8, 32])
        zeros = sb("zeros", [P, P])
        sts, mvs = sb("sts", [P, TILES, 6]), sb("mvs", [P, TILES, 2])
        ves, rstd = sb("ves", [P, TILES]), sb("rstd", [P, TILES])
        each = lambda name, shape, dt=F32: [sb(f"{name}{j}", shape, dt) for j in two]
        h, hb, hT = each("h", [P, CT, D]), each("hb", [P, CT, D]), each("hT", [P, 256])
        qx, kT, v = each("qx", [P, 16, 4, 16]), each("kT", [P, 256]), each("v", [P, CT, P])
        mx, sd, ex = each("mx", [P, 8]), each("sd", [P, 8, 32]), each("ex", [P, 8, 32])
        su, rs, pr = each("su", [P, 8]), each("rs", [P, 8]), each("pr", [P, 8, 32])
        ptx, oT = each("ptx", [P, CT, 4, P]), each("oT", [P, CT, P])
        r, st, mv, ve, rst = (each("r", [P, CT, D]), each("st", [P, CT, 6]), each("mv", [P, CT, 2]), each("ve", [P, CT]),
                              each("rst", [P, CT]))
        rg, y, yT = each("rg", [P, CT, D]), each("y", [P, CT, D]), each("yT", [P, 256])
        lmx, eq, ei, em, oh = (each("lmx", [P, CT]), each("eq", [P, CT, EXPERTS]), each("ei", [P, CT, EXPERTS]),
                               each("em", [P, CT]), each("oh", [P, CT, EXPERTS]))
        oh16 = each("oh16", [P, CT, EXPERTS], BF16)
        rk, rsel, dest, base = (each("rk", [P, CT, EXPERTS]), each("rsel", [P, CT, EXPERTS]), each("dest", [P, CT], I32),
                                each("base", [P, EXPERTS]))
        ps = ctx.enter_context(nc.psum_tensor(tag + "ps", [P, 8, 512], F32))
        bank = lambda j, b: ps[:, 4 * j + b, :]
        hT_ps = [bank(j, 0)[:, 0:256] for j in two]
        s_ps = [bank(j, 0)[:, 256:512] for j in two]
        q_ps = [bank(j, 1)[:, 0:256] for j in two]
        pt_ps = [bank(j, 1)[:, 256:512] for j in two]
        k_ps = [bank(j, 2)[:, 0:256] for j in two]
        v_ps = [bank(j, 2)[:, 256:512] for j in two]
        pv_ps = [bank(j, 3)[:, 0:256] for j in two]
        mha_ps = [bank(j, 3)[:, 256:512] for j in two]
        yT_ps = [bank(j, 3)[:, 0:256] for j in two]
        lg_ps = [bank(j, 3)[:, 256:272] for j in two]
        rank_ps = [bank(j, 3)[:, 288:312] for j in two]

        (s_w, s_bn, s_aggr, s_rstd, s_h, s_hb, s_hTp, s_hT, s_q, s_kv, s_qx, s_kvc, s_s, s_sd, s_ex, s_pr, s_pt, s_pxa,
         s_pxd, s_pv, s_oT, s_mha, s_st, s_rst, s_y, s_yTp, s_yT, s_lg, s_oh, s_rank, s_dest, s_scat, s_zero,
         s_c16, s_tab) = (sem(k) for k in (
             "weights_loaded", "bn_stats", "mean_var", "rstd", "normed", "h_plus_bo", "hT_psum", "hT_copied", "q_product",
             "kv_product", "q_spread", "kv_copied", "scores", "scores_less_max", "scores_exp", "probs", "probsT_psum",
             "probsT_spread_by_act", "probsT_spread_by_dve", "pv_product", "oT_copied", "mha_product",
             "r_stats", "r_rstd", "y_ready", "yT_psum", "yT_copied", "logits", "one_hot", "ranks", "dest_ready",
             "scattered", "spreads_zeroed", "masks_ready", "tables_ready"))
        c_dve, c_pool = sem("dve_steps"), sem("pool_steps")
        units = lambda i: [(j, i * PAIR + j) for j in two]
        WEIGHTS = 13
        apart = sem("apart")
        block = ctx.enter_context(nc.Block())

        @block.sync
        def _(sp):
            for k in range(4):
                for lp in range(8):
                    sp.dma_start(x[16 * lp:16 * lp + 16, 8 * k:8 * k + 8, :],
                                 x_dram.rearrange("s (g l) d -> l s g d", l=8)[lp, :, 8 * k:8 * k + 8, :]
                                 ).then_inc(F["s_x"][k], 16)

        def row(a, lo=0, hi=P):
            return a[lo:hi].unsqueeze(0).to_broadcast([P, hi - lo])

        def pT_quarter(j, k):
            rows = slice(32 * k, 32 * k + 32)
            return ptx[j][rows, :, k, :], pt_ps[j][rows, :].rearrange("p (c e) -> p c e", c=CT)

        @block.tensor
        def _(pe):
            def to_hT(i):
                for j, n in units(i):
                    pe.wait_ge(s_h, n + 1)
                    for c in range(CT):
                        last = nc.tensor.transpose(hT_ps[j][:, P * c:P * c + P], h[j][:, c, :], C["ident"])
                    last.then_inc(s_hTp, 1)

            def qkv(i):
                for j, n in units(i):
                    pe.wait_ge(s_hT, n + 1)
                    nc.tensor.matmul(q_ps[j], wq[:, :], hT[j][:, :], start=True, stop=True).then_inc(s_q, 1)
                    nc.tensor.matmul(k_ps[j], wk[:, :], hT[j][:, :], start=True, stop=True)
                    for c in range(CT):
                        last = nc.tensor.matmul(v_ps[j][:, P * c:P * c + P], hT[j][:, P * c:P * c + P], wv[:, :],
                                                start=True, stop=True)
                    last.then_inc(s_kv, 1)

            def scores(i):
                for j, n in units(i):
                    pe.wait_ge(s_qx, n + 1)
                    pe.wait_ge(s_kvc, n + 1)
                    nc.tensor.matmul(s_ps[j], C["ident"], mask[:, :, :], start=True, stop=False, skip_group_check=True)
                    for pair in range(8):
                        last = nc.tensor.matmul(s_ps[j][:, 32 * pair:32 * pair + 32], qx[j][:, 2 * pair:2 * pair + 2, :, :],
                                                kT[j][:, 32 * pair:32 * pair + 32], start=False, stop=(pair == 7),
                                                skip_group_check=True)
                    last.then_inc(s_s, 1)

            def to_pT(i):
                for j, n in units(i):
                    pe.wait_ge(s_pr, n + 1)
                    for c in range(CT):
                        last = nc.tensor.transpose(pt_ps[j][:, P * c:P * c + P], pr[j][:, 4 * c:4 * c + 4, :], C["ident"])
                    last.then_inc(s_pt, 1)

            def weighted(i, first):
                for j, n in units(i):
                    pe.wait_ge(s_pxa, n + 1)
                    pe.wait_ge(s_pxd, n + 1)
                    if not first:
                        pe.wait_ge(s_dest, n + 1 - PAIR)
                    for c in range(CT):
                        for hd in range(4):
                            rows = slice(32 * hd, 32 * hd + 32)
                            probs = ptx[j][:, c, :, :].rearrange("p k (l h q) -> p (k l) h q", l=2, h=4)[:, :, hd, :]
                            last = nc.tensor.matmul(pv_ps[j][rows, P * c:P * c + P], v[j][:, c, rows], probs,
                                                    start=True, stop=True)
                    last.then_inc(s_pv, 1)

            def mha(i):
                for j, n in units(i):
                    pe.wait_ge(s_oT, n + 1)
                    for c in range(CT):
                        last = nc.tensor.matmul(mha_ps[j][:, P * c:P * c + P], oT[j][:, c, :], wo[:, :], start=True,
                                                stop=True)
                    last.then_inc(s_mha, 1)

            def logits(i):
                for j, n in units(i):
                    pe.wait_ge(s_y, n + 1)
                    for c in range(CT):
                        last = nc.tensor.transpose(yT_ps[j][:, P * c:P * c + P], y[j][:, c, :], C["ident"])
                    last.then_inc(s_yTp, 1)
                for j, n in units(i):
                    pe.wait_ge(s_yT, n + 1)
                    for c in range(CT):
                        last = nc.tensor.matmul(lg_ps[j][:, 8 * c:8 * c + 8], yT[j][:, P * c:P * c + P], wg[:, :],
                                                start=True, stop=True)
                    last.then_inc(s_lg, 1)

            def ranks(i):
                for j, n in units(i):
                    pe.wait_ge(s_oh, n + 1)
                    nc.tensor.matmul(rank_ps[j][:, 0:16], strict16[:, :], oh16[j][:, :, :], start=True, stop=False,
                                     skip_group_check=True)
                    nc.tensor.matmul(rank_ps[j][:, 8:16], ones16[:, :], oh16[j][:, 0, :], start=False, stop=False,
                                     skip_group_check=True)
                    nc.tensor.matmul(rank_ps[j][:, 16:24], ones16[:, :], oh16[j][:, 0, :], start=False, stop=False,
                                     skip_group_check=True)
                    nc.tensor.matmul(rank_ps[j][:, 16:24], ones16[:, :], oh16[j][:, 1, :], start=False, stop=True,
                                     skip_group_check=True).then_inc(s_rank, 1)

            def turn(i, more, first=False):
                weighted(i, first)
                if more:
                    to_hT(i + 1)
                mha(i)
                if more:
                    qkv(i + 1)
                    scores(i + 1)
                logits(i)
                if more:
                    to_pT(i + 1)
                ranks(i)

            pe.wait_ge(s_w, 16 * WEIGHTS)
            pe.wait_ge(s_c16, 1)
            to_hT(0)
            qkv(0)
            scores(0)
            to_pT(0)
            turn(0, True, True)
            with pe.Fori(1, TURNS - 1) as i:
                turn(i, True)
            turn(TURNS - 1, False)

        @block.scalar
        def _(act):
            def copy_hT(i):
                for j, n in units(i):
                    act.wait_ge(s_hTp, n + 1)
                    nc.scalar.activation(hT[j][:, :], hT_ps[j], ACT.Copy).then_inc(s_hT, 1)

            def spread_q(i):
                for j, n in units(i):
                    act.wait_ge(s_q, n + 1)
                    for hd in range(4):
                        rows = slice(32 * hd, 32 * hd + 32)
                        last = nc.scalar.activation(qx[j][rows, :, hd, :], q_ps[j][rows, :].rearrange("p (l s) -> p l s", s=16),
                                                    ACT.Identity, bias=bq[rows, :])
                    last.then_inc(s_qx, 1)
                    act.wait_ge(s_kv, n + 1)
                    nc.scalar.activation(kT[j][:, :], k_ps[j], ACT.Identity, bias=bk[:, :])
                    nc.scalar.activation(v[j][:, :, :], v_ps[j].rearrange("p (c e) -> p c e", c=CT), ACT.Copy
                                         ).then_inc(s_kvc, 1)

            def exp(i):
                for j, n in units(i):
                    act.wait_ge(s_sd, n + 1)
                    nc.scalar.activation(ex[j][:, :, :], sd[j][:, :, :], ACT.Exp, scale=SCALE).then_inc(s_ex, 1)

            def spread_pT(i):
                for j, n in units(i):
                    act.wait_ge(s_pt, n + 1)
                    for k in range(2):
                        last = nc.scalar.activation(*pT_quarter(j, k), ACT.Copy)
                    last.then_inc(s_pxa, 1)

            def copy_oT(i):
                for j, n in units(i):
                    act.wait_ge(s_pv, n + 1)
                    nc.scalar.activation(oT[j][:, :, :], pv_ps[j].rearrange("p (c e) -> p c e", c=CT), ACT.Identity,
                                         bias=bv[:, :]).then_inc(s_oT, 1)

            def copy_yT(i):
                for j, n in units(i):
                    act.wait_ge(s_yTp, n + 1)
                    nc.scalar.activation(yT[j][:, :], yT_ps[j], ACT.Copy).then_inc(s_yT, 1)

            def turn(i, more):
                copy_oT(i)
                if more:
                    copy_hT(i + 1)
                    spread_q(i + 1)
                    exp(i + 1)
                copy_yT(i)
                if more:
                    spread_pT(i + 1)

            for dst, src in ((wq, io["WqT"]), (wk, io["WkT"]), (wv, io["WvT"]), (wo, io["WoT"]), (wg, io["WgT"]),
                             (bq, io["bq_col"]), (bk, io["bk_col"]), (bv, io["bv_col"]), (zeros, io["zeros"])):
                act.dma_start(dst[:, :], src).then_inc(s_w, 16)
            for dst, src in ((bo, io["bo"]), (g1, io["g1"]), (be1, io["be1"])):
                act.dma_start(dst[:, :], row(src)).then_inc(s_w, 16)
            act.dma_start(F["scratch_rows"][EXPERTS * REGION:ROWS, :].rearrange("(b p) d -> p b d", p=P),
                          io["zeros8"]).then_inc(s_w, 16)
            act.wait_ge(s_w, 16 * WEIGHTS)
            act.wait_ge(s_zero, 1)
            copy_hT(0)
            spread_q(0)
            exp(0)
            spread_pT(0)
            with act.Fori(0, TURNS - 1) as i:
                turn(i, True)
            turn(TURNS - 1, False)

        @block.gpsimd
        def _(pool):
            chain = Chain(pool, c_pool, apart)
            for j in two:
                nc.gpsimd.memset(qx[j][:, :, :, :], 0.0)
                last = nc.gpsimd.memset(ptx[j][:, :, :, :], 0.0)
            last.then_inc(s_zero, 1)
            pool.wait_ge(s_w, 16 * WEIGHTS)
            pool.wait_ge(s_aggr, STAT_STEPS)
            nc.gpsimd.tensor_tensor(rstd[:, :], ves[:, :], C["neg_half"][:, 0:TILES], ALU.pow).then_inc(s_rstd, 1)
            wide = lambda a: a[:, :].unsqueeze(1).to_broadcast([P, CT, P])

            def add_bo(i):
                for j, n in units(i):
                    pool.wait_ge(s_h, n + 1)
                    nc.gpsimd.tensor_tensor(hb[j][:, :, :], h[j][:, :, :], wide(bo), ALU.add).then_inc(s_hb, 1)

            def turn(i, more):
                for j, n in units(i):
                    wait_apart(pool, apart, s_st, n + 1)
                    chain.link(nc.gpsimd.tensor_scalar(ve[j][:, :], mv[j][:, :, 1], EPS, None, ALU.add))
                    nc.gpsimd.tensor_tensor(rst[j][:, :], ve[j][:, :], C["neg_half"][:, 0:CT], ALU.pow).then_inc(s_rst, 1)
                if more:
                    add_bo(i + 1)
                for j, n in units(i):
                    wait_apart(pool, apart, s_dest, n + 1)
                    for c in range(CT):
                        nc.gpsimd.indirect_dma_start(
                            F["scratch_rows"], bass.IndirectOffsetOnAxis(ap=dest[j][:, c:c + 1], axis=0),
                            y[j][:, c, :], None).then_inc(s_scat, 16)

            add_bo(0)
            with pool.Fori(0, TURNS - 1) as i:
                chain.enter(i * POOL_TURN)
                turn(i, True)
                chain.leave(POOL_TURN)
            chain.enter((TURNS - 1) * POOL_TURN)
            turn(TURNS - 1, False)
            pool.wait_ge(s_scat, 32 * UNITS)
            pool.wait_ge(s_tab, 1)
            for e in range(EXPERTS):
                start = nc.gpsimd.value_load(F["tables"][0:1, 2 * BLOCKS + e:2 * BLOCKS + e + 1], min_val=0,
                                             max_val=ROWS - P)
                nc.gpsimd.dma_start(F["scratch_rows"][bass.ds(start, P), :], zeros[:, :]).then_inc(s_scat, 16)
            pool.wait_ge(s_scat, 32 * UNITS + 16 * EXPERTS)

        @block.vector
        def _(dve):
            chain = Chain(dve, c_dve)
            V = nc.vector

            def norm(i, first=False):
                for j, n in units(i):
                    if not first:
                        dve.wait_ge(s_hb, n + 1 - PAIR)
                    for c in range(CT):
                        last = V.tensor_scalar(h[j][:, c, :], x[:, n * CT + c, :], mvs[:, n * CT + c, 0:1],
                                               rstd[:, bass.ts(n * CT + c, 1)], ALU.subtract, ALU.mult)
                    last.then_inc(s_h, 1)

            def less_max(i):
                for j, n in units(i):
                    dve.wait_ge(s_s, n + 1)
                    scores = s_ps[j].rearrange("p (g k) -> p g k", k=32)
                    chain.link(V.tensor_reduce(mx[j][:, :], scores, AX.X, ALU.max))
                    V.tensor_tensor(sd[j][:, :, :], scores, mx[j][:, :].unsqueeze(2).to_broadcast([P, 8, 32]),
                                    ALU.subtract).then_inc(s_sd, 1)

            def probs(i):
                for j, n in units(i):
                    dve.wait_ge(s_ex, n + 1)
                    chain.link(V.tensor_reduce(su[j][:, :], ex[j][:, :, :], AX.X, ALU.add))
                    chain.link(V.reciprocal(rs[j][:, :], su[j][:, :]))
                    V.tensor_tensor(pr[j][:, :, :], ex[j][:, :, :], rs[j][:, :].unsqueeze(2).to_broadcast([P, 8, 32]),
                                    ALU.mult).then_inc(s_pr, 1)

            def spread_pT(i):
                for j, n in units(i):
                    dve.wait_ge(s_pt, n + 1)
                    for k in range(2, 4):
                        last = V.tensor_copy(*pT_quarter(j, k))
                    last.then_inc(s_pxd, 1)

            def residual(i):
                for j, n in units(i):
                    dve.wait_ge(s_mha, n + 1)
                    dve.wait_ge(s_hb, n + 1)
                    chain.link(V.tensor_tensor(r[j][:, :, :], mha_ps[j].rearrange("p (c e) -> p c e", c=CT),
                                               hb[j][:, :, :], ALU.add))
                    for c in range(CT):
                        last = chain.mark(V.bn_stats(st[j][:, c, :], r[j][:, c, :]))
                    chain.need(last, apart)
                    for c in range(CT):
                        last = V.bn_aggr(mv[j][:, c, :], st[j][:, c, :])
                    last.then_inc(s_st, 1)

            def normed(i, first):
                for j, n in units(i):
                    dve.wait_ge(s_st, n + 1)
                    for c in range(CT):
                        last = chain.mark(V.scalar_tensor_tensor(rg[j][:, c, :], r[j][:, c, :], mv[j][:, c, 0:1], g1[:, :],
                                                                 ALU.subtract, ALU.mult))
                if not first:
                    dve.wait_ge(s_scat, i * 32 * PAIR)
                for j, n in units(i):
                    dve.wait_ge(s_rst, n + 1)
                    chain.need(last - (CT if j == 0 else 0))
                    for c in range(CT):
                        mine = V.scalar_tensor_tensor(y[j][:, c, :], rg[j][:, c, :], rst[j][:, c:c + 1], be1[:, :],
                                                      ALU.mult, ALU.add)
                    mine.then_inc(s_y, 1)

            def one_hot(i):
                for j, n in units(i):
                    dve.wait_ge(s_lg, n + 1)
                    lg = lg_ps[j].rearrange("p (c e) -> p c e", c=CT)
                    spread = lambda a: a[:, :].unsqueeze(2).to_broadcast([P, CT, EXPERTS])
                    index = C["expert_less_8"].unsqueeze(1).to_broadcast([P, CT, EXPERTS])
                    chain.link(V.tensor_reduce(lmx[j][:, :], lg, AX.X, ALU.max))
                    chain.link(V.tensor_tensor(eq[j][:, :, :], lg, spread(lmx[j]), ALU.is_ge))
                    chain.link(V.tensor_tensor(ei[j][:, :, :], eq[j][:, :, :], index, ALU.mult))
                    chain.link(V.tensor_reduce(em[j][:, :], ei[j][:, :, :], AX.X, ALU.min))
                    V.tensor_tensor(oh[j][:, :, :], index, spread(em[j]), ALU.is_equal)
                    V.tensor_tensor(oh16[j][:, :, :], index, spread(em[j]), ALU.is_equal).then_inc(s_oh, 1)

            def destinations(i):
                for j, n in units(i):
                    dve.wait_ge(s_rank, n + 1)
                    chain.link(V.tensor_tensor(rk[j][:, :, :], rank_ps[j][:, 0:16].rearrange("p (c e) -> p c e", c=CT),
                                               base[j][:, :].unsqueeze(1).to_broadcast([P, CT, EXPERTS]), ALU.add))
                    chain.mark(V.tensor_tensor(rsel[j][:, :, :], rk[j][:, :, :], oh[j][:, :, :], ALU.mult))
                    chain.link(V.tensor_tensor(base[1 - j][:, :], rank_ps[j][:, 16:24], base[j][:, :], ALU.add))
                    with nc.allow_low_precision(reason="whole numbers below 2**24"):
                        chain.link(V.tensor_reduce(dest[j][:, :], rsel[j][:, :, :], AX.X, ALU.add))
                    V.tensor_copy(F["dest"][:, bass.ts(n, CT)], dest[j][:, :]).then_inc(s_dest, 1)

            def front(i):
                norm(i, True)
                less_max(i)
                probs(i)
                spread_pT(i)

            def turn(i, more, first=False):
                if more:
                    norm(i + 1)
                residual(i)
                normed(i, first)
                if more:
                    less_max(i + 1)
                one_hot(i)
                if more:
                    probs(i + 1)
                    spread_pT(i + 1)
                destinations(i)

            dve.wait_ge(C["loaded"], C["loads"])
            dve.wait_ge(s_zero, 1)
            V.tensor_copy(strict16[:, :], C["strict"])
            V.tensor_copy(base[0][:, :], C["region_start"])
            V.tensor_copy(mask[:, :, :], C["pairmask"].unsqueeze(1).to_broadcast([P, 8, 32]))
            V.tensor_copy(ones16[:, :], C["ones"][:, 0:P]).then_inc(s_c16, 1)
            for k in range(4):
                dve.wait_ge(F["s_x"][k], 16 * 8 * F["use"])
                with dve.Fori(8 * k, 8 * k + 8) as c:
                    V.bn_stats(sts[:, c, :], x[:, c, :]).then_inc(s_bn, 1)
            dve.wait_ge(s_bn, TILES)
            stats_to_mean_var(nc, dve, s_aggr, sts[:, :, :], mvs[:, :, :], var_eps=ves[:, :])
            dve.wait_ge(s_rstd, 1)
            dve.wait_ge(s_w, 16 * WEIGHTS)
            front(0)
            chain.leave(DVE_FRONT)
            chain.enter(DVE_FRONT)
            turn(0, True, True)
            chain.leave(DVE_TURN)
            with dve.Fori(1, TURNS - 1) as i:
                chain.enter(i * DVE_TURN + DVE_FRONT)
                turn(i, True)
                chain.leave(DVE_TURN)
            chain.enter((TURNS - 1) * DVE_TURN + DVE_FRONT)
            turn(TURNS - 1, False)
            routing_tables(nc, dve, C, F, base[0], sb, sem, s_tab)


def routing_tables(nc, dve, C, F, base, sb, sem, s_tab):
    s = sem("table_steps")
    count = [0]

    def link(ins):
        count[0] += 1
        ins.then_inc(s, 1)
        dve.wait_ge(s, count[0])

    n_f, n_i, nb_i, nb, cum = (sb("t_n", [P, EXPERTS]), sb("t_ni", [P, EXPERTS], I32), sb("t_nbi", [P, EXPERTS], I32),
                               sb("t_nb", [P, EXPERTS]), sb("t_cum", [P, EXPERTS]))
    skip, past, pskip = sb("t_skip", [P, EXPERTS]), sb("t_past", [P, BLOCKS, EXPERTS]), sb("t_ps", [P, BLOCKS, EXPERTS])
    expert, rows = sb("t_e", [P, BLOCKS]), sb("t_r", [P, BLOCKS])
    link(nc.vector.tensor_tensor(n_f[:, :], base[:, :], C["region_start"], ALU.subtract))
    link(nc.vector.tensor_scalar(n_i[:, :], n_f[:, :], float(P - 1), None, ALU.add))
    link(nc.vector.tensor_scalar(nb_i[:, :], n_i[:, :], 7, None, ALU.logical_shift_right))
    link(nc.vector.tensor_copy(nb[:, :], nb_i[:, :]))
    link(nc.vector.tensor_tensor_scan(cum[:, :], C["ones"][:, 0:EXPERTS], nb[:, :], 0.0, ALU.mult, ALU.add))
    link(nc.vector.tensor_scalar(skip[:, :], nb[:, :], -float(P), float(REGION), ALU.mult, ALU.add))
    shape = [P, BLOCKS, EXPERTS]
    block = C["block"].unsqueeze(2).to_broadcast(shape)
    link(nc.vector.tensor_tensor(past[:, :, :], block, cum[:, :].unsqueeze(1).to_broadcast(shape), ALU.is_ge))
    link(nc.vector.tensor_tensor(pskip[:, :, :], past[:, :, :], skip[:, :].unsqueeze(1).to_broadcast(shape), ALU.mult))
    link(nc.vector.tensor_reduce(expert[:, :], past[:, :, :], AX.X, ALU.add))
    link(nc.vector.tensor_reduce(rows[:, :], pskip[:, :, :], AX.X, ALU.add))
    link(nc.vector.tensor_scalar(F["tables"][0:1, 0:BLOCKS], expert[0:1, :], float(EXPERTS - 1), None, ALU.min))
    link(nc.vector.scalar_tensor_tensor(F["tables"][0:1, BLOCKS:2 * BLOCKS], C["block"][0:1, :], float(P), rows[0:1, :],
                                        ALU.mult, ALU.add))
    link(nc.vector.tensor_copy(F["tables"][0:1, 2 * BLOCKS:2 * BLOCKS + EXPERTS], base[0:1, :]))
    tiles = SEQ * L // P
    behind, unused, less = sb("t_bh", [P, tiles, EXPERTS]), sb("t_un", [P, tiles, EXPERTS]), sb("t_ls", [P, tiles])
    shape = [P, tiles, EXPERTS]
    link(nc.vector.tensor_tensor(behind[:, :, :], F["dest"][:, :].unsqueeze(2).to_broadcast(shape),
                                 C["region_end"].unsqueeze(1).to_broadcast(shape), ALU.is_ge))
    link(nc.vector.tensor_tensor(unused[:, :, :], behind[:, :, :], skip[:, :].unsqueeze(1).to_broadcast(shape), ALU.mult))
    link(nc.vector.tensor_reduce(less[:, :], unused[:, :, :], AX.X, ALU.add))
    link(nc.vector.tensor_tensor(F["place"][:, :], F["dest"][:, :], less[:, :], ALU.subtract))
    dve.sem_inc(s_tab, 1)


def ffn_experts(nc, io, C, F, tag):
    LANES = 4
    TURNS = BLOCKS // LANES
    assert TURNS * LANES == BLOCKS
    FC = DF // P
    WCOLS = DF + FC + P
    with ExitStack() as ctx:
        sb = lambda name, shape, dt=F32: ctx.enter_context(nc.sbuf_tensor(tag + name, shape, dt))
        sem = PhaseSemaphores(nc, ctx, tag)
        lanes = range(LANES)
        each = lambda name, shape, dt=F32: [sb(f"{name}{j}", shape, dt) for j in lanes]
        w2 = F["w2"]
        g2, be2 = sb("g2", [P, P]), sb("be2", [P, P])
        y, yT, wst = each("y", [P, D]), each("yT", [P, P]), each("wst", [P, WCOLS])
        hh, r, st, mv, ve, rst = (each("hh", [P, FC, P]), each("r", [P, D]), each("st", [P, 6]), each("mv", [P, 2]),
                                  each("ve", [P, 1]), each("rst", [P, 1]))
        yb, rg = each("yb", [P, D]), each("rg", [P, D])
        z = sb("z", [P, LANES, D])
        ps = ctx.enter_context(nc.psum_tensor(tag + "ps", [P, 8, 512], F32))
        hh_ps = [ps[:, 2 * j, :] for j in lanes]
        yT_ps = [ps[:, 2 * j + 1, 0:P] for j in lanes]
        out_ps = [ps[:, 2 * j + 1, 256:256 + D] for j in lanes]
        (s_w, s_yTp, s_yT, s_h, s_hr, s_yb, s_out, s_st, s_rst, s_z) = (sem(k) for k in (
            "affine_loaded", "yT_psum", "yT_copied", "hidden_product", "hidden_ready", "y_plus_bias", "out_product",
            "r_stats", "r_rstd", "z_ready"))
        s_store = sem("z_stored")
        s_wst = [sem(f"weights_staged{j}") for j in lanes]
        s_load = [sem(f"y_loaded{j}") for j in lanes]
        c_dve, c_pool, apart = sem("dve_steps"), sem("pool_steps"), sem("apart")
        DVE_TURN, POOL_TURN = 3 * LANES, LANES
        units = lambda i: [(j, i * LANES + j) for j in lanes]
        expert = lambda eng, b: eng.value_load(F["tables"][0:1, bass.ds(b, 1)], min_val=0, max_val=EXPERTS - 1)
        first_row = lambda eng, b: eng.value_load(F["tables"][0:1, bass.ds(b + BLOCKS, 1)], min_val=0, max_val=ROWS - P)
        by_sync, by_pool = range(0, LANES // 2), range(LANES // 2, LANES)

        def load(eng, j, b):
            eng.dma_start(y[j][:, :], F["scratch_rows"][bass.ds(first_row(eng, b), P), :]).then_inc(s_load[j], 16)

        def load_ahead(eng, own, i, apart=None):
            for j, b in units(i):
                if j in own:
                    wait_apart(eng, apart, s_yTp, b + 1)
                    wait_apart(eng, apart, s_yb, b + 1)
                    load(eng, j, b + LANES)

        block = ctx.enter_context(nc.Block())

        @block.sync
        def _(sp):
            def turn(i, more):
                for j, b in units(i):
                    if more:
                        sp.wait_ge(s_hr, b + 1)
                        sp.wait_ge(s_yb, b + 1)
                        stage(j, b + LANES)
                if more == 2:
                    load_ahead(sp, by_sync, i + 1)
                sp.wait_ge(s_z, (i + 1) * LANES)
                sp.dma_start(F["result_rows"][bass.ts(i, LANES * P), :].rearrange("(j p) d -> p j d", p=P), z[:, :, :]
                             ).then_inc(s_store, 16)

            def stage(j, b):
                sp.dma_start(wst[j][:, :], io["w1b"][bass.ds(expert(sp, b), 1)].rearrange("e p w -> p (e w)")
                             ).then_inc(s_wst[j], 16)

            sp.dma_start(g2[:, :], io["g2"].unsqueeze(0).to_broadcast([P, P])).then_inc(s_w, 16)
            sp.dma_start(be2[:, :], io["be2"].unsqueeze(0).to_broadcast([P, P])).then_inc(s_w, 16)
            for j in by_sync:
                load(sp, j, j)
            for j, b in units(0):
                stage(j, b)
            load_ahead(sp, by_sync, 0)
            with sp.Fori(0, TURNS - 2) as i:
                turn(i, 2)
            turn(TURNS - 2, 1)
            turn(TURNS - 1, 0)
            sp.wait_ge(s_store, 16 * TURNS)

        @block.gpsimd
        def _(pool):
            chain = Chain(pool, c_pool, apart)

            def add_bias(i):
                for j, b in units(i):
                    pool.wait_ge(s_load[j], 16 * i + 16)
                    wait_apart(pool, apart, s_wst[j], 16 * i + 16)
                    nc.gpsimd.tensor_tensor(yb[j][:, :], y[j][:, :], wst[j][:, DF + FC:WCOLS], ALU.add).then_inc(s_yb, 1)

            def turn(i, more):
                for j, b in units(i):
                    wait_apart(pool, apart, s_st, b + 1)
                    chain.link(nc.gpsimd.tensor_scalar(ve[j][:, :], mv[j][:, 1:2], EPS, None, ALU.add))
                    nc.gpsimd.tensor_tensor(rst[j][:, :], ve[j][:, :], C["neg_half"][:, 0:1], ALU.pow).then_inc(s_rst, 1)
                if more:
                    add_bias(i + 1)
                if more == 2:
                    load_ahead(nc.gpsimd, by_pool, i + 1, apart)

            for j in by_pool:
                load(nc.gpsimd, j, j)
            add_bias(0)
            load_ahead(nc.gpsimd, by_pool, 0, apart)
            with pool.Fori(0, TURNS - 2) as i:
                chain.enter(i * POOL_TURN)
                turn(i, 2)
                chain.leave(POOL_TURN)
            for i in (TURNS - 2, TURNS - 1):
                chain.enter(i * POOL_TURN)
                turn(i, i < TURNS - 1)

        @block.tensor
        def _(pe):
            def to_yT(j, i):
                pe.wait_ge(s_load[j], 16 * i + 16)
                nc.tensor.transpose(yT_ps[j], y[j][:, :], C["ident"]).then_inc(s_yTp, 1)

            def turn(i, more):
                experts = []
                for j, b in units(i):
                    experts.append(expert(pe, b))
                    pe.wait_ge(s_yT, b + 1)
                    pe.wait_ge(s_wst[j], 16 * i + 16)
                    for f in range(FC):
                        last = nc.tensor.matmul(hh_ps[j][:, P * f:P * f + P], wst[j][:, P * f:P * f + P], yT[j][:, :],
                                                start=True, stop=True)
                    last.then_inc(s_h, 1)
                for j, b in units(i):
                    pe.wait_ge(s_hr, b + 1)
                    for f in range(FC):
                        last = nc.tensor.matmul(out_ps[j], hh[j][:, f, :], w2[:, bass.ds(experts[j] * (FC * D) + f * D, D)],
                                                start=(f == 0), stop=(f == FC - 1))
                    last.then_inc(s_out, 1)
                if more:
                    for j, b in units(i):
                        pe.wait_ge(s_st, b + 1)
                        to_yT(j, i + 1)

            for j in lanes:
                to_yT(j, 0)
            with pe.Fori(0, TURNS - 1) as i:
                turn(i, True)
            turn(TURNS - 1, False)

        @block.scalar
        def _(act):
            def copy_yT(i):
                for j, b in units(i):
                    act.wait_ge(s_yTp, b + 1)
                    nc.scalar.activation(yT[j][:, :], yT_ps[j], ACT.Copy).then_inc(s_yT, 1)

            def turn(i, more):
                for j, b in units(i):
                    act.wait_ge(s_h, b + 1)
                    for f in range(FC):
                        last = nc.scalar.activation(hh[j][:, f, :], hh_ps[j][:, P * f:P * f + P], ACT.Relu,
                                                    bias=wst[j][:, DF + f:DF + f + 1])
                    last.then_inc(s_hr, 1)
                if more:
                    copy_yT(i + 1)

            act.preload_act_table_set(EXP_LN)
            copy_yT(0)
            with act.Fori(0, TURNS - 1) as i:
                turn(i, True)
            turn(TURNS - 1, False)

        @block.vector
        def _(dve):
            chain = Chain(dve, c_dve)

            def turn(i, first):
                for j, b in units(i):
                    dve.wait_ge(s_out, b + 1)
                    dve.wait_ge(s_yb, b + 1)
                    chain.link(nc.vector.tensor_tensor(r[j][:, :], out_ps[j], yb[j][:, :], ALU.add))
                    chain.link(nc.vector.bn_stats(st[j][:, :], r[j][:, :]), apart)
                    nc.vector.bn_aggr(mv[j][:, :], st[j][:, :]).then_inc(s_st, 1)
                if not first:
                    dve.wait_ge(s_store, 16 * i)
                for j, b in units(i):
                    dve.wait_ge(s_rst, b + 1)
                    chain.link(nc.vector.scalar_tensor_tensor(rg[j][:, :], r[j][:, :], mv[j][:, 0:1], g2[:, :],
                                                              ALU.subtract, ALU.mult))
                    nc.vector.scalar_tensor_tensor(z[:, j, :], rg[j][:, :], rst[j][:, 0:1], be2[:, :], ALU.mult,
                                                   ALU.add).then_inc(s_z, 1)

            dve.wait_ge(s_w, 32)
            turn(0, True)
            chain.leave(DVE_TURN)
            with dve.Fori(1, TURNS) as i:
                chain.enter(i * DVE_TURN)
                turn(i, False)
                chain.leave(DVE_TURN)


def ffn_gather(nc, io, C, F, out_dram, tag):
    TILES, GROUP = SEQ * L // P, 4
    TURNS = TILES // GROUP
    with ExitStack() as ctx:
        sb = lambda name, shape, dt=F32: ctx.enter_context(nc.sbuf_tensor(tag + name, shape, dt))
        sem = PhaseSemaphores(nc, ctx, tag)
        x = F["x"]
        z = [sb(f"z{k}", [P, D]) for k in range(2 * GROUP)]
        at = sb("at", [P, 2, GROUP], I32)
        s_at, s_z, s_sum, s_out = sem("places_copied"), [sem("gathered0"), sem("gathered1")], sem("summed"), sem("stored")
        apart = sem("apart")
        block = ctx.enter_context(nc.Block())

        @block.gpsimd
        def _(pool):

            with pool.Fori(0, TURNS // 2) as i:
                for k in range(2):
                    wait_apart(pool, apart, s_at, 2 * i + k + 1)
                    for g in range(GROUP):
                        nc.gpsimd.indirect_dma_start(z[GROUP * k + g][:, :], None, F["result_rows"],
                                                     bass.IndirectOffsetOnAxis(ap=at[:, k, g:g + 1], axis=0)
                                                     ).then_inc(s_z[k], 16)

        @block.vector
        def _(dve):
            def place(i, k):
                nc.vector.tensor_copy(at[:, k, :], F["place"][:, bass.ts(2 * i + k, GROUP)]).then_inc(s_at, 1)

            def add(i, k):
                dve.wait_ge(s_z[k], 16 * GROUP * (i + 1))
                for g in range(GROUP):
                    xs = x[:, (2 * i + k) * GROUP + g, :]
                    last = nc.vector.tensor_tensor(xs, xs, z[GROUP * k + g][:, :], ALU.add)
                last.then_inc(s_sum, 1)

            for k in range(2):
                place(0, k)
            with dve.Fori(0, TURNS // 2 - 1) as i:
                for k in range(2):
                    add(i, k)
                    place(i + 1, k)
            for k in range(2):
                add(TURNS // 2 - 1, k)

        @block.sync
        def _(sp):
            for k in range(TURNS // 2):
                sp.wait_ge(s_sum, 2 * k + 2)
                for lp in range(8):
                    sp.dma_start(out_dram.rearrange("s (g l) d -> l s g d", l=8)[lp, :, 8 * k:8 * k + 8, :],
                                 x[16 * lp:16 * lp + 16, 8 * k:8 * k + 8, :]).then_inc(s_out, 16)
            sp.wait_ge(s_out, 16 * 8 * (TURNS // 2))


def rwkv_phase(nc, io, C, x_dram, out_dram, tag="rk_"):
    UNITS, PAIR, CT = SEQ, 2, 2
    TURNS = UNITS // PAIR
    FC = DF // P
    LIM = 30.0
    DVE_FRONT, DVE_TURN, ACT_FRONT, ACT_TURN, POOL_TURN = 22, 32, 8, 12, 4
    with ExitStack() as ctx:
        sb = lambda name, shape, dt=F32: ctx.enter_context(nc.sbuf_tensor(tag + name, shape, dt))
        sem = PhaseSemaphores(nc, ctx, tag)
        two = range(PAIR)
        each = lambda name, shape, dt=F32: [sb(f"{name}{j}", shape, dt) for j in two]
        x = sb("x", [P, UNITS * CT, D])
        wk, wv, wr, wcr = sb("wk", [P, P]), sb("wv", [P, P]), sb("wr", [P, P]), sb("wcr", [P, P])
        wck, wcv = sb("wck", [P, DF]), sb("wcv", [P, FC, D])
        cols = sb("cols", [P, 11])
        ln1g, ln1b, ln2g, ln2b, mixk, mixv, mixr, cmixk, cmixr, decay, first = (cols[:, k:k + 1] for k in range(11))
        U = sb("U", [P, 1])
        sts, mvs = sb("sts", [P, UNITS * CT, 6]), sb("mvs", [P, UNITS * CT, 2])
        ves, rs1, t1, t2, rs2, rs12 = (sb(k, [P, UNITS * CT]) for k in ("ves", "rs1", "t1", "t2", "rs2", "rs12"))
        u, hn, hT, dh = each("u", [P, CT, D]), each("hn", [P, CT, D]), each("hT", [P, L + 1]), each("dh", [P, L])
        xk, xv, xr = each("xk", [P, L]), each("xv", [P, L]), each("xr", [P, L])
        m, mu, muc, X, Xi = each("m", [P, L + 1]), each("mu", [P, L]), each("muc", [P, L]), each("X", [P, L]), each("Xi", [P, L])
        e1, e2, Q, lnQ, lam = each("e1", [P, L]), each("e2", [P, L]), each("Q", [P, L + 1]), each("lnQ", [P, L]), each("lam", [P, L])
        G, Gi, al, bv, a = each("G", [P, L]), each("Gi", [P, L]), each("al", [P, L]), each("bv", [P, L]), each("a", [P, L + 1])
        lw, sw, rc, re, rl, sr = (each("lw", [P, L]), each("sw", [P, L]), each("rc", [P, L]), each("re", [P, L]),
                                  each("rl", [P, L]), each("sr", [P, L]))
        d1, d2, yv, ry = each("d1", [P, L]), each("d2", [P, L]), each("yv", [P, L]), each("ry", [P, L])
        xp, st, mv, ve, rst = (each("xp", [P, CT, D]), each("st", [P, CT, 6]), each("mv", [P, CT, 2]), each("ve", [P, CT]),
                               each("rst", [P, CT]))
        h2, h2T, dh2, ck, cr = each("h2", [P, CT, D]), each("h2T", [P, L + 1]), each("dh2", [P, L]), each("ck", [P, L]), each("cr", [P, L])
        rk, kk = each("rk", [P, FC, L]), each("kk", [P, FC, L])
        cc, ce, cl, sc, o, xs = (each("cc", [P, L]), each("ce", [P, L]), each("cl", [P, L]), each("sc", [P, L]),
                                 each("o", [P, CT, D]), each("xs", [P, CT, D]))
        ps = ctx.enter_context(nc.psum_tensor(tag + "ps", [P, 8, 512], F32))
        bank = lambda j, b: ps[:, 4 * j + b, :]
        hT_ps = [bank(j, 0)[:, 0:256] for j in two]
        r_ps = [bank(j, 0)[:, 256:512] for j in two]
        k_ps = [bank(j, 1)[:, 0:256] for j in two]
        v_ps = [bank(j, 1)[:, 256:512] for j in two]
        w_ps = [bank(j, 2)[:, 0:256] for j in two]
        h2T_ps = [bank(j, 3)[:, 0:256] for j in two]
        kk_ps = [ps[:, 4 * j + 2:4 * j + 4, :] for j in two]
        kv_ps = [bank(j, 2)[:, 0:256] for j in two]
        cr_ps = [bank(j, 2)[:, 256:512] for j in two]
        names = ("weights_loaded bn_stats mean_var rstd1 var2 rstd2 rstd12 first_exp normed hT_psum hT_copied mixed kvr_product "
                 "shift_ready shift_exp Q_ready Q_ln lam_ready lam_exp r_clamped r_sigmoid y_sigmoid ry_ready w_psum "
                 "xp_stats xp_rstd h2_ready h2T_psum h2T_copied cmixed kk_product relu_ready kk_ready ckv_product cr_clamped "
                 "cr_sigmoid x_plus_xp x_out stored bounds_set").split()
        (s_w, s_bn, s_mv, s_rs1, s_var2, s_rs2, s_rs12, s_U, s_h, s_hTp, s_hT, s_mix, s_kvr, s_mu, s_X, s_Q, s_lnQ, s_lam, s_G,
         s_rc, s_sr, s_sw, s_ry, s_wp, s_st, s_rst, s_h2, s_h2Tp, s_h2T, s_cmix, s_kk, s_relu, s_kk2, s_kv, s_cc, s_sc,
         s_xs, s_out, s_store, s_set) = (sem(k) for k in names)
        s_x = [sem(f"x_loaded{k}") for k in range(4)]
        c_dve, c_act, c_pool, apart = sem("dve_steps"), sem("act_steps"), sem("pool_steps"), sem("apart")
        units = lambda i: [(j, i * PAIR + j) for j in two]
        tiles = lambda t: t.rearrange("p (c e) -> p c e", c=CT)
        WEIGHTS = 7
        block = ctx.enter_context(nc.Block())

        @block.sync
        def _(sp):
            for k in range(4):
                sp.dma_start(x[:, 8 * k:8 * k + 8, :],
                             x_dram[4 * k:4 * k + 4].rearrange("s (c p) d -> p (s c) d", p=P)).then_inc(s_x[k], 16)
            with sp.Fori(0, UNITS) as n:
                sp.wait_ge(s_out, n + 1)
                sp.dma_start(out_dram[bass.ts(n, 1)].rearrange("s (c p) d -> p (s c) d", p=P),
                             x[:, bass.ts(n, CT), :]).then_inc(s_store, 16)
            sp.wait_ge(s_store, 16 * UNITS)

        @block.tensor
        def _(pe):
            def to_hT(i):
                for j, n in units(i):
                    pe.wait_ge(s_h, n + 1)
                    for c in range(CT):
                        last = nc.tensor.transpose(hT_ps[j][:, P * c:P * c + P], hn[j][:, c, :], C["ident"])
                    last.then_inc(s_hTp, 1)

            def to_kvr(i):
                for j, n in units(i):
                    pe.wait_ge(s_mix, n + 1)
                    nc.tensor.matmul(k_ps[j], wk[:, :], xk[j][:, :], start=True, stop=True)
                    nc.tensor.matmul(v_ps[j], wv[:, :], xv[j][:, :], start=True, stop=True)
                    nc.tensor.matmul(r_ps[j], wr[:, :], xr[j][:, :], start=True, stop=True).then_inc(s_kvr, 1)

            def front(i):
                to_hT(i)
                to_kvr(i)

            def turn(i, more):
                pe.wait_ge(s_out, i * PAIR)
                for j, n in units(i):
                    pe.wait_ge(s_ry, n + 1)
                    for c in range(CT):
                        last = nc.tensor.transpose(w_ps[j][:, P * c:P * c + P], ry[j][:, P * c:P * c + P], C["ident"])
                    last.then_inc(s_wp, 1)
                if more:
                    to_hT(i + 1)
                for j, n in units(i):
                    pe.wait_ge(s_h2, n + 1)
                    for c in range(CT):
                        last = nc.tensor.transpose(h2T_ps[j][:, P * c:P * c + P], h2[j][:, c, :], C["ident"])
                    last.then_inc(s_h2Tp, 1)
                if more:
                    to_kvr(i + 1)
                for j, n in units(i):
                    pe.wait_ge(s_cmix, n + 1)
                    for f in range(FC):
                        last = nc.tensor.matmul(kk_ps[j][:, f // 2, 256 * (f % 2):256 * (f % 2) + 256],
                                                wck[:, P * f:P * f + P], ck[j][:, :], start=True, stop=True)
                    last.then_inc(s_kk, 1)
                for j, n in units(i):
                    pe.wait_ge(s_relu, n + 1)
                    pe.wait_ge(s_kk2, n + 1)
                    for c in range(CT):
                        nc.tensor.matmul(cr_ps[j][:, P * c:P * c + P], cr[j][:, P * c:P * c + P], wcr[:, :], start=True,
                                         stop=True)
                    for c in range(CT):
                        for f in range(FC):
                            last = nc.tensor.matmul(kv_ps[j][:, P * c:P * c + P], kk[j][:, f, P * c:P * c + P], wcv[:, f, :],
                                                    start=(f == 0), stop=(f == FC - 1))
                    last.then_inc(s_kv, 1)

            pe.wait_ge(C["loaded"], C["loads"])
            pe.wait_ge(s_w, 16 * WEIGHTS)
            pipelined(pe, Chain(pe, None), TURNS, 0, 0, front, turn)

        @block.scalar
        def _(act):
            chain = Chain(act, c_act)

            def sigmoid(out, l, e, src):
                chain.link(nc.scalar.activation(e, src, ACT.Exp, scale=-1.0))
                chain.link(nc.scalar.activation(l, e, ACT.Ln, bias=1.0))
                return nc.scalar.activation(out, l, ACT.Exp, scale=-1.0)

            def copy_hT(i):
                for j, n in units(i):
                    act.wait_ge(s_hTp, n + 1)
                    nc.scalar.activation(hT[j][:, 1:L + 1], hT_ps[j], ACT.Identity, bias=ln1b, scale=ln1g).then_inc(s_hT, 1)

            def exps(i):
                for j, n in units(i):
                    act.wait_ge(s_mu, n + 1)
                    nc.scalar.activation(X[j][:, :], muc[j][:, :], ACT.Exp)
                    nc.scalar.activation(Xi[j][:, :], muc[j][:, :], ACT.Exp, scale=-1.0).then_inc(s_X, 1)
                for j, n in units(i):
                    act.wait_ge(s_rc, n + 1)
                    sigmoid(sr[j][:, :], rl[j][:, :], re[j][:, :], rc[j][:, :]).then_inc(s_sr, 1)
                for j, n in units(i):
                    act.wait_ge(s_Q, n + 1)
                    nc.scalar.activation(lnQ[j][:, :], Q[j][:, 0:L], ACT.Ln).then_inc(s_lnQ, 1)
                for j, n in units(i):
                    act.wait_ge(s_lam, n + 1)
                    chain.link(nc.scalar.activation(Gi[j][:, :], lam[j][:, :], ACT.Exp, scale=-1.0))
                    nc.scalar.activation(G[j][:, :], lam[j][:, :], ACT.Exp).then_inc(s_G, 1)
                    chain.link(nc.scalar.activation(lw[j][:, :], Gi[j][:, :], ACT.Ln, bias=1.0, scale=U[:, :]))
                    nc.scalar.activation(sw[j][:, :], lw[j][:, :], ACT.Exp, scale=-1.0).then_inc(s_sw, 1)

            def front(i):
                copy_hT(i)
                exps(i)

            def turn(i, more):
                if more:
                    copy_hT(i + 1)
                for j, n in units(i):
                    act.wait_ge(s_h2Tp, n + 1)
                    nc.scalar.activation(h2T[j][:, 1:L + 1], h2T_ps[j], ACT.Identity, bias=ln2b, scale=ln2g).then_inc(s_h2T, 1)
                for j, n in units(i):
                    act.wait_ge(s_kk, n + 1)
                    nc.scalar.activation(rk[j][:, :, :].rearrange("p f t -> p (f t)"), kk_ps[j].rearrange("p b t -> p (b t)"),
                                         ACT.Relu).then_inc(s_relu, 1)
                if more:
                    exps(i + 1)
                for j, n in units(i):
                    act.wait_ge(s_cc, n + 1)
                    sigmoid(sc[j][:, :], cl[j][:, :], ce[j][:, :], cc[j][:, :]).then_inc(s_sc, 1)

            for dst, src in ((wk[:, :], io["w_tk"]), (wv[:, :], io["w_tv"]), (wr[:, :], io["w_tr"]), (wcr[:, :], io["w_cr"]),
                             (wck[:, :], io["w_ck"]), (wcv[:, :, :], io["w_cv"].rearrange("(f p) d -> p f d", p=P)),
                             (cols[:, :], io["rwkv_cols"])):
                act.dma_start(dst, src).then_inc(s_w, 16)
            act.preload_act_table_set(EXP_LN)
            act.wait_ge(s_w, 16 * WEIGHTS)
            nc.scalar.activation(U[:, :], first, ACT.Exp).then_inc(s_U, 1)
            act.wait_ge(s_U, 1)
            pipelined(act, chain, TURNS, ACT_FRONT, ACT_TURN, front, turn)

        @block.gpsimd
        def _(pool):
            chain = Chain(pool, c_pool, apart)
            for j in two:
                nc.gpsimd.memset(hT[j][:, 0:1], 0.0)
                nc.gpsimd.memset(h2T[j][:, 0:1], 0.0)
                nc.gpsimd.memset(m[j][:, 0:1], -1e38)
                nc.gpsimd.memset(Q[j][:, 0:1], 1.0)
                last = nc.gpsimd.memset(a[j][:, 0:1], 0.0)
            last.then_inc(s_set, 1)
            pool.wait_ge(C["loaded"], C["loads"])
            pool.wait_ge(s_mv, STAT_STEPS)
            nc.gpsimd.tensor_tensor(rs1[:, :], ves[:, :], C["neg_half"][:, 0:UNITS * CT], ALU.pow).then_inc(s_rs1, 1)
            pool.wait_ge(s_var2, 3)
            nc.gpsimd.tensor_tensor(rs2[:, :], t1[:, :], C["neg_half"][:, 0:UNITS * CT], ALU.pow).then_inc(s_rs2, 1)
            with pool.Fori(0, TURNS) as i:
                chain.enter(i * POOL_TURN)
                for j, n in units(i):
                    wait_apart(pool, apart, s_st, n + 1)
                    chain.link(nc.gpsimd.tensor_scalar(ve[j][:, :], mv[j][:, :, 1], EPS, None, ALU.add))
                    nc.gpsimd.tensor_tensor(rst[j][:, :], ve[j][:, :], C["neg_half"][:, 0:CT], ALU.pow).then_inc(s_rst, 1)
                for j, n in units(i):
                    pool.wait_ge(s_relu, n + 1)
                    chain.mark(nc.gpsimd.tensor_tensor(kk[j][:, :, :], rk[j][:, :, :], rk[j][:, :, :], ALU.mult))
                    pool.wait_ge(c_pool, i * POOL_TURN + 3 + j)
                    pool.sem_inc(s_kk2, 1)
                for j, n in units(i):
                    nc.gpsimd.tensor_tensor(xs[j][:, :, :], xp[j][:, :, :], x[:, bass.ts(n, CT), :], ALU.add).then_inc(s_xs, 1)
                chain.leave(POOL_TURN)

        @block.vector
        def _(dve):
            chain = Chain(dve, c_dve)
            V = nc.vector

            def norm(i):
                for j, n in units(i):
                    for c in range(CT):
                        at = bass.ts(n * CT + c, 1)
                        V.tensor_scalar(u[j][:, c, :], x[:, n * CT + c, :], mvs[:, n * CT + c, 0:1], rs1[:, at], ALU.subtract,
                                        ALU.mult)
                        last = V.tensor_scalar(hn[j][:, c, :], x[:, n * CT + c, :], mvs[:, n * CT + c, 0:1], rs12[:, at],
                                               ALU.subtract, ALU.mult)
                    last.then_inc(s_h, 1)

            def mixed(i):
                for j, n in units(i):
                    dve.wait_ge(s_hT, n + 1)
                    now, before = hT[j][:, 1:L + 1], hT[j][:, 0:L]
                    chain.link(V.tensor_tensor(dh[j][:, :], now, before, ALU.subtract))
                    V.scalar_tensor_tensor(xk[j][:, :], dh[j][:, :], mixk, before, ALU.mult, ALU.add)
                    V.scalar_tensor_tensor(xv[j][:, :], dh[j][:, :], mixv, before, ALU.mult, ALU.add)
                    V.scalar_tensor_tensor(xr[j][:, :], dh[j][:, :], mixr, before, ALU.mult, ALU.add).then_inc(s_mix, 1)

            def maxima(i):
                for j, n in units(i):
                    dve.wait_ge(s_kvr, n + 1)
                    chain.link(V.tensor_tensor_scan(m[j][:, 1:L + 1], k_ps[j], decay.to_broadcast([P, L]), -1e38, ALU.max,
                                                    ALU.add))
                    chain.link(V.tensor_tensor(mu[j][:, :], m[j][:, 0:L], k_ps[j], ALU.subtract))
                    V.tensor_scalar(muc[j][:, :], mu[j][:, :], LIM, -LIM, ALU.min, ALU.max).then_inc(s_mu, 1)
                    V.tensor_scalar(rc[j][:, :], r_ps[j], -SIG_CLAMP, None, ALU.max).then_inc(s_rc, 1)

            def denominators(i):
                for j, n in units(i):
                    dve.wait_ge(s_X, n + 1)
                    chain.mark(V.tensor_scalar(e1[j][:, :], X[j][:, :], 1.0, None, ALU.min))
                    chain.link(V.tensor_scalar(e2[j][:, :], Xi[j][:, :], 1.0, None, ALU.min))
                    V.tensor_tensor_scan(Q[j][:, 1:L + 1], e1[j][:, :], e2[j][:, :], 1.0, ALU.mult, ALU.add).then_inc(s_Q, 1)

            def ratios(i):
                for j, n in units(i):
                    dve.wait_ge(s_lnQ, n + 1)
                    V.tensor_tensor(lam[j][:, :], muc[j][:, :], lnQ[j][:, :], ALU.add).then_inc(s_lam, 1)

            def outputs(i):
                for j, n in units(i):
                    dve.wait_ge(s_G, n + 1)
                    chain.mark(V.tensor_scalar(al[j][:, :], G[j][:, :], 1.0, None, ALU.min))
                    chain.link(V.scalar_tensor_tensor(bv[j][:, :], Gi[j][:, :], 1.0, v_ps[j], ALU.min, ALU.mult))
                    chain.link(V.tensor_tensor_scan(a[j][:, 1:L + 1], al[j][:, :], bv[j][:, :], 0.0, ALU.mult, ALU.add))
                for j, n in units(i):
                    chain.link(V.tensor_tensor(d1[j][:, :], a[j][:, 0:L], v_ps[j], ALU.subtract))
                    dve.wait_ge(s_sw, n + 1)
                    chain.link(V.tensor_tensor(d2[j][:, :], d1[j][:, :], sw[j][:, :], ALU.mult))
                    chain.link(V.tensor_tensor(yv[j][:, :], d2[j][:, :], v_ps[j], ALU.add))
                    dve.wait_ge(s_sr, n + 1)
                    V.tensor_tensor(ry[j][:, :], yv[j][:, :], sr[j][:, :], ALU.mult).then_inc(s_ry, 1)

            def front(i):
                norm(i)
                mixed(i)
                maxima(i)
                denominators(i)
                ratios(i)
                outputs(i)

            def turn(i, more):
                for j, n in units(i):
                    dve.wait_ge(s_wp, n + 1)
                    chain.link(V.tensor_tensor(xp[j][:, :, :], tiles(w_ps[j]), u[j][:, :, :], ALU.add))
                    for c in range(CT):
                        last = chain.mark(V.bn_stats(st[j][:, c, :], xp[j][:, c, :]))
                    chain.need(last, apart)
                    for c in range(CT):
                        last = V.bn_aggr(mv[j][:, c, :], st[j][:, c, :])
                    last.then_inc(s_st, 1)
                if more:
                    norm(i + 1)
                for j, n in units(i):
                    dve.wait_ge(s_rst, n + 1)
                    for c in range(CT):
                        last = V.tensor_scalar(h2[j][:, c, :], xp[j][:, c, :], mv[j][:, c, 0:1], rst[j][:, c:c + 1],
                                               ALU.subtract, ALU.mult)
                    last.then_inc(s_h2, 1)
                if more:
                    mixed(i + 1)
                for j, n in units(i):
                    dve.wait_ge(s_h2T, n + 1)
                    now, before = h2T[j][:, 1:L + 1], h2T[j][:, 0:L]
                    chain.link(V.tensor_tensor(dh2[j][:, :], now, before, ALU.subtract))
                    V.scalar_tensor_tensor(ck[j][:, :], dh2[j][:, :], cmixk, before, ALU.mult, ALU.add)
                    V.scalar_tensor_tensor(cr[j][:, :], dh2[j][:, :], cmixr, before, ALU.mult, ALU.add).then_inc(s_cmix, 1)
                if more:
                    maxima(i + 1)
                    denominators(i + 1)
                    ratios(i + 1)
                    outputs(i + 1)
                for j, n in units(i):
                    dve.wait_ge(s_kv, n + 1)
                    V.tensor_scalar(cc[j][:, :], cr_ps[j], -SIG_CLAMP, None, ALU.max).then_inc(s_cc, 1)
                for j, n in units(i):
                    dve.wait_ge(s_sc, n + 1)
                    chain.link(V.tensor_tensor(o[j][:, :, :], tiles(kv_ps[j]), tiles(sc[j][:, :]), ALU.mult))
                    dve.wait_ge(s_xs, n + 1)
                    V.tensor_tensor(x[:, bass.ts(n, CT), :], o[j][:, :, :], xs[j][:, :, :], ALU.add).then_inc(s_out, 1)

            dve.wait_ge(C["loaded"], C["loads"])
            dve.wait_ge(s_w, 16 * WEIGHTS)
            dve.wait_ge(s_set, 1)
            for k in range(4):
                dve.wait_ge(s_x[k], 16)
                with dve.Fori(8 * k, 8 * k + 8) as c:
                    V.bn_stats(sts[:, c, :], x[:, c, :]).then_inc(s_bn, 1)
            dve.wait_ge(s_bn, UNITS * CT)
            stats_to_mean_var(nc, dve, s_mv, sts[:, :, :], mvs[:, :, :], var_eps=ves[:, :])
            dve.wait_ge(s_rs1, 1)
            for step, (dst, p, q) in enumerate(((t1, mvs[:, :, 1], rs1[:, :]), (t2, t1[:, :], rs1[:, :]))):
                V.tensor_tensor(dst[:, :], p, q, ALU.mult).then_inc(s_var2, 1)
                dve.wait_ge(s_var2, step + 1)
            V.tensor_scalar(t1[:, :], t2[:, :], EPS, None, ALU.add).then_inc(s_var2, 1)
            dve.wait_ge(s_rs2, 1)
            V.tensor_tensor(rs12[:, :], rs1[:, :], rs2[:, :], ALU.mult).then_inc(s_rs12, 1)
            dve.wait_ge(s_rs12, 1)
            pipelined(dve, chain, TURNS, DVE_FRONT, DVE_TURN, front, turn)


def ffn_state(nc, ctx):
    t = lambda name, shape, dt=F32: ctx.enter_context(nc.sbuf_tensor("ffn_" + name, shape, dt))
    dram = lambda name, rows: nc.dram_tensor(name, [rows, D], F32, kind="Internal").ap()
    tiles = SEQ * L // P
    return dict(x=t("x", [P, tiles, D]), dest=t("dest", [P, tiles], I32), place=t("place", [P, tiles], I32),
                tables=t("tables", [1, 2 * BLOCKS + EXPERTS], I32),
                w2=t("w2", [P, EXPERTS * DF // P * D]),
                s_x=[ctx.enter_context(nc.semaphore(f"ffn_x_loaded{k}")) for k in range(4)],
                scratch_rows=dram("scratch_rows", ROWS), result_rows=dram("result_rows", BLOCKS * P))


def hybrid_layers(nc, io, out):
    with ExitStack() as ctx:
        C = load_consts(nc, ctx, io)
        F = ffn_state(nc, ctx)
        x1, x2, x3 = (nc.dram_tensor(name, [SEQ, L, D], F32, kind="Internal").ap() for name in ("x1", "x2", "x3"))
        loaded = ctx.enter_context(nc.semaphore("expert_weights_loaded"))
        with nc.Block() as block:
            @block.sync
            def _(sp):
                sp.dma_start(C["tensor"][:, :], io["consts"]).then_inc(C["loaded"], C["loads"])
                sp.dma_start(F["w2"][:, :], io["w2"]).then_inc(loaded, 16)
        gla_phase(nc, io, C, io["x"], x1)
        with nc.Block() as block:
            @block.sync
            def _(sp):
                sp.wait_ge(loaded, 16)
        for use, (source, result) in enumerate(((x1, x2), (x3, out))):
            F["use"] = use + 1
            ffn_attention(nc, io, C, F, source, f"att{use}_")
            ffn_experts(nc, io, C, F, f"experts{use}_")
            ffn_gather(nc, io, C, F, result, f"gather{use}_")
            if use == 0:
                rwkv_phase(nc, io, C, x2, x3)


def laid_out(inputs):
    a = {k[len("L0_attn_a_"):]: v for k, v in inputs.items() if k.startswith("L0_attn_a_")}
    b = {k[len("L0_attn_b_"):]: v for k, v in inputs.items() if k.startswith("L0_attn_b_")}
    f = {k[len("L0_ffn_"):]: v for k, v in inputs.items() if k.startswith("L0_ffn_")}
    fc = DF // P
    w1b = np.concatenate([f["W1"].transpose(1, 0, 2), f["b1"].reshape(EXPERTS, fc, P).transpose(2, 0, 1),
                          np.broadcast_to(f["b2"][None], (P, EXPERTS, D))], 2).transpose(1, 0, 2)
    rows = ("ln1_g", "ln1_b", "ln2_g", "ln2_b", "mix_k", "mix_v", "mix_r", "cmix_k", "cmix_r", "time_decay",
            "time_first")
    io = {
        "x": a["x"], "consts": const_array(),
        "Wq": a["Wq"], "Wk": a["Wk"], "Wv": a["Wv"], "Wg": a["Wg"], "gk_w1T": a["gk_w1"].T, "gk_w2": a["gk_w2"],
        "Wo_a": a["Wo"], "g_norm_col": np.tile(a["g_norm_w"], 2)[:, None], "gk_b2_col": a["gk_b2"][:, None],
        "WqT": f["Wqkv"][0:P].T, "WkT": f["Wqkv"][P:2 * P].T, "WvT": f["Wqkv"][2 * P:3 * P].T, "WoT": f["Wo"].T,
        "WgT": f["Wg"].T, "bq_col": f["bqkv"][0:P, None], "bk_col": f["bqkv"][P:2 * P, None],
        "bv_col": f["bqkv"][2 * P:3 * P, None], "bo": f["bo"], "g1": f["g1"], "be1": f["be1"], "g2": f["g2"], "be2": f["be2"],
        "w1b": w1b, "w2": f["W2"].reshape(EXPERTS, fc, P, D).transpose(2, 0, 1, 3).reshape(P, -1),
        "zeros": np.zeros((P, P), np.float32), "zeros8": np.zeros((P, EXPERTS, P), np.float32),
        "w_tk": b["w_tk"], "w_tv": b["w_tv"], "w_tr": b["w_tr"], "w_cr": b["w_cr"], "w_ck": b["w_ck"],
        "w_cv": b["w_cv"], "rwkv_cols": np.stack([b[k].reshape(-1) for k in rows], 1),
    }
    return {k: np.ascontiguousarray(v) for k, v in io.items()}


def kernel(**inputs):
    import concourse.bacc as bacc
    from concourse.bass_utils import run_bass_kernel_spmd

    nc = bacc.Bacc("TRN2", target_bir_lowering=False, num_devices=1)
    arrays, io = {}, {}
    for name, array in laid_out({k: np.asarray(v) for k, v in inputs.items()}).items():
        arrays[f"in_{name}_dram"] = array
        io[name] = nc.dram_tensor(f"in_{name}_dram", array.shape, mybir.dt.from_np(array.dtype),
                                  kind="ExternalInput").ap()
    out = nc.dram_tensor("out_0_dram", [SEQ, L, D], F32, kind="ExternalOutput").ap()
    hybrid_layers(nc, io, out)
    result = run_bass_kernel_spmd(nc, [arrays], core_ids=[0])
    return result.results[0]["out_0_dram"]
```

```python
from contextlib import ExitStack
import numpy as np
import concourse.bass as bass
import concourse.mybir as mybir

F32, I32, BF16 = mybir.dt.float32, mybir.dt.int32, mybir.dt.bfloat16
ALU, ACT, AX = mybir.AluOpType, mybir.ActivationFunctionType, mybir.AxisListType
P, D, SEQ, L = 128, 128, 16, 256
EPS = 1e-5
EXP_LN = "natural_log_exp_and_others"
SIG_CLAMP = 40.0

class PhaseSemaphores:
    def __init__(self, nc, ctx, tag):
        self.nc, self.tag, self.sems = nc, tag, []
        ctx.callback(self.clear)

    def __call__(self, name):
        self.sems.append(self.nc.alloc_semaphore(name=self.tag + name))
        return self.sems[-1]

    def clear(self):
        self.nc.clear_and_free_semaphores(self.sems)
        self.nc.all_engine_barrier()


def wait_apart(eng, apart, sem, value):
    eng.wait_ge(sem, value)
    if apart is not None and not isinstance(value, int):
        eng.sem_inc(apart, 1)


class Chain:
    def __init__(self, eng, sem, apart=None):
        self.eng, self.sem, self.apart, self.base, self.n = eng, sem, apart, 0, 0

    def enter(self, base):
        self.base, self.n = base, 0

    def mark(self, ins):
        self.n += 1
        ins.then_inc(self.sem, 1)
        return self.n

    def need(self, n, apart=None):
        wait_apart(self.eng, apart or self.apart, self.sem, self.base + n)

    def link(self, ins, apart=None):
        self.need(self.mark(ins), apart)

    def leave(self, steps):
        assert self.n == steps, (self.n, steps)


CONST_COLS = {}
EXPERTS, DF = 8, 512
REGION = SEQ * L + P
RESULTS = SEQ * L + 2 * EXPERTS * P
BLOCKS = SEQ * L // P + EXPERTS
ROW = 2 * D + 1
ROWS = EXPERTS * REGION + EXPERTS * P


def const_array():
    p = np.arange(P)
    e = np.arange(EXPERTS)
    cols = []
    CONST_COLS.clear()

    def put(name, a):
        CONST_COLS[name] = (sum(c.shape[1] for c in cols), a.shape[1])
        cols.append(a.astype(np.float32))

    row = lambda v: np.broadcast_to(np.asarray(v)[None, :], (P, len(v)))
    put("ident", np.eye(P))
    put("causal", p[:, None] <= p[None, :])
    put("strict", p[:, None] < p[None, :])
    put("ones", np.ones((P, 256)))
    put("headmask", (p[:, None] // 32) == (np.arange(256)[None, :] // 64))
    put("pairmask", np.where((p[:, None] // 64) == (np.arange(32)[None, :] // 16), 0.0, -1e30))
    put("neg_half", np.full((P, 32), -0.5))
    put("expert_less_8", row(e - EXPERTS))
    put("region_start", row(e * REGION))
    put("block", row(np.arange(BLOCKS)))
    put("token", (p[:, None] % SEQ) * L + 8 * np.arange(SEQ * L // P)[None, :] + p[:, None] // SEQ)
    return np.concatenate(cols, 1)


def pad_rows():
    rows = np.zeros((P, 2 * EXPERTS, ROW), np.float32)
    rows[:, :, 2 * D] = SEQ * L + P * np.arange(2 * EXPERTS)[None, :] + np.arange(P)[:, None]
    return rows


def load_consts(nc, ctx, io):
    const_array()
    t = ctx.enter_context(nc.sbuf_tensor("consts", list(io["consts"].shape), F32))
    s = ctx.enter_context(nc.semaphore("consts_loaded"))
    C = {k: t[:, a:a + n] for k, (a, n) in CONST_COLS.items()}
    C["ones_row"] = C["ones"]
    C["causal4"] = C["causal"].unsqueeze(1).to_broadcast([P, 4, P])
    C["loaded"], C["loads"], C["tensor"] = s, 16, t
    return C


WEIGHTS = {"gla": {"Wqk": 2 * D, "Wvg": 4 * D, "Wo": 2 * D, "gk_w1T": D, "gk_w2": D, "g_norm_col": 1, "gk_b2_col": 1},
           "ffn": {"WqT": P, "WkT": P, "WvT": P, "WoT": P, "WgT": EXPERTS, "bq": 1, "bk": 1, "bv": 1, "bo": D,
                   "g1": D, "be1": D, "g2": D, "be2": D},
           "rwkv": {"w_tk": D, "w_tv": D, "w_tr": D, "w_cr": D, "w_ck": DF, "w_cv": DF, "rwkv_cols": 11}}


def weights_side_by_side(nc, ctx, layer):
    t = ctx.enter_context(nc.sbuf_tensor(layer + "_weights", [P, sum(WEIGHTS[layer].values())], F32))
    views, at = {}, 0
    for name, cols in WEIGHTS[layer].items():
        views[name] = t[:, at:at + cols]
        at += cols
    return t, views


def gla_phase(nc, io, C, x_dram, x1_dram, load_later_weights):
    UNITS, CH = 16, 2
    GATE, SCALE, CLAMP = 1.0 / 16.0, 32.0 ** -0.5, 16.0 * 80.0
    with ExitStack() as ctx:
        sb = lambda name, shape: ctx.enter_context(nc.sbuf_tensor("gla_" + name, shape, F32))
        sem = PhaseSemaphores(nc, ctx, "gla_")
        each = lambda name, shape: [sb(f"{name}{j}", shape) for j in range(2)]
        x = sb("x", [P, UNITS * CH, D])
        weights, W = weights_side_by_side(nc, ctx, "gla")
        wqk, wvg, w1t, w2, wn, b2 = (W[k] for k in ("Wqk", "Wvg", "gk_w1T", "gk_w2", "g_norm_col", "gk_b2_col"))
        wo = W["Wo"].rearrange("p (c d) -> p c d", d=D)
        w12, won = sb("w12", [P, P]), sb("won", [P, 2, D])
        st, mv, ve, rs = each("st", [P, CH, 6]), each("mv", [P, CH, 2]), each("ve", [P, CH]), each("rs", [P, CH])
        h, hT = each("h", [P, CH, D]), each("hT", [P, L])
        za, ze, zl, zm, zg = (each(k, [P, L]) for k in ("za", "ze", "zl", "zm", "zg"))
        cum, dl, dc, eq, ek, qt, kt = (each(k, [P, L]) for k in ("cum", "dl", "dc", "eq", "ek", "qt", "kt"))
        dm, dS = each("dm", [P, 1]), each("dS", [P, 1])
        v, gc, qx = each("v", [P, CH, 256]), each("gc", [P, CH, 256]), each("qx", [P, CH, 4, P])
        ktok, S, am = each("ktok", [P, P]), each("S", [P, 256]), each("am", [P, CH, 4, P])
        ge, gl, gs, gg = (each(k, [P, CH, 256]) for k in ("ge", "gl", "gs", "gg"))
        sq, ss, sv, rr = each("sq", [P, CH * 256]), each("ss", [P, 8]), each("sv", [P, 8]), each("rr", [P, 8])
        og, on, oT = each("og", [P, CH, 256]), each("on", [P, CH, 256]), each("oT", [P, 4, P])
        ps = ctx.enter_context(nc.psum_tensor("gla_ps", [P, 8, 512], F32))
        hT_ps = z_ps = ps[:, 0, 0:256]
        q_ps, k_ps = ps[:, 1, 0:256], ps[:, 1, 256:512]
        kt_ps, u_ps = ps[:, 1, 0:P], ps[:, 1, 256:512]
        v_ps, g_ps = ps[:, 2, :], ps[:, 3, :]
        a_ps = lambda c: ps[:, 4 + c, :]
        o_ps = ps[:, 6, :]
        oT_ps, out_ps = ps[:, 7, :], ps[:, 7, 0:256]
        two_chunks = lambda a: a.rearrange("p (c e) -> p c e", c=CH)

        s_w, s_w12, s_w12c, s_won, s_qz = (sem(k) for k in (
            "weights_loaded", "w12_product", "w12_copied", "won_ready", "qx_zeroed"))
        s_x = [sem(f"x_loaded{j}") for j in range(2)]
        s_mv, s_rs, s_h, s_hTp, s_hT, s_z, s_zl, s_dec, s_e = (sem(k) for k in (
            "x_stats", "x_rstd", "normed", "hT_psum", "hT_copied", "gate_product", "softplus", "decay_ready", "decay_exp"))
        s_qk, s_vp, s_gp, s_v, s_gc, s_qt, s_qx = (sem(k) for k in (
            "qk_product", "v_product", "g_product", "v_copied", "g_clamped", "qk_decayed", "qx_ready"))
        s_ktp, s_ktok, s_u, s_S, s_a, s_am, s_o, s_gs, s_gg = (sem(k) for k in (
            "k_transposed", "k_copied", "state_product", "state_ready", "scores", "scores_masked", "o_product",
            "g_sigmoid", "g_silu"))
        s_sq, s_ss, s_rr, s_og, s_on, s_oTp, s_oT, s_out, s_x1, s_st = (sem(k) for k in (
            "o_squared", "o_sums", "o_rstd", "o_gated", "o_normed", "oT_psum", "oT_copied", "out_product", "x1_ready",
            "x1_stored"))
        c_dve_s, c_dve_a, c_act_a, c_act_b, c_pool_s, c_pool_c, apart = (sem(k) for k in (
            "dve_steps_statistics", "dve_steps_projections", "act_steps_projections", "act_steps_attention",
            "pool_steps_statistics", "pool_steps_output", "apart"))

        def bodies(eng, body):
            for n in range(-3, 3):
                body(n, n % 2, [n + k >= 0 for k in range(-1, 4)])
            with eng.Fori(0, (UNITS - 6) // 2) as i:
                for k in range(2):
                    body(2 * i + k + 3, (k + 1) % 2, [True] * 5)
            for n in range(UNITS - 3, UNITS + 1):
                body(n, n % 2, [n + k < UNITS for k in range(-1, 4)])

        def q_of_head(j, hd):
            rows = slice(32 * hd, 32 * hd + 32)
            return qx[j][rows, :, hd, :], qt[j][rows, :].rearrange("p (c t) -> p c t", c=CH)

        block = ctx.enter_context(nc.Block())

        @block.sync
        def _(sp):
            def load(n, j):
                sp.dma_start(x[:, bass.ds(n * CH, CH), :], x_dram[bass.ds(n, 1)].rearrange("s (c p) d -> p (s c) d", p=P)
                             ).then_inc(s_x[j], 16)
            for j in range(2):
                load(j, j)
            with sp.Fori(0, UNITS // 2 - 1) as i:
                for j in range(2):
                    sp.wait_ge(s_x[j], 16 * i + 16)
                    load(2 * i + 2 + j, j)
            load_later_weights(sp)
            with sp.Fori(0, UNITS) as n:
                sp.wait_ge(s_x1, n + 1)
                sp.dma_start(x1_dram[bass.ts(n, 1)].rearrange("s (c p) d -> p (s c) d", p=P),
                             x[:, bass.ts(n, CH), :]).then_inc(s_st, 16)
            sp.wait_ge(s_st, 16 * UNITS)

        @block.tensor
        def _(pe):
            def body(n, j, has):
                d, c, b, a = n - 1, n, n + 1, n + 2
                bj, dj, has_d, has_c, has_b, has_a = 1 - j, 1 - j, *has[0:4]
                if has_b:
                    pe.wait_ge(s_qt, b + 1)
                    nc.tensor.transpose(kt_ps, kt[bj][:, 0:P], C["ident"]).then_inc(s_ktp, 1)
                if has_a:
                    pe.wait_ge(s_h, a + 1)
                    for ch in range(CH):
                        last = nc.tensor.transpose(hT_ps[:, P * ch:P * ch + P], h[j][:, ch, :], C["ident"])
                    last.then_inc(s_hTp, 1)
                if has_d:
                    pe.wait_ge(s_on, d + 1)
                    if not isinstance(n, int) or n > 1:
                        pe.wait_ge(s_x1, d)
                    for ch in range(CH):
                        for half in range(2):
                            last = nc.tensor.transpose(oT_ps[:, P * (2 * ch + half):P * (2 * ch + half) + P],
                                                       on[dj][:, ch, P * half:P * half + P], C["ident"])
                    last.then_inc(s_oTp, 1)
                if has_b:
                    pe.wait_ge(s_qx, b + 1)
                    nc.tensor.matmul(a_ps(0), kt[bj][:, 0:P], qx[bj][:, 0, :, :], start=True, stop=True).then_inc(s_a, 1)
                if has_a:
                    pe.wait_ge(s_hT, a + 1)
                    nc.tensor.matmul(z_ps, w12[:, :], hT[j][:, :], start=True, stop=True).then_inc(s_z, 1)
                if has_b:
                    nc.tensor.matmul(a_ps(1), kt[bj][:, P:256], qx[bj][:, 1, :, :], start=True, stop=True).then_inc(s_a, 1)
                    pe.wait_ge(s_ktok, b + 1)
                    pe.wait_ge(s_v, b + 1)
                    nc.tensor.matmul(u_ps, ktok[bj][:, :], v[bj][:, 0, :], start=True, stop=True).then_inc(s_u, 1)
                if has_a:
                    for ch in range(CH):
                        last = nc.tensor.matmul(v_ps[:, 256 * ch:256 * ch + 256], hT[j][:, P * ch:P * ch + P],
                                                wvg[:, 0:256], start=True, stop=True)
                    last.then_inc(s_vp, 1)
                    if has_b:
                        pe.wait_ge(s_gc, b + 1)
                    for ch in range(CH):
                        last = nc.tensor.matmul(g_ps[:, 256 * ch:256 * ch + 256], hT[j][:, P * ch:P * ch + P],
                                                wvg[:, 256:512], start=True, stop=True)
                    last.then_inc(s_gp, 1)
                    if has_b:
                        pe.wait_ge(s_S, b + 1)
                    nc.tensor.matmul(q_ps, wqk[:, 0:P], hT[j][:, :], start=True, stop=True)
                    nc.tensor.matmul(k_ps, wqk[:, P:256], hT[j][:, :], start=True, stop=True).then_inc(s_qk, 1)
                if has_d:
                    pe.wait_ge(s_oT, d + 1)
                    for ch in range(CH):
                        for half in range(2):
                            last = nc.tensor.matmul(out_ps[:, P * ch:P * ch + P], oT[dj][:, 2 * ch + half, :],
                                                    won[:, half, :], start=(half == 0), stop=(half == 1))
                    last.then_inc(s_out, 1)
                if has_b:
                    if has_c:
                        pe.wait_ge(s_og, c + 1)
                    pe.wait_ge(s_am, (b + 1) * CH)
                    for ch in range(CH):
                        for hd in range(4):
                            nc.tensor.matmul(o_ps[:, 256 * ch + 64 * hd:256 * ch + 64 * hd + 64], am[bj][:, ch, hd, :],
                                             v[bj][:, ch, 64 * hd:64 * hd + 64], start=(ch == 0 and hd == 0), stop=False,
                                             skip_group_check=True)
                    pe.wait_ge(s_S, b + 1)
                    nc.tensor.matmul(o_ps[:, 256:512], qt[bj][:, P:256], S[bj][:, :], start=False, stop=True,
                                     skip_group_check=True).then_inc(s_o, 1)

            pe.wait_ge(C["loaded"], C["loads"])
            pe.wait_ge(s_w, 16)
            nc.tensor.matmul(ps[:, 0, 0:P], w1t[0:16], w2[0:16], start=True, stop=True).then_inc(s_w12, 1)
            pe.wait_ge(s_w12c, 1)
            pe.wait_ge(s_won, 1)
            bodies(pe, body)

        @block.scalar
        def _(act):
            in_a, in_b = Chain(act, c_act_a), Chain(act, c_act_b)

            def body(n, j, has):
                d, c, b, a = n - 1, n, n + 1, n + 2
                bj, dj, has_d, has_c, has_b, has_a = 1 - j, 1 - j, *has[0:4]
                in_a.enter(a * 2)
                in_b.enter(b * 2)
                if has_c:
                    act.wait_ge(s_o, c + 1)
                    nc.scalar.activation(sq[j][:, :], o_ps, ACT.Square).then_inc(s_sq, 1)
                if has_b:
                    act.wait_ge(s_ktp, b + 1)
                    nc.scalar.activation(ktok[bj][:, :], kt_ps, ACT.Copy).then_inc(s_ktok, 1)
                if has_a:
                    act.wait_ge(s_hTp, a + 1)
                    nc.scalar.activation(hT[j][:, :], hT_ps, ACT.Copy).then_inc(s_hT, 1)
                if has_d:
                    act.wait_ge(s_oTp, d + 1)
                    nc.scalar.activation(oT[dj][:, :, :], oT_ps, ACT.Copy).then_inc(s_oT, 1)
                if has_b:
                    act.wait_ge(s_gc, b + 1)
                    in_b.link(nc.scalar.activation(ge[bj][:, :, :], gc[bj][:, :, :], ACT.Exp, scale=-1.0))
                    in_b.mark(nc.scalar.activation(gl[bj][:, :, :], ge[bj][:, :, :], ACT.Ln, bias=1.0))
                if has_a:
                    act.wait_ge(s_z, a + 1)
                    in_a.link(nc.scalar.activation(za[j][:, :], z_ps, ACT.Abs, bias=b2))
                    in_a.link(nc.scalar.activation(ze[j][:, :], za[j][:, :], ACT.Exp, scale=-1.0))
                    nc.scalar.activation(zl[j][:, :], ze[j][:, :], ACT.Ln, bias=1.0).then_inc(s_zl, 1)
                if has_b:
                    in_b.need(2)
                    nc.scalar.activation(gs[bj][:, :, :], gl[bj][:, :, :], ACT.Exp, scale=-1.0).then_inc(s_gs, 1)
                if has_a:
                    act.wait_ge(s_vp, a + 1)
                    nc.scalar.activation(v[j][:, :, :], two_chunks(v_ps), ACT.Copy).then_inc(s_v, 1)
                    act.wait_ge(s_dec, a + 1)
                    nc.scalar.activation(eq[j][:, :], dc[j][:, :], ACT.Exp, scale=GATE)
                    nc.scalar.activation(ek[j][:, :], dc[j][:, :], ACT.Exp, scale=-GATE)
                    nc.scalar.activation(dS[j][:, :], dm[j][:, :], ACT.Exp, scale=GATE).then_inc(s_e, 1)
                if has_a:
                    act.wait_ge(s_qt, a + 1)
                    for hd in range(4):
                        last = nc.scalar.activation(*q_of_head(j, hd), ACT.Copy)
                    last.then_inc(s_qx, 1)

            act.dma_start(weights[:, :], io["gla_weights"]).then_inc(s_w, 16)
            act.preload_act_table_set(EXP_LN)
            act.wait_ge(s_w, 16)
            act.wait_ge(s_qz, 2)
            bodies(act, body)

        @block.gpsimd
        def _(pool):
            in_s, in_c = Chain(pool, c_pool_s, apart), Chain(pool, c_pool_c, apart)

            def body(n, j, has):
                d, c, b, a, s = n - 1, n, n + 1, n + 2, n + 3
                dj, bj, sj, has_d, has_c, has_b, has_a, has_s = 1 - j, 1 - j, 1 - j, *has
                in_s.enter(s)
                in_c.enter(c)
                if has_s:
                    wait_apart(pool, apart, s_mv, s + 1)
                    in_s.link(nc.gpsimd.tensor_scalar(ve[sj][:, :], mv[sj][:, :, 1], EPS, None, ALU.add))
                    nc.gpsimd.tensor_tensor(rs[sj][:, :], ve[sj][:, :], C["neg_half"][:, 0:CH], ALU.pow).then_inc(s_rs, 1)
                if has_c:
                    wait_apart(pool, apart, s_ss, c + 1)
                    in_c.link(nc.gpsimd.tensor_scalar(sv[j][:, :], ss[j][:, :], 1.0 / 64, EPS, ALU.mult, ALU.add))
                    nc.gpsimd.tensor_tensor(rr[j][:, :], sv[j][:, :], C["neg_half"][:, 0:8], ALU.pow).then_inc(s_rr, 1)
                    pool.wait_ge(s_rr, c + 1)
                    wait_apart(pool, apart, s_og, c + 1)
                    nc.gpsimd.tensor_tensor(on[j][:, :, :].rearrange("p c (g e) -> p (c g) e", e=64),
                                            og[j][:, :, :].rearrange("p c (g e) -> p (c g) e", e=64),
                                            rr[j][:, :].unsqueeze(2).to_broadcast([P, 8, 64]), ALU.mult).then_inc(s_on, 1)
                if has_b:
                    pool.wait_ge(s_gs, b + 1)
                    nc.gpsimd.tensor_tensor(gg[bj][:, :, :], gc[bj][:, :, :], gs[bj][:, :, :], ALU.mult).then_inc(s_gg, 1)

            for j in range(2):
                nc.gpsimd.memset(qx[j][:, :, :, :], 0.0).then_inc(s_qz, 1)
            pool.wait_ge(s_qz, 2)
            pool.wait_ge(C["loaded"], C["loads"])
            bodies(pool, body)

        @block.vector
        def _(dve):
            in_s, in_a = Chain(dve, c_dve_s), Chain(dve, c_dve_a)
            V = nc.vector

            def body(n, j, has):
                d, c, b, a, s = n - 1, n, n + 1, n + 2, n + 3
                dj, bj, sj, has_d, has_c, has_b, has_a, has_s = 1 - j, 1 - j, 1 - j, *has
                in_s.enter(s * CH)
                in_a.enter(a * 5)
                if has_c:
                    dve.wait_ge(s_sq, c + 1)
                    V.tensor_reduce(ss[j][:, :], sq[j][:, :].rearrange("p (g e) -> p g e", e=64), AX.X, ALU.add
                                    ).then_inc(s_ss, 1)
                    dve.wait_ge(s_gg, c + 1)
                    V.tensor_tensor(og[j][:, :, :], two_chunks(o_ps), gg[j][:, :, :], ALU.mult).then_inc(s_og, 1)
                if has_b:
                    for ch in range(CH):
                        dve.wait_ge(s_a, b * CH + ch + 1)
                        V.tensor_tensor(am[bj][:, ch, :, :], a_ps(ch).rearrange("p (g t) -> p g t", g=4),
                                        C["causal4"], ALU.mult).then_inc(s_am, 1)
                    dve.wait_ge(s_u, b + 1)
                    V.scalar_tensor_tensor(S[bj][:, :], u_ps, dS[bj][:, 0:1], C["headmask"], ALU.mult, ALU.mult
                                           ).then_inc(s_S, 1)
                if has_s:
                    dve.wait_ge(s_x[sj], s // 2 * 16 + 16 if isinstance(s, int) else s * 8 + (16 - 8 * sj))
                    for ch in range(CH):
                        last = in_s.mark(V.bn_stats(st[sj][:, ch, :], x[:, s * CH + ch, :]))
                    in_s.need(last, apart)
                    for ch in range(CH):
                        last = V.bn_aggr(mv[sj][:, ch, :], st[sj][:, ch, :])
                    last.then_inc(s_mv, 1)
                if has_a:
                    dve.wait_ge(s_zl, a + 1)
                    in_a.link(V.tensor_scalar(zm[j][:, :], z_ps, b2, 0.0, ALU.add, ALU.min))
                    in_a.link(V.tensor_tensor(zg[j][:, :], zm[j][:, :], zl[j][:, :], ALU.subtract))
                    in_a.link(V.tensor_tensor_scan(cum[j][:, :], C["ones_row"], zg[j][:, :], 0.0, ALU.mult, ALU.add))
                    for ch in range(CH):
                        mid = cum[j][:, P * ch + P // 2 - 1:P * ch + P // 2]
                        last = in_a.mark(V.tensor_scalar(dl[j][:, P * ch:P * ch + P], cum[j][:, P * ch:P * ch + P],
                                                         mid, -CLAMP, ALU.subtract, ALU.max))
                    V.tensor_tensor(dm[j][:, :], cum[j][:, P + P // 2 - 1:P + P // 2], cum[j][:, P // 2 - 1:P // 2],
                                    ALU.subtract)
                    in_a.need(last)
                    V.tensor_scalar(dc[j][:, :], dl[j][:, :], CLAMP, None, ALU.min).then_inc(s_dec, 1)
                if has_d:
                    dve.wait_ge(s_out, d + 1)
                    xs = x[:, bass.ds(d * CH, CH), :]
                    V.tensor_tensor(xs, xs, two_chunks(out_ps), ALU.add).then_inc(s_x1, 1)
                if has_a:
                    dve.wait_ge(s_e, a + 1)
                    dve.wait_ge(s_qk, a + 1)
                    V.scalar_tensor_tensor(qt[j][:, :], q_ps, SCALE, eq[j][:, :], ALU.mult, ALU.mult)
                    V.tensor_tensor(kt[j][:, :], k_ps, ek[j][:, :], ALU.mult).then_inc(s_qt, 1)
                if has_s:
                    dve.wait_ge(s_rs, s + 1)
                    for ch in range(CH):
                        last = V.tensor_scalar(h[sj][:, ch, :], x[:, s * CH + ch, :], mv[sj][:, ch, 0:1],
                                               rs[sj][:, ch:ch + 1], ALU.subtract, ALU.mult)
                    last.then_inc(s_h, 1)
                if has_a:
                    dve.wait_ge(s_gp, a + 1)
                    V.tensor_scalar(gc[j][:, :, :], two_chunks(g_ps), -SIG_CLAMP, None, ALU.max).then_inc(s_gc, 1)

            dve.wait_ge(C["loaded"], C["loads"])
            dve.wait_ge(s_w, 16)
            V.tensor_scalar(won[:, :, :], wo, wn, None, ALU.mult).then_inc(s_won, 1)
            dve.wait_ge(s_w12, 1)
            V.tensor_copy(w12[:, :], ps[:, 0, 0:P]).then_inc(s_w12c, 1)
            bodies(dve, body)


def ffn_attention(nc, C, F, x_dram, tag):
    UNITS, CT = 16, 2
    TILES = UNITS * CT
    DVE_S, DVE_B, DVE_C, DVE_D = 2, 3, 4, 8
    SCALE = 32.0 ** -0.5
    with ExitStack() as ctx:
        sb = lambda name, shape, dt=F32: ctx.enter_context(nc.sbuf_tensor(tag + name, shape, dt))
        sem = PhaseSemaphores(nc, ctx, tag)
        each = lambda name, shape, dt=F32: [sb(f"{name}{j}", shape, dt) for j in range(2)]
        x = sb("x", [P, TILES, D])
        wq, wk, wv, wo, wg, bq, bk, bv, bo, g1, be1 = (F["weights"][k] for k in (
            "WqT", "WkT", "WvT", "WoT", "WgT", "bq", "bk", "bv", "bo", "g1", "be1"))
        strict16, ones16, mask, pads = F["strict16"], F["ones16"], F["mask"], F["pads"]
        sst, smv, sve, srs = each("sst", [P, CT, 6]), each("smv", [P, CT, 2]), each("sve", [P, CT]), each("srs", [P, CT])
        h, hb, hT = each("h", [P, CT, D]), each("hb", [P, CT, D]), each("hT", [P, 256])
        kT, v = each("kT", [P, 256]), each("v", [P, CT, P])
        mx, sd, ex = each("mx", [P, 8]), each("sd", [P, 8, 32]), each("ex", [P, 8, 32])
        su, rs, pr = each("su", [P, 8]), each("rs", [P, 8]), each("pr", [P, 8, 32])
        qx, ptx = F["q_spread"], F["probs_spread"]
        oT = each("oT", [P, CT, P])
        r, st, mv, ve, rst = (each("r", [P, CT, D]), each("st", [P, CT, 6]), each("mv", [P, CT, 2]), each("ve", [P, CT]),
                              each("rst", [P, CT]))
        rg, row, yT = each("rg", [P, CT, D]), each("row", [P, CT, ROW]), each("yT", [P, 256])
        lmx, eq, ei, em, oh = (each("lmx", [P, CT]), each("eq", [P, CT, EXPERTS]), each("ei", [P, CT, EXPERTS]),
                               each("em", [P, CT]), each("oh", [P, CT, EXPERTS]))
        oh16 = each("oh16", [P, CT, EXPERTS], BF16)
        rk, rsel, dest, base = (each("rk", [P, CT, EXPERTS]), each("rsel", [P, CT, EXPERTS]), each("dest", [P, CT], I32),
                                each("base", [P, EXPERTS]))
        ps = ctx.enter_context(nc.psum_tensor(tag + "ps", [P, 8, 512], F32))
        hT_ps, q_ps, k_ps, v_ps = ps[:, 0, 0:256], ps[:, 1, 0:256], ps[:, 2, 0:256], ps[:, 2, 256:512]
        s_ps, pt_ps, pv_ps, mha_ps = ps[:, 3, 0:256], ps[:, 4, 0:256], ps[:, 5, 0:256], ps[:, 5, 256:512]
        yT_ps, lg_ps, rank_ps = ps[:, 6, 0:256], ps[:, 7, 0:16], ps[:, 7, 32:56]

        s_ends, s_pads, s_x = sem("expert_ends_ready"), sem("pads_stored"), sem("x_ready")
        s_xl = [sem(f"x_loaded{j}") for j in range(2)]
        s_smv, s_srs, s_h, s_hb, s_hTp, s_hT, s_q, s_kv, s_qx, s_kvc = (sem(k) for k in (
            "x_stats", "x_rstd", "normed", "h_plus_bo", "hT_psum", "hT_copied", "q_product", "kv_product", "q_spread",
            "kv_copied"))
        s_s, s_sd, s_ex, s_pr, s_pt, s_px, s_pv, s_oT = (sem(k) for k in (
            "scores", "scores_less_max", "scores_exp", "probs", "probsT_psum", "probsT_spread", "pv_product", "oT_copied"))
        s_mha, s_r, s_st, s_rst, s_y, s_xc, s_yTp, s_yT = (sem(k) for k in (
            "mha_product", "r_ready", "r_stats", "r_rstd", "y_ready", "x_in_row", "yT_psum", "yT_copied"))
        s_lg, s_oh, s_rank, s_dest = (sem(k) for k in ("logits", "one_hot", "ranks", "dest_ready"))
        s_scat = [sem(f"scattered{j}") for j in range(2)]
        c_s, c_b, c_c, c_d, c_pool_s, c_pool_c, apart = (sem(k) for k in (
            "dve_steps_s", "dve_steps_b", "dve_steps_c", "dve_steps_d", "pool_steps_s", "pool_steps_c", "apart"))
        tiles = lambda a: a.rearrange("p (c e) -> p c e", c=CT)

        def bodies(eng, body):
            for n in range(-3, 3):
                body(n, n % 2, [n + k >= 0 for k in range(-1, 4)])
            with eng.Fori(0, (UNITS - 6) // 2) as i:
                for k in range(2):
                    body(2 * i + k + 3, (k + 1) % 2, [True] * 5)
            for n in range(UNITS - 3, UNITS + 1):
                body(n, n % 2, [n + k < UNITS for k in range(-1, 4)])

        def pT_quarter(j, k):
            rows = slice(32 * k, 32 * k + 32)
            return ptx[j][rows, :, k, :], tiles(pt_ps[rows, :])

        def store_pads(eng, experts):
            eng.wait_ge(s_ends, 1)
            for e in experts:
                start = eng.value_load(F["tables"][0:1, 2 * BLOCKS + e:2 * BLOCKS + e + 1], min_val=0, max_val=ROWS - P)
                eng.dma_start(F["scratch_rows"][bass.ds(start, P), :], pads[:, e, :]).then_inc(s_pads, 16)

        block = ctx.enter_context(nc.Block())

        @block.sync
        def _(sp):
            by_tile = x_dram.rearrange("s (g l) d -> g l s d", l=8)

            def load(n, j):
                for t in range(CT):
                    sp.dma_start(x[:, bass.ds(n * CT + t, 1), :], by_tile[bass.ds(n * CT + t, 1)]).then_inc(s_xl[j], 16)

            def loaded(count, j):
                sp.wait_ge(s_xl[j], count)
                sp.sem_inc(s_x, 1)

            load(0, 0)
            load(1, 1)
            with sp.Fori(0, UNITS // 2 - 1) as i:
                for j in range(2):
                    loaded(16 * CT * (i + 1), j)
                    load(2 * i + 2 + j, j)
            for j in range(2):
                loaded(16 * CT * (UNITS // 2), j)
            store_pads(sp, range(0, EXPERTS // 2))
            sp.wait_ge(s_pads, 16 * EXPERTS)

        @block.tensor
        def _(pe):
            def body(n, j, has):
                d, c, b, a = n - 1, n, n + 1, n + 2
                dj, cj, bj, aj = 1 - j, j, 1 - j, j
                has_d, has_c, has_b, has_a, has_s = has
                if has_a:
                    pe.wait_ge(s_h, a + 1)
                    for t in range(CT):
                        last = nc.tensor.transpose(hT_ps[:, P * t:P * t + P], h[aj][:, t, :], C["ident"])
                    last.then_inc(s_hTp, 1)
                if has_c:
                    pe.wait_ge(s_oT, c + 1)
                    for t in range(CT):
                        last = nc.tensor.matmul(mha_ps[:, P * t:P * t + P], oT[cj][:, t, :], wo, start=True, stop=True)
                    last.then_inc(s_mha, 1)
                if has_d:
                    pe.wait_ge(s_yT, d + 1)
                    if not isinstance(n, int) or d > 0:
                        pe.wait_ge(s_dest, d)
                    for t in range(CT):
                        last = nc.tensor.matmul(lg_ps[:, 8 * t:8 * t + 8], yT[dj][:, P * t:P * t + P], wg,
                                                start=True, stop=True)
                    last.then_inc(s_lg, 1)
                if has_a:
                    pe.wait_ge(s_hT, a + 1)
                    nc.tensor.matmul(q_ps, wq, hT[aj][:, :], start=True, stop=True).then_inc(s_q, 1)
                    nc.tensor.matmul(k_ps, wk, hT[aj][:, :], start=True, stop=True)
                    for t in range(CT):
                        last = nc.tensor.matmul(v_ps[:, P * t:P * t + P], hT[aj][:, P * t:P * t + P], wv,
                                                start=True, stop=True)
                    last.then_inc(s_kv, 1)
                if has_b:
                    pe.wait_ge(s_pr, b + 1)
                    for t in range(CT):
                        last = nc.tensor.transpose(pt_ps[:, P * t:P * t + P], pr[bj][:, 4 * t:4 * t + 4, :], C["ident"])
                    last.then_inc(s_pt, 1)
                if has_d:
                    pe.wait_ge(s_oh, d + 1)
                    nc.tensor.matmul(rank_ps[:, 0:16], strict16[:, :], oh16[dj][:, :, :], start=True, stop=False,
                                     skip_group_check=True)
                    nc.tensor.matmul(rank_ps[:, 8:16], ones16[:, :], oh16[dj][:, 0, :], start=False, stop=False,
                                     skip_group_check=True)
                    nc.tensor.matmul(rank_ps[:, 16:24], ones16[:, :], oh16[dj][:, 0, :], start=False, stop=False,
                                     skip_group_check=True)
                    nc.tensor.matmul(rank_ps[:, 16:24], ones16[:, :], oh16[dj][:, 1, :], start=False, stop=True,
                                     skip_group_check=True).then_inc(s_rank, 1)
                if has_a:
                    pe.wait_ge(s_qx, a + 1)
                    pe.wait_ge(s_kvc, a + 1)
                    if has_b:
                        pe.wait_ge(s_sd, b + 1)
                    nc.tensor.matmul(s_ps, C["ident"], mask[:, :, :], start=True, stop=False, skip_group_check=True)
                    for pair in range(8):
                        last = nc.tensor.matmul(s_ps[:, 32 * pair:32 * pair + 32], qx[aj][:, 2 * pair:2 * pair + 2, :, :],
                                                kT[aj][:, 32 * pair:32 * pair + 32], start=False, stop=(pair == 7),
                                                skip_group_check=True)
                    last.then_inc(s_s, 1)
                if has_b:
                    pe.wait_ge(s_px, b + 1)
                    if has_c:
                        pe.wait_ge(s_r, c + 1)
                    for t in range(CT):
                        for hd in range(4):
                            rows = slice(32 * hd, 32 * hd + 32)
                            probs = ptx[bj][:, t, :, :].rearrange("p k (l h q) -> p (k l) h q", l=2, h=4)[:, :, hd, :]
                            last = nc.tensor.matmul(pv_ps[rows, P * t:P * t + P], v[bj][:, t, rows], probs,
                                                    start=True, stop=True)
                    last.then_inc(s_pv, 1)
                if has_c:
                    pe.wait_ge(s_y, c + 1)
                    for t in range(CT):
                        last = nc.tensor.transpose(yT_ps[:, P * t:P * t + P], row[cj][:, t, 0:D], C["ident"])
                    last.then_inc(s_yTp, 1)

            bodies(pe, body)

        @block.scalar
        def _(act):
            def body(n, j, has):
                c, b, a = n, n + 1, n + 2
                cj, bj, aj = j, 1 - j, j
                has_d, has_c, has_b, has_a, has_s = has
                if has_a:
                    act.wait_ge(s_hTp, a + 1)
                    nc.scalar.activation(hT[aj][:, :], hT_ps, ACT.Copy).then_inc(s_hT, 1)
                if has_b:
                    act.wait_ge(s_sd, b + 1)
                    nc.scalar.activation(ex[bj][:, :, :], sd[bj][:, :, :], ACT.Exp, scale=SCALE).then_inc(s_ex, 1)
                if has_a:
                    act.wait_ge(s_q, a + 1)
                    for hd in range(4):
                        rows = slice(32 * hd, 32 * hd + 32)
                        last = nc.scalar.activation(qx[aj][rows, :, hd, :], q_ps[rows, :].rearrange("p (l s) -> p l s", s=16),
                                                    ACT.Identity, bias=bq[rows])
                    last.then_inc(s_qx, 1)
                if has_a:
                    act.wait_ge(s_kv, a + 1)
                    nc.scalar.activation(kT[aj][:, :], k_ps, ACT.Identity, bias=bk)
                    nc.scalar.activation(v[aj][:, :, :], tiles(v_ps), ACT.Copy).then_inc(s_kvc, 1)
                if has_b:
                    act.wait_ge(s_pt, b + 1)
                    for k in range(4):
                        last = nc.scalar.activation(*pT_quarter(bj, k), ACT.Copy)
                    last.then_inc(s_px, 1)
                if has_b:
                    act.wait_ge(s_pv, b + 1)
                    nc.scalar.activation(oT[bj][:, :, :], tiles(pv_ps), ACT.Identity, bias=bv).then_inc(s_oT, 1)
                if has_c:
                    act.wait_ge(s_yTp, c + 1)
                    nc.scalar.activation(yT[cj][:, :], yT_ps, ACT.Copy).then_inc(s_yT, 1)
                    nc.scalar.activation(row[cj][:, :, D:2 * D], x[:, bass.ds(c * CT, CT), :], ACT.Copy).then_inc(s_xc, 1)

            act.preload_act_table_set(EXP_LN)
            bodies(act, body)
            store_pads(act, range(EXPERTS // 2, EXPERTS))

        @block.gpsimd
        def _(pool):
            in_s, in_c = Chain(pool, c_pool_s, apart), Chain(pool, c_pool_c, apart)
            G_ = nc.gpsimd
            wide = lambda a: a.unsqueeze(1).to_broadcast([P, CT, P])

            def body(n, j, has):
                d, c, b, s = n - 1, n, n + 1, n + 3
                dj, cj, bj, sj = 1 - j, j, 1 - j, 1 - j
                has_d, has_c, has_b, has_a, has_s = has
                in_s.enter(s)
                in_c.enter(c)
                if has_b:
                    pool.wait_ge(s_h, b + 1)
                    G_.tensor_tensor(hb[bj][:, :, :], h[bj][:, :, :], wide(bo), ALU.add).then_inc(s_hb, 1)
                if has_c:
                    wait_apart(pool, apart, s_st, c + 1)
                    in_c.link(G_.tensor_scalar(ve[cj][:, :], mv[cj][:, :, 1], EPS, None, ALU.add))
                    G_.tensor_tensor(rst[cj][:, :], ve[cj][:, :], C["neg_half"][:, 0:CT], ALU.pow).then_inc(s_rst, 1)
                if has_s:
                    wait_apart(pool, apart, s_smv, s + 1)
                    in_s.link(G_.tensor_scalar(sve[sj][:, :], smv[sj][:, :, 1], EPS, None, ALU.add))
                    G_.tensor_tensor(srs[sj][:, :], sve[sj][:, :], C["neg_half"][:, 0:CT], ALU.pow).then_inc(s_srs, 1)
                if has_d:
                    wait_apart(pool, apart, s_xc, d + 1)
                    wait_apart(pool, apart, s_dest, d + 1)
                    for t in range(CT):
                        G_.indirect_dma_start(F["scratch_rows"], bass.IndirectOffsetOnAxis(ap=dest[dj][:, t:t + 1], axis=0),
                                              row[dj][:, t, :], None).then_inc(s_scat[dj], 16)

            bodies(pool, body)
            for j in range(2):
                pool.wait_ge(s_scat[j], 16 * CT * UNITS // 2)

        @block.vector
        def _(dve):
            in_s, in_b, in_c, in_d = (Chain(dve, k) for k in (c_s, c_b, c_c, c_d))
            V = nc.vector

            def body(n, j, has):
                d, c, b, s = n - 1, n, n + 1, n + 3
                dj, cj, bj, sj = 1 - j, j, 1 - j, 1 - j
                has_d, has_c, has_b, has_a, has_s = has
                in_s.enter(s * DVE_S)
                in_b.enter(b * DVE_B)
                in_c.enter(c * DVE_C)
                in_d.enter(d * DVE_D)
                if has_b:
                    dve.wait_ge(s_s, b + 1)
                    scores = s_ps.rearrange("p (g k) -> p g k", k=32)
                    in_b.link(V.tensor_reduce(mx[bj][:, :], scores, AX.X, ALU.max))
                    V.tensor_tensor(sd[bj][:, :, :], scores, mx[bj][:, :].unsqueeze(2).to_broadcast([P, 8, 32]),
                                    ALU.subtract).then_inc(s_sd, 1)
                if has_s:
                    dve.wait_ge(s_x, s + 1)
                    for t in range(CT):
                        taken = in_s.mark(V.bn_stats(sst[sj][:, t, :], x[:, s * CT + t, :]))
                if has_d:
                    dve.wait_ge(s_lg, d + 1)
                    lg = tiles(lg_ps)
                    spread = lambda a: a[:, :].unsqueeze(2).to_broadcast([P, CT, EXPERTS])
                    index = C["expert_less_8"].unsqueeze(1).to_broadcast([P, CT, EXPERTS])
                    in_d.link(V.tensor_reduce(lmx[dj][:, :], lg, AX.X, ALU.max))
                    in_d.link(V.tensor_tensor(eq[dj][:, :, :], lg, spread(lmx[dj]), ALU.is_ge))
                    in_d.mark(V.tensor_tensor(ei[dj][:, :, :], eq[dj][:, :, :], index, ALU.mult))
                if has_b:
                    dve.wait_ge(s_ex, b + 1)
                    in_b.mark(V.tensor_reduce(su[bj][:, :], ex[bj][:, :, :], AX.X, ALU.add))
                if has_s:
                    in_s.need(taken, apart)
                    for t in range(CT):
                        last = V.bn_aggr(smv[sj][:, t, :], sst[sj][:, t, :])
                    last.then_inc(s_smv, 1)
                if has_d:
                    in_d.need(3)
                    in_d.mark(V.tensor_reduce(em[dj][:, :], ei[dj][:, :, :], AX.X, ALU.min))
                if has_b:
                    in_b.need(2)
                    in_b.mark(V.reciprocal(rs[bj][:, :], su[bj][:, :]))
                if has_d:
                    in_d.need(4)
                    V.tensor_tensor(oh[dj][:, :, :], index, spread(em[dj]), ALU.is_equal)
                    V.tensor_tensor(oh16[dj][:, :, :], index, spread(em[dj]), ALU.is_equal).then_inc(s_oh, 1)
                if has_b:
                    in_b.need(3)
                    V.tensor_tensor(pr[bj][:, :, :], ex[bj][:, :, :], rs[bj][:, :].unsqueeze(2).to_broadcast([P, 8, 32]),
                                    ALU.mult).then_inc(s_pr, 1)
                if has_c:
                    dve.wait_ge(s_mha, c + 1)
                    dve.wait_ge(s_hb, c + 1)
                    V.tensor_tensor(r[cj][:, :, :], tiles(mha_ps), hb[cj][:, :, :], ALU.add).then_inc(s_r, 1)
                    dve.wait_ge(s_r, c + 1)
                    for t in range(CT):
                        last = in_c.mark(V.bn_stats(st[cj][:, t, :], r[cj][:, t, :]))
                    in_c.need(last, apart)
                    for t in range(CT):
                        last = V.bn_aggr(mv[cj][:, t, :], st[cj][:, t, :])
                    last.then_inc(s_st, 1)
                if has_d:
                    dve.wait_ge(s_rank, d + 1)
                    in_d.mark(V.tensor_tensor(rk[dj][:, :, :], tiles(rank_ps[:, 0:16]),
                                              base[dj][:, :].unsqueeze(1).to_broadcast([P, CT, EXPERTS]), ALU.add))
                    in_d.mark(V.tensor_tensor(base[1 - dj][:, :], rank_ps[:, 16:24], base[dj][:, :], ALU.add))
                if has_c:
                    dve.wait_ge(s_st, c + 1)
                    for t in range(CT):
                        last = in_c.mark(V.scalar_tensor_tensor(rg[cj][:, t, :], r[cj][:, t, :], mv[cj][:, t, 0:1], g1,
                                                                ALU.subtract, ALU.mult))
                if has_d:
                    in_d.need(5)
                    in_d.link(V.tensor_tensor(rsel[dj][:, :, :], rk[dj][:, :, :], oh[dj][:, :, :], ALU.mult))
                    with nc.allow_low_precision(reason="whole numbers below 2**24"):
                        in_d.mark(V.tensor_reduce(dest[dj][:, :], rsel[dj][:, :, :], AX.X, ALU.add))
                if has_c:
                    if not isinstance(n, int) or n >= 2:
                        dve.wait_ge(s_scat[cj], (n - cj) * 8 * CT)
                    V.tensor_copy(row[cj][:, :, 2 * D:ROW], C["token"][:, bass.ds(c * CT, CT)].unsqueeze(2))
                    dve.wait_ge(s_rst, c + 1)
                    in_c.need(last)
                    for t in range(CT):
                        mine = V.scalar_tensor_tensor(row[cj][:, t, 0:D], rg[cj][:, t, :], rst[cj][:, t:t + 1], be1,
                                                      ALU.mult, ALU.add)
                    mine.then_inc(s_y, 1)
                if has_d:
                    in_d.need(4 + 4)
                    dve.sem_inc(s_dest, 1)
                if has_s:
                    dve.wait_ge(s_srs, s + 1)
                    if has_b:
                        dve.wait_ge(s_hb, b + 1)
                    for t in range(CT):
                        mine = V.tensor_scalar(h[sj][:, t, :], x[:, s * CT + t, :], smv[sj][:, t, 0:1], srs[sj][:, t:t + 1],
                                               ALU.subtract, ALU.mult)
                    mine.then_inc(s_h, 1)

            V.tensor_copy(base[0][:, :], C["region_start"])
            bodies(dve, body)
            routing_tables(nc, dve, C, F, base[0], sb, sem, s_ends)


def routing_tables(nc, dve, C, F, base, sb, sem, s_ends):
    s = sem("table_steps")
    count = [0]

    def link(ins):
        count[0] += 1
        ins.then_inc(s, 1)
        dve.wait_ge(s, count[0])

    n_f, n_i, nb_i, nb, cum = (sb("t_n", [P, EXPERTS]), sb("t_ni", [P, EXPERTS], I32), sb("t_nbi", [P, EXPERTS], I32),
                               sb("t_nb", [P, EXPERTS]), sb("t_cum", [P, EXPERTS]))
    skip, past, pskip = sb("t_skip", [P, EXPERTS]), sb("t_past", [P, BLOCKS, EXPERTS]), sb("t_ps", [P, BLOCKS, EXPERTS])
    expert, rows = sb("t_e", [P, BLOCKS]), sb("t_r", [P, BLOCKS])
    nc.vector.tensor_copy(F["tables"][0:1, 2 * BLOCKS:2 * BLOCKS + EXPERTS], base[0:1, :]).then_inc(s_ends, 1)
    link(nc.vector.tensor_tensor(n_f[:, :], base[:, :], C["region_start"], ALU.subtract))
    link(nc.vector.tensor_scalar(n_i[:, :], n_f[:, :], float(P - 1), None, ALU.add))
    link(nc.vector.tensor_scalar(nb_i[:, :], n_i[:, :], 7, None, ALU.logical_shift_right))
    link(nc.vector.tensor_copy(nb[:, :], nb_i[:, :]))
    link(nc.vector.tensor_tensor_scan(cum[:, :], C["ones"][:, 0:EXPERTS], nb[:, :], 0.0, ALU.mult, ALU.add))
    link(nc.vector.tensor_scalar(skip[:, :], nb[:, :], -float(P), float(REGION), ALU.mult, ALU.add))
    shape = [P, BLOCKS, EXPERTS]
    block = C["block"].unsqueeze(2).to_broadcast(shape)
    link(nc.vector.tensor_tensor(past[:, :, :], block, cum[:, :].unsqueeze(1).to_broadcast(shape), ALU.is_ge))
    link(nc.vector.tensor_tensor(pskip[:, :, :], past[:, :, :], skip[:, :].unsqueeze(1).to_broadcast(shape), ALU.mult))
    link(nc.vector.tensor_reduce(expert[:, :], past[:, :, :], AX.X, ALU.add))
    link(nc.vector.tensor_reduce(rows[:, :], pskip[:, :, :], AX.X, ALU.add))
    link(nc.vector.tensor_scalar(F["tables"][0:1, 0:BLOCKS], expert[0:1, :], float(EXPERTS - 1), None, ALU.min))
    link(nc.vector.scalar_tensor_tensor(F["tables"][0:1, BLOCKS:2 * BLOCKS], C["block"][0:1, :], float(P), rows[0:1, :],
                                        ALU.mult, ALU.add))


def ffn_experts(nc, io, C, F, out_rows, tag):
    LANES = 4
    TURNS = BLOCKS // LANES
    assert TURNS * LANES == BLOCKS and TURNS % 2 == 0
    FC = DF // P
    WCOLS = DF + FC + P
    with ExitStack() as ctx:
        sb = lambda name, shape, dt=F32: ctx.enter_context(nc.sbuf_tensor(tag + name, shape, dt))
        sem = PhaseSemaphores(nc, ctx, tag)
        lanes = range(LANES)
        each = lambda name, shape, dt=F32: [sb(f"{name}{j}", shape, dt) for j in lanes]
        both = lambda name, shape, dt=F32: [each(f"{name}{k}_", shape, dt) for k in range(2)]
        w2, g2, be2 = F["w2"], F["weights"]["g2"], F["weights"]["be2"]
        row, wst = both("row", [P, ROW]), both("wst", [P, WCOLS])
        hh, yb, xb, to = both("hh", [P, FC, P]), both("yb", [P, D]), both("xb", [P, D]), both("to", [P, 1], I32)
        yT, r, st, rg, z = each("yT", [P, P]), each("r", [P, D]), each("st", [P, 6]), each("rg", [P, D]), each("z", [P, D])
        mv, ve, rst = sb("mv", [P, LANES, 2]), sb("ve", [P, LANES]), sb("rst", [P, LANES])
        ps = ctx.enter_context(nc.psum_tensor(tag + "ps", [P, 8, 512], F32))
        hh_ps = [ps[:, 2 * j, :] for j in lanes]
        yT_ps = [ps[:, 2 * j + 1, 0:P] for j in lanes]
        out_ps = [ps[:, 2 * j + 1, 256:256 + D] for j in lanes]
        s_yTp, s_yT, s_h, s_hr, s_out = (sem(k) for k in (
            "yT_psum", "yT_copied", "hidden_product", "hidden_ready", "out_product"))
        s_yb, s_xb, s_to, s_r, s_st, s_rg, s_z = (sem(k) for k in (
            "y_plus_bias", "x_plus_bias", "place_ready", "r_ready", "r_sums", "r_scaled", "z_ready"))
        s_mv, s_ve, s_rst, apart = (sem(k) for k in ("r_stats", "r_variance", "r_rstd", "apart"))
        s_store = [sem(f"z_stored{j}") for j in lanes]
        s_wst = [[sem(f"weights_staged{k}_{j}") for j in lanes] for k in range(2)]
        s_load = [[sem(f"rows_loaded{k}_{j}") for j in lanes] for k in range(2)]
        by_sync, by_act = range(0, LANES // 2), range(LANES // 2, LANES)

        def units(n):
            return [(j, n * LANES + j) for j in lanes]

        def times16(n, k):
            return (n - k) * 8 + 16

        def bodies(eng, body):
            for n in range(-2, 1):
                body(n, n % 2, [n + t >= 0 for t in range(3)])
            with eng.Fori(0, (TURNS - 4) // 2) as i:
                for k in (1, 0):
                    body(2 * i + 2 - k, k, [True] * 3)
            for n in range(TURNS - 3, TURNS):
                body(n, n % 2, [n + t < TURNS for t in range(3)])

        def expert(eng, b):
            return eng.value_load(F["tables"][0:1, bass.ds(b, 1)], min_val=0, max_val=EXPERTS - 1)

        def load(eng, k, j, b):
            first = eng.value_load(F["tables"][0:1, bass.ds(b + BLOCKS, 1)], min_val=0, max_val=ROWS - P)
            eng.dma_start(row[k][j][:, :], F["scratch_rows"][bass.ds(first, P), :]).then_inc(s_load[k][j], 16)

        def load_over(eng, own, n, k):
            for j, b in units(n):
                if j in own:
                    eng.wait_ge(s_yTp, b + 1)
                    eng.wait_ge(s_to, b + 1)
                    load(eng, k, j, b + 2 * LANES)

        block = ctx.enter_context(nc.Block())

        @block.sync
        def _(sp):
            def stage(k, j, b):
                sp.dma_start(wst[k][j][:, :], io["w1b"][bass.ds(expert(sp, b), 1)].rearrange("e p w -> p (e w)")
                             ).then_inc(s_wst[k][j], 16)

            def body(n, k, has):
                has_n, has_next, has_ahead = has
                if has_n and has_ahead:
                    load_over(sp, by_sync, n, k)
                    for j, b in units(n):
                        sp.wait_ge(s_hr, b + 1)
                        sp.wait_ge(s_yb, b + 1)
                        stage(k, j, b + 2 * LANES)

            for k in range(2):
                for j in by_sync:
                    load(sp, k, j, LANES * k + j)
                for j in lanes:
                    stage(k, j, LANES * k + j)
            bodies(sp, body)

        @block.gpsimd
        def _(pool):
            def body(n, k, has):
                if has[0]:
                    wait_apart(pool, apart, s_mv, n + 1)
                    nc.gpsimd.tensor_scalar(ve[:, :], mv[:, :, 1], EPS, None, ALU.add).then_inc(s_ve, 1)
                    wait_apart(pool, apart, s_ve, n + 1)
                    nc.gpsimd.tensor_tensor(rst[:, :], ve[:, :], C["neg_half"][:, 0:LANES], ALU.pow).then_inc(s_rst, 1)
                    for j, b in units(n):
                        wait_apart(pool, apart, s_z, b + 1)
                        nc.gpsimd.indirect_dma_start(out_rows, bass.IndirectOffsetOnAxis(ap=to[k][j][:, 0:1], axis=0),
                                                     z[j][:, :], None).then_inc(s_store[j], 16)

            bodies(pool, body)
            for j in lanes:
                pool.wait_ge(s_store[j], 16 * TURNS)

        @block.tensor
        def _(pe):
            def body(n, k, has):
                has_n, has_next, has_ahead = has
                experts = []
                if has_next:
                    for j, b in units(n + 1):
                        pe.wait_ge(s_yT, b + 1)
                        pe.wait_ge(s_wst[1 - k][j], times16(n + 1, 1 - k))
                        if has_n:
                            pe.wait_ge(s_hr, b - LANES + 1)
                        for f in range(FC):
                            last = nc.tensor.matmul(hh_ps[j][:, P * f:P * f + P], wst[1 - k][j][:, P * f:P * f + P],
                                                    yT[j][:, :], start=True, stop=True)
                        last.then_inc(s_h, 1)
                        if has_n:
                            experts.append(expert(pe, b - LANES))
                if has_n:
                    if not has_next:
                        experts = [expert(pe, b) for j, b in units(n)]
                    for j, b in units(n):
                        pe.wait_ge(s_hr, b + 1)
                        if isinstance(n, int) and n == TURNS - 1:
                            pe.wait_ge(s_r, b - LANES + 1)
                        for f in range(FC):
                            last = nc.tensor.matmul(out_ps[j], hh[k][j][:, f, :],
                                                    w2[:, bass.ds(experts[j] * (FC * D) + f * D, D)],
                                                    start=(f == 0), stop=(f == FC - 1))
                        last.then_inc(s_out, 1)
                if has_ahead:
                    for j, b in units(n + 2):
                        pe.wait_ge(s_load[k][j], times16(n + 2, k))
                        if has_n:
                            pe.wait_ge(s_r, b - 2 * LANES + 1)
                        elif has_next:
                            pe.wait_ge(s_yT, b - LANES + 1)
                        nc.tensor.transpose(yT_ps[j], row[k][j][:, 0:D], C["ident"]).then_inc(s_yTp, 1)

            bodies(pe, body)

        @block.scalar
        def _(act):
            def body(n, k, has):
                has_n, has_next, has_ahead = has
                if has_n and has_ahead:
                    load_over(act, by_act, n, k)
                if has_next:
                    for j, b in units(n + 1):
                        act.wait_ge(s_h, b + 1)
                        for f in range(FC):
                            last = nc.scalar.activation(hh[1 - k][j][:, f, :], hh_ps[j][:, P * f:P * f + P], ACT.Relu,
                                                        bias=wst[1 - k][j][:, DF + f:DF + f + 1])
                        last.then_inc(s_hr, 1)
                if has_ahead:
                    for j, b in units(n + 2):
                        act.wait_ge(s_yTp, b + 1)
                        nc.scalar.activation(yT[j][:, :], yT_ps[j], ACT.Copy).then_inc(s_yT, 1)

            for k in range(2):
                for j in by_act:
                    load(act, k, j, LANES * k + j)
            act.preload_act_table_set(EXP_LN)
            bodies(act, body)

        @block.vector
        def _(dve):
            V = nc.vector

            def body(n, k, has):
                has_n, has_next, has_ahead = has
                if has_n:
                    for j, b in units(n):
                        dve.wait_ge(s_out, b + 1)
                        dve.wait_ge(s_yb, b + 1)
                        V.tensor_tensor(r[j][:, :], out_ps[j], yb[k][j][:, :], ALU.add).then_inc(s_r, 1)
                    for j, b in units(n):
                        dve.wait_ge(s_r, b + 1)
                        V.bn_stats(st[j][:, :], r[j][:, :]).then_inc(s_st, 1)
                    wait_apart(dve, apart, s_st, n * LANES + LANES)
                    for j in lanes:
                        last = V.bn_aggr(mv[:, j, :], st[j][:, :])
                    last.then_inc(s_mv, 1)
                if has_next:
                    for j, b in units(n + 1):
                        dve.wait_ge(s_load[1 - k][j], times16(n + 1, 1 - k))
                        dve.wait_ge(s_wst[1 - k][j], times16(n + 1, 1 - k))
                        V.tensor_tensor(yb[1 - k][j][:, :], row[1 - k][j][:, 0:D], wst[1 - k][j][:, DF + FC:WCOLS], ALU.add
                                        ).then_inc(s_yb, 1)
                        if not isinstance(n, int) or n > 0:
                            dve.wait_ge(s_z, b - 2 * LANES + 1)
                        V.tensor_tensor(xb[1 - k][j][:, :], row[1 - k][j][:, D:2 * D], be2, ALU.add).then_inc(s_xb, 1)
                if has_n:
                    dve.wait_ge(s_rst, n + 1)
                    for j, b in units(n):
                        V.scalar_tensor_tensor(rg[j][:, :], r[j][:, :], mv[:, j, 0:1], g2, ALU.subtract, ALU.mult
                                               ).then_inc(s_rg, 1)
                for j in lanes:
                    if not isinstance(n, int) or n > 0:
                        dve.wait_ge(s_store[j], 16 * n)
                    if has_next:
                        V.tensor_copy(to[1 - k][j][:, :], row[1 - k][j][:, 2 * D:ROW]).then_inc(s_to, 1)
                    if has_n:
                        b = n * LANES + j
                        dve.wait_ge(s_rg, b + 1)
                        dve.wait_ge(s_xb, b + 1)
                        V.scalar_tensor_tensor(z[j][:, :], rg[j][:, :], rst[:, j:j + 1], xb[k][j][:, :], ALU.mult, ALU.add
                                               ).then_inc(s_z, 1)

            bodies(dve, body)


def rwkv_phase(nc, C, W, x_dram, out_dram):
    UNITS, CT = SEQ, 2
    FC = DF // P
    LIM = 30.0
    DVE_EVEN, DVE_ODD, DVE_A, DVE_B, DVE_C, ACT_B, ACT_D, POOL_C = 4, 2, 1, 7, 5, 4, 2, 2
    with ExitStack() as ctx:
        sb = lambda name, shape, dt=F32: ctx.enter_context(nc.sbuf_tensor("rk_" + name, shape, dt))
        sem = PhaseSemaphores(nc, ctx, "rk_")
        each = lambda names, shape: ([sb(f"{name}{j}", shape) for j in range(2)] for name in names.split())
        x = sb("x", [P, UNITS * CT, D])
        wk, wv, wr, wcr, wck, cols = (W[k] for k in ("w_tk", "w_tv", "w_tr", "w_cr", "w_ck", "rwkv_cols"))
        wcv = W["w_cv"].rearrange("p (f d) -> p f d", d=D)
        ln1g, ln1b, ln2g, ln2b, mixk, mixv, mixr, cmixk, cmixr, decay, first = (cols[:, k:k + 1] for k in range(11))
        U = sb("U", [P, 1])
        TWO = 2 * CT
        sst, smv = sb("sst", [P, TWO, 6]), sb("smv", [P, TWO, 2])
        sve, rs1, t1, t2, rs2, rs12, nm12, rs1u, nm1 = (sb(k, [P, TWO]) for k in (
            "sve", "rs1", "t1", "t2", "rs2", "rs12", "nm12", "rs1u", "nm1"))
        u, hn = each("u hn", [P, CT, D])
        hT, = each("hT", [P, L + 1])
        dh, xk, xv, xr = each("dh xk xv xr", [P, L])
        m, Q, wkv = each("m Q wkv", [P, L + 1])
        mu, muc, X, Xi, e1, e2, lnQ, lam, G, Gi, al, bv, vs = each("mu muc X Xi e1 e2 lnQ lam G Gi al bv vs", [P, L])
        lw, sw, rc, re, rl, sr = each("lw sw rc re rl sr", [P, L])
        d1, d2, yv, ry = each("d1 d2 yv ry", [P, L])
        xp, h2, xs = each("xp h2 xs", [P, CT, D])
        st, = each("st", [P, CT, 6])
        mv, = each("mv", [P, CT, 2])
        ve, rst, nm = each("ve rst rnm", [P, CT])
        h2T, = each("h2T", [P, L + 1])
        dh2, ck, cr = each("dh2 ck cr", [P, L])
        rk, kk = each("rk kk", [P, FC, L])
        cc, ce, cl, sc = each("cc ce cl sc", [P, L])
        o, = each("o", [P, CT, D])
        ps = ctx.enter_context(nc.psum_tensor("rk_ps", [P, 8, 512], F32))
        hT_ps, k_ps, r_ps, v_ps = ps[:, 0, 0:256], ps[:, 1, 0:256], ps[:, 1, 256:512], ps[:, 2, 0:256]
        w_ps, h2T_ps = ps[:, 3, 0:256], ps[:, 3, 256:512]
        kk_ps, kv_ps, cr_ps = ps[:, 4:6, :], ps[:, 6, 0:256], ps[:, 7, 0:256]
        s_U, s_set, s_store = (sem(k) for k in ("first_exp", "bounds_set", "stored"))
        s_smv, s_rs1, s_var2, s_rs2, s_r12, s_n12, s_n1 = (sem(k) for k in (
            "x_stats", "x_rstd", "var2_ready", "rstd2", "rstd12", "norm12_ready", "norm1_ready"))
        s_hn, s_u, s_hTp, s_hT, s_mix, s_kvr = (sem(k) for k in (
            "normed_twice", "normed", "hT_psum", "hT_copied", "mixed", "kvr_product"))
        s_mu, s_X, s_Q, s_lnQ, s_lam, s_G, s_rc, s_sr, s_sw, s_vs = (sem(k) for k in (
            "shift_ready", "shift_exp", "Q_ready", "Q_ln", "lam_ready", "lam_exp", "r_clamped", "r_sigmoid", "y_sigmoid",
            "v_copied"))
        s_d2, s_ry, s_wp, s_st, s_rst, s_nm, s_h2, s_h2Tp, s_h2T, s_cmix, s_xs = (sem(k) for k in (
            "d2_ready", "ry_ready", "w_psum", "xp_stats", "xp_rstd", "xp_norm_ready", "h2_ready", "h2T_psum",
            "h2T_copied", "cmixed", "x_plus_xp"))
        s_kk, s_relu, s_kk2, s_crp, s_kv, s_cc, s_sc, s_o, s_out = (sem(k) for k in (
            "kk_product", "relu_ready", "kk_squared", "cr_product", "kv_product", "cr_clamped", "cr_sigmoid", "o_ready",
            "x_out"))
        s_x, s_cr = [sem(f"x_loaded{k}") for k in range(2)], sem("cr_mixed")
        c_even, c_odd, c_a, c_b, c_c, c_act_b, c_act_d, c_pool, c_pool_s, apart = (sem(k) for k in (
            "dve_steps_even", "dve_steps_odd", "dve_steps_a", "dve_steps_b", "dve_steps_c", "act_steps_b", "act_steps_d",
            "pool_steps_c", "pool_steps_statistics", "apart"))
        tiles = lambda t: t.rearrange("p (c e) -> p c e", c=CT)

        def pair_of(a, pair):
            return a // 2 if isinstance(a, int) else pair - 1

        def bodies(eng, body):
            def whole(n):
                a = n + 3
                pair = a // 2 + 1
                body(n, n % 2, [0 <= n + k < UNITS for k in range(-1, 4)], pair if pair < UNITS // 2 else None)
            for n in range(-3, 1):
                whole(n)
            with eng.Fori(0, (UNITS - 6) // 2) as i:
                body(2 * i + 1, 1, [True] * 5, i + 3)
                body(2 * i + 2, 0, [True] * 5, i + 3)
            for n in range(UNITS - 5, UNITS + 1):
                whole(n)

        block = ctx.enter_context(nc.Block())

        @block.sync
        def _(sp):
            def load(n, j):
                sp.dma_start(x[:, bass.ds(n * CT, CT), :], x_dram[bass.ds(n, 1)].rearrange("s (c p) d -> p (s c) d", p=P)
                             ).then_inc(s_x[j], 16)
            for j in range(2):
                load(j, j)
            with sp.Fori(0, UNITS // 2 - 1) as i:
                for j in range(2):
                    sp.wait_ge(s_x[j], 16 * i + 16)
                    load(2 * i + 2 + j, j)
            with sp.Fori(0, UNITS) as n:
                sp.wait_ge(s_out, n + 1)
                sp.dma_start(out_dram[bass.ts(n, 1)].rearrange("s (c p) d -> p (s c) d", p=P),
                             x[:, bass.ts(n, CT), :]).then_inc(s_store, 16)
            sp.wait_ge(s_store, 16 * UNITS)

        @block.tensor
        def _(pe):
            def body(n, j, has, pair):
                e, d, c, b, a = n - 1, n, n + 1, n + 2, n + 3
                ej, dj, cj, aj = 1 - j, j, 1 - j, 1 - j
                has_e, has_d, has_c, has_b, has_a = has
                if has_d:
                    pe.wait_ge(s_cmix, d + 1)
                    if not isinstance(n, int) or n > 0:
                        pe.wait_ge(s_relu, d)
                        pe.wait_ge(s_cc, d)
                    for f in range(FC):
                        last = nc.tensor.matmul(kk_ps[:, f // 2, 256 * (f % 2):256 * (f % 2) + 256],
                                                wck[:, P * f:P * f + P], ck[dj][:, :], start=True, stop=True)
                    last.then_inc(s_kk, 1)
                if has_a:
                    pe.wait_ge(s_hn, a + 1)
                    for t in range(CT):
                        last = nc.tensor.transpose(hT_ps[:, P * t:P * t + P], hn[aj][:, t, :], C["ident"])
                    last.then_inc(s_hTp, 1)
                if has_c:
                    pe.wait_ge(s_ry, c + 1)
                    for t in range(CT):
                        last = nc.tensor.transpose(w_ps[:, P * t:P * t + P], ry[cj][:, P * t:P * t + P], C["ident"])
                    last.then_inc(s_wp, 1)
                if has_d:
                    pe.wait_ge(s_cr, d + 1)
                    for t in range(CT):
                        last = nc.tensor.matmul(cr_ps[:, P * t:P * t + P], cr[dj][:, P * t:P * t + P], wcr,
                                                start=True, stop=True)
                    last.then_inc(s_crp, 1)
                if has_e:
                    pe.wait_ge(s_kk2, 2 * e + 2)
                    if not isinstance(n, int) or e > 0:
                        pe.wait_ge(s_o, e)
                    for t in range(CT):
                        for f in range(FC):
                            last = nc.tensor.matmul(kv_ps[:, P * t:P * t + P], kk[ej][:, f, P * t:P * t + P], wcv[:, f, :],
                                                    start=(f == 0), stop=(f == FC - 1))
                    last.then_inc(s_kv, 1)
                if has_c:
                    pe.wait_ge(s_h2, c + 1)
                    for t in range(CT):
                        last = nc.tensor.transpose(h2T_ps[:, P * t:P * t + P], h2[cj][:, t, :], C["ident"])
                    last.then_inc(s_h2Tp, 1)
                if has_a:
                    pe.wait_ge(s_mix, a + 1)
                    if has_b:
                        pe.wait_ge(s_mu, b + 1)
                        pe.wait_ge(s_rc, b + 1)
                        pe.wait_ge(s_vs, b + 1)
                    nc.tensor.matmul(k_ps, wk, xk[aj][:, :], start=True, stop=True)
                    nc.tensor.matmul(v_ps, wv, xv[aj][:, :], start=True, stop=True)
                    nc.tensor.matmul(r_ps, wr, xr[aj][:, :], start=True, stop=True).then_inc(s_kvr, 1)

            bodies(pe, body)

        @block.scalar
        def _(act):
            in_b, in_d = Chain(act, c_act_b), Chain(act, c_act_d)

            def body(n, j, has, pair):
                e, d, c, b, a = n - 1, n, n + 1, n + 2, n + 3
                ej, dj, cj, bj, aj = 1 - j, j, 1 - j, j, 1 - j
                has_e, has_d, has_c, has_b, has_a = has
                in_b.enter(b * ACT_B)
                in_d.enter(d * ACT_D)
                if has_b:
                    act.wait_ge(s_kvr, b + 1)
                    nc.scalar.activation(vs[bj][:, :], v_ps, ACT.Copy).then_inc(s_vs, 1)
                if has_a:
                    wait_apart(act, apart, s_n12, pair_of(a, pair) + 1)
                    for t in range(CT):
                        at = CT * aj + t
                        last = nc.scalar.activation(hn[aj][:, t, :], x[:, a * CT + t, :], ACT.Identity,
                                                    scale=rs12[:, at:at + 1], bias=nm12[:, at:at + 1])
                    last.then_inc(s_hn, 1)
                if has_b:
                    act.wait_ge(s_mu, b + 1)
                    nc.scalar.activation(X[bj][:, :], muc[bj][:, :], ACT.Exp)
                    nc.scalar.activation(Xi[bj][:, :], muc[bj][:, :], ACT.Exp, scale=-1.0).then_inc(s_X, 1)
                if has_d:
                    act.wait_ge(s_kk, d + 1)
                    nc.scalar.activation(rk[dj][:, :, :].rearrange("p f t -> p (f t)"), kk_ps.rearrange("p b t -> p (b t)"),
                                         ACT.Relu).then_inc(s_relu, 1)
                if has_a:
                    act.wait_ge(s_hTp, a + 1)
                    nc.scalar.activation(hT[aj][:, 1:L + 1], hT_ps, ACT.Identity, bias=ln1b, scale=ln1g).then_inc(s_hT, 1)
                if has_b:
                    act.wait_ge(s_Q, b + 1)
                    nc.scalar.activation(lnQ[bj][:, :], Q[bj][:, 0:L], ACT.Ln).then_inc(s_lnQ, 1)
                if has_b:
                    act.wait_ge(s_lam, b + 1)
                    in_b.mark(nc.scalar.activation(Gi[bj][:, :], lam[bj][:, :], ACT.Exp, scale=-1.0))
                    nc.scalar.activation(G[bj][:, :], lam[bj][:, :], ACT.Exp).then_inc(s_G, 1)
                    in_b.need(1)
                    in_b.link(nc.scalar.activation(lw[bj][:, :], Gi[bj][:, :], ACT.Ln, bias=1.0, scale=U[:, :]))
                    nc.scalar.activation(sw[bj][:, :], lw[bj][:, :], ACT.Exp, scale=-1.0).then_inc(s_sw, 1)
                if has_c:
                    act.wait_ge(s_nm, c + 1)
                    for t in range(CT):
                        last = nc.scalar.activation(h2[cj][:, t, :], xp[cj][:, t, :], ACT.Identity,
                                                    scale=rst[cj][:, t:t + 1], bias=nm[cj][:, t:t + 1])
                    last.then_inc(s_h2, 1)
                if has_a:
                    if not isinstance(n, int) or n > -2:
                        wait_apart(act, apart, s_st, a - 1)
                    wait_apart(act, apart, s_n1, pair_of(a, pair) + 1)
                    for t in range(CT):
                        at = CT * aj + t
                        last = nc.scalar.activation(u[aj][:, t, :], x[:, a * CT + t, :], ACT.Identity,
                                                    scale=rs1u[:, at:at + 1], bias=nm1[:, at:at + 1])
                    last.then_inc(s_u, 1)
                if has_c:
                    act.wait_ge(s_h2Tp, c + 1)
                    nc.scalar.activation(h2T[cj][:, 1:L + 1], h2T_ps, ACT.Identity, bias=ln2b, scale=ln2g
                                         ).then_inc(s_h2T, 1)
                if has_d:
                    act.wait_ge(s_cc, d + 1)
                    in_d.mark(nc.scalar.activation(ce[dj][:, :], cc[dj][:, :], ACT.Exp, scale=-1.0))
                if has_b:
                    act.wait_ge(s_rc, b + 1)
                    in_b.mark(nc.scalar.activation(re[bj][:, :], rc[bj][:, :], ACT.Exp, scale=-1.0))
                if has_d:
                    in_d.need(1)
                    in_d.mark(nc.scalar.activation(cl[dj][:, :], ce[dj][:, :], ACT.Ln, bias=1.0))
                if has_b:
                    in_b.need(3)
                    in_b.mark(nc.scalar.activation(rl[bj][:, :], re[bj][:, :], ACT.Ln, bias=1.0))
                if has_d:
                    in_d.need(2)
                    nc.scalar.activation(sc[dj][:, :], cl[dj][:, :], ACT.Exp, scale=-1.0).then_inc(s_sc, 1)
                if has_b:
                    in_b.need(4)
                    nc.scalar.activation(sr[bj][:, :], rl[bj][:, :], ACT.Exp, scale=-1.0).then_inc(s_sr, 1)

            act.preload_act_table_set(EXP_LN)
            nc.scalar.activation(U[:, :], first, ACT.Exp).then_inc(s_U, 1)
            act.wait_ge(s_U, 1)
            bodies(act, body)

        @block.gpsimd
        def _(pool):
            in_c, in_s = Chain(pool, c_pool, apart), Chain(pool, c_pool_s, apart)
            G_ = nc.gpsimd

            def rstd1(pair):
                in_s.enter(pair)
                wait_apart(pool, apart, s_smv, pair + 1)
                in_s.link(G_.tensor_scalar(sve[:, :], smv[:, :, 1], EPS, None, ALU.add))
                G_.tensor_tensor(rs1[:, :], sve[:, :], C["neg_half"][:, 0:TWO], ALU.pow).then_inc(s_rs1, 1)

            def square(dj, f):
                part = rk[dj][:, f:f + FC // 2, :]
                G_.tensor_tensor(kk[dj][:, f:f + FC // 2, :], part, part, ALU.mult).then_inc(s_kk2, 1)

            def rstd2(pair):
                pool.wait_ge(s_var2, pair + 1)
                G_.tensor_tensor(rs2[:, :], t1[:, :], C["neg_half"][:, 0:TWO], ALU.pow).then_inc(s_rs2, 1)

            def body(n, j, has, pair):
                e, d, c, b, a = n - 1, n, n + 1, n + 2, n + 3
                ej, dj, cj = 1 - j, j, 1 - j
                has_e, has_d, has_c, has_b, has_a = has
                in_c.enter(c * POOL_C)
                if has_c:
                    pool.wait_ge(s_d2, c + 1)
                    pool.wait_ge(s_vs, c + 1)
                    in_c.link(G_.tensor_tensor(yv[cj][:, :], d2[cj][:, :], vs[cj][:, :], ALU.add))
                    wait_apart(pool, apart, s_sr, c + 1)
                    G_.tensor_tensor(ry[cj][:, :], yv[cj][:, :], sr[cj][:, :], ALU.mult).then_inc(s_ry, 1)
                if has_d:
                    pool.wait_ge(s_relu, d + 1)
                    square(dj, 0)
                if has_c:
                    wait_apart(pool, apart, s_st, c + 1)
                    in_c.link(G_.tensor_scalar(ve[cj][:, :], mv[cj][:, :, 1], EPS, None, ALU.add))
                    G_.tensor_tensor(rst[cj][:, :], ve[cj][:, :], C["neg_half"][:, 0:CT], ALU.pow).then_inc(s_rst, 1)
                if has_d:
                    square(dj, FC // 2)
                if has_e:
                    pool.wait_ge(s_o, e + 1)
                    wait_apart(pool, apart, s_xs, e + 1)
                    G_.tensor_tensor(x[:, bass.ds(e * CT, CT), :], o[ej][:, :, :], xs[ej][:, :, :], ALU.add
                                     ).then_inc(s_out, 1)
                if has_c:
                    if has_e:
                        pool.wait_ge(s_out, c - 1)
                    G_.tensor_tensor(xs[cj][:, :, :], xp[cj][:, :, :], x[:, bass.ds(c * CT, CT), :], ALU.add
                                     ).then_inc(s_xs, 1)
                if pair is not None:
                    if j == 1:
                        rstd1(pair)
                    else:
                        rstd2(pair)

            for j in range(2):
                G_.memset(hT[j][:, 0:1], 0.0)
                G_.memset(h2T[j][:, 0:1], 0.0)
                G_.memset(m[j][:, 0:1], -1e38)
                G_.memset(Q[j][:, 0:1], 1.0)
                last = G_.memset(wkv[j][:, 0:1], 0.0)
            last.then_inc(s_set, 1)
            rstd1(0)
            rstd2(0)
            bodies(pool, body)

        @block.vector
        def _(dve):
            even, odd = Chain(dve, c_even), Chain(dve, c_odd)
            in_a, in_b, in_c = Chain(dve, c_a), Chain(dve, c_b), Chain(dve, c_c)
            V = nc.vector

            def statistics(pair):
                even.enter(pair * DVE_EVEN)
                for j in range(2):
                    dve.wait_ge(s_x[j], 16 * pair + 16)
                    for t in range(CT):
                        last = even.mark(V.bn_stats(sst[:, CT * j + t, :], x[:, pair * 2 * CT + CT * j + t, :]))
                even.need(last, apart)
                for t in range(TWO):
                    last = V.bn_aggr(smv[:, t, :], sst[:, t, :])
                last.then_inc(s_smv, 1)
                even.leave(DVE_EVEN)

            def second_variance(pair):
                odd.enter(pair * DVE_ODD)
                dve.wait_ge(s_rs1, pair + 1)
                odd.link(V.tensor_tensor(t1[:, :], smv[:, :, 1], rs1[:, :], ALU.mult))
                odd.link(V.tensor_tensor(t2[:, :], t1[:, :], rs1[:, :], ALU.mult))
                V.tensor_scalar(t1[:, :], t2[:, :], EPS, None, ALU.add).then_inc(s_var2, 1)
                odd.leave(DVE_ODD)

            def norm12(pair):
                dve.wait_ge(s_rs2, pair + 1)
                V.tensor_tensor(rs12[:, :], rs1[:, :], rs2[:, :], ALU.mult).then_inc(s_r12, 1)
                dve.wait_ge(s_r12, pair + 1)
                V.scalar_tensor_tensor(nm12[:, :], smv[:, :, 0], -1.0, rs12[:, :], ALU.mult, ALU.mult).then_inc(s_n12, 1)

            def norm1(pair):
                V.tensor_copy(rs1u[:, :], rs1[:, :])
                V.scalar_tensor_tensor(nm1[:, :], smv[:, :, 0], -1.0, rs1[:, :], ALU.mult, ALU.mult).then_inc(s_n1, 1)

            def body(n, j, has, pair):
                e, d, c, b, a = n - 1, n, n + 1, n + 2, n + 3
                ej, dj, cj, bj, aj = 1 - j, j, 1 - j, j, 1 - j
                has_e, has_d, has_c, has_b, has_a = has
                in_a.enter(a * DVE_A)
                in_b.enter(b * DVE_B)
                in_c.enter(c * DVE_C)
                if has_c:
                    dve.wait_ge(c_b, (c + 1) * DVE_B)
                    in_c.mark(V.tensor_tensor(d1[cj][:, :], wkv[cj][:, 0:L], vs[cj][:, :], ALU.subtract))
                if has_b:
                    dve.wait_ge(s_kvr, b + 1)
                    in_b.mark(V.tensor_tensor_scan(m[bj][:, 1:L + 1], k_ps, decay.to_broadcast([P, L]), -1e38, ALU.max,
                                                   ALU.add))
                if has_c:
                    in_c.need(1)
                    dve.wait_ge(s_sw, c + 1)
                    V.tensor_tensor(d2[cj][:, :], d1[cj][:, :], sw[cj][:, :], ALU.mult).then_inc(s_d2, 1)
                if has_b:
                    in_b.need(1)
                    in_b.mark(V.tensor_tensor(mu[bj][:, :], m[bj][:, 0:L], k_ps, ALU.subtract))
                    in_b.need(2)
                    V.tensor_scalar(muc[bj][:, :], mu[bj][:, :], LIM, -LIM, ALU.min, ALU.max).then_inc(s_mu, 1)
                    V.tensor_scalar(rc[bj][:, :], r_ps, -SIG_CLAMP, None, ALU.max).then_inc(s_rc, 1)
                if has_d:
                    V.scalar_tensor_tensor(cr[dj][:, :], dh2[dj][:, :], cmixr, h2T[dj][:, 0:L], ALU.mult, ALU.add
                                           ).then_inc(s_cr, 1)
                if has_a and j == 1:
                    if not isinstance(n, int) or n > -3:
                        dve.wait_ge(s_u, a)
                    norm1(pair_of(a, pair))
                if has_b:
                    dve.wait_ge(s_X, b + 1)
                    in_b.mark(V.tensor_scalar(e1[bj][:, :], X[bj][:, :], 1.0, None, ALU.min))
                    in_b.link(V.tensor_scalar(e2[bj][:, :], Xi[bj][:, :], 1.0, None, ALU.min))
                    V.tensor_tensor_scan(Q[bj][:, 1:L + 1], e1[bj][:, :], e2[bj][:, :], 1.0, ALU.mult, ALU.add
                                         ).then_inc(s_Q, 1)
                if has_c:
                    dve.wait_ge(s_wp, c + 1)
                    dve.wait_ge(s_u, c + 1)
                    summed = in_c.mark(V.tensor_tensor(xp[cj][:, :, :], tiles(w_ps), u[cj][:, :, :], ALU.add))
                if has_a:
                    dve.wait_ge(s_hT, a + 1)
                    now, before = hT[aj][:, 1:L + 1], hT[aj][:, 0:L]
                    in_a.mark(V.tensor_tensor(dh[aj][:, :], now, before, ALU.subtract))
                if has_c:
                    in_c.need(summed)
                    for t in range(CT):
                        last = in_c.mark(V.bn_stats(st[cj][:, t, :], xp[cj][:, t, :]))
                if has_b:
                    dve.wait_ge(s_lnQ, b + 1)
                    V.tensor_tensor(lam[bj][:, :], muc[bj][:, :], lnQ[bj][:, :], ALU.add).then_inc(s_lam, 1)
                if has_c:
                    in_c.need(last, apart)
                    for t in range(CT):
                        last = V.bn_aggr(mv[cj][:, t, :], st[cj][:, t, :])
                    last.then_inc(s_st, 1)
                if has_a:
                    in_a.need(1)
                    V.scalar_tensor_tensor(xk[aj][:, :], dh[aj][:, :], mixk, before, ALU.mult, ALU.add)
                    V.scalar_tensor_tensor(xv[aj][:, :], dh[aj][:, :], mixv, before, ALU.mult, ALU.add)
                    V.scalar_tensor_tensor(xr[aj][:, :], dh[aj][:, :], mixr, before, ALU.mult, ALU.add).then_inc(s_mix, 1)
                if has_c:
                    dve.wait_ge(s_rst, c + 1)
                    V.scalar_tensor_tensor(nm[cj][:, :], mv[cj][:, :, 0], -1.0, rst[cj][:, :], ALU.mult, ALU.mult
                                           ).then_inc(s_nm, 1)
                if has_e:
                    dve.wait_ge(s_kv, e + 1)
                    dve.wait_ge(s_sc, e + 1)
                    V.tensor_tensor(o[ej][:, :, :], tiles(kv_ps), tiles(sc[ej][:, :]), ALU.mult).then_inc(s_o, 1)
                if has_d:
                    dve.wait_ge(s_crp, d + 1)
                    V.tensor_scalar(cc[dj][:, :], cr_ps, -SIG_CLAMP, None, ALU.max).then_inc(s_cc, 1)
                if has_b:
                    dve.wait_ge(s_G, b + 1)
                    in_b.mark(V.tensor_scalar(al[bj][:, :], G[bj][:, :], 1.0, None, ALU.min))
                    in_b.link(V.scalar_tensor_tensor(bv[bj][:, :], Gi[bj][:, :], 1.0, vs[bj][:, :], ALU.min, ALU.mult))
                    in_b.mark(V.tensor_tensor_scan(wkv[bj][:, 1:L + 1], al[bj][:, :], bv[bj][:, :], 0.0, ALU.mult, ALU.add))
                if pair is not None:
                    if j == 1:
                        statistics(pair)
                    else:
                        second_variance(pair)
                if has_c:
                    dve.wait_ge(s_h2T, c + 1)
                    now, before = h2T[cj][:, 1:L + 1], h2T[cj][:, 0:L]
                    in_c.link(V.tensor_tensor(dh2[cj][:, :], now, before, ALU.subtract))
                    V.scalar_tensor_tensor(ck[cj][:, :], dh2[cj][:, :], cmixk, before, ALU.mult, ALU.add).then_inc(s_cmix, 1)
                if pair is not None and j == 0:
                    norm12(pair)

            dve.wait_ge(s_set, 1)
            statistics(0)
            second_variance(0)
            norm12(0)
            bodies(dve, body)


def ffn_state(nc, ctx):
    t = lambda name, shape, dt=F32: ctx.enter_context(nc.sbuf_tensor("ffn_" + name, shape, dt))
    all_weights, weights = weights_side_by_side(nc, ctx, "ffn")
    return dict(weights=weights, all_weights=all_weights, w2=t("w2", [P, EXPERTS * DF // P * D]),
                tables=t("tables", [1, 2 * BLOCKS + EXPERTS], I32), pads=t("pads", [P, EXPERTS, ROW]),
                strict16=t("strict16", [P, P], BF16), ones16=t("ones16", [P, P], BF16), mask=t("mask", [P, 8, 32]),
                q_spread=[t(f"q_spread{j}", [P, 16, 4, 16]) for j in range(2)],
                probs_spread=[t(f"probs_spread{j}", [P, 2, 4, P]) for j in range(2)],
                scratch_rows=nc.dram_tensor("scratch_rows", [ROWS, ROW], F32, kind="Internal").ap())


def start_of_program(nc, io, C, F):
    with nc.Block() as block:
        @block.sync
        def _(sp):
            sp.dma_start(C["tensor"][:, :], io["consts"]).then_inc(C["loaded"], C["loads"])

        @block.gpsimd
        def _(pool):
            for j in range(2):
                nc.gpsimd.memset(F["q_spread"][j][:, :, :, :], 0.0)
                nc.gpsimd.memset(F["probs_spread"][j][:, :, :, :], 0.0)


def later_weights_loader(io, F, rwkv_weights, loaded):
    def start(eng):
        spare = F["scratch_rows"][EXPERTS * REGION:ROWS, :].rearrange("(b p) d -> p b d", p=P)
        for dst, src in ((F["all_weights"][:, :], io["ffn_weights"]), (F["w2"][:, :], io["w2"]),
                         (F["pads"][:, :, :], io["pads"][:, 0:EXPERTS, :]), (spare, io["pads"][:, EXPERTS:2 * EXPERTS, :]),
                         (rwkv_weights[:, :], io["rwkv_weights"])):
            eng.dma_start(dst, src).then_inc(loaded, 16)
    return start, 5 * 16


def behind_the_first_layer(nc, C, F, loaded, loads):
    with nc.Block() as block:
        @block.sync
        def _(sp):
            sp.wait_ge(loaded, loads)

        @block.vector
        def _(dve):
            nc.vector.tensor_copy(F["strict16"][:, :], C["strict"])
            nc.vector.tensor_copy(F["ones16"][:, :], C["ones"][:, 0:P])
            nc.vector.tensor_copy(F["mask"][:, :, :], C["pairmask"].unsqueeze(1).to_broadcast([P, 8, 32]))


def hybrid_layers(nc, io, out_rows):
    with ExitStack() as ctx:
        C = load_consts(nc, ctx, io)
        F = ffn_state(nc, ctx)
        x1, x3 = (nc.dram_tensor(name, [SEQ, L, D], F32, kind="Internal").ap() for name in ("x1", "x3"))
        x2_rows = nc.dram_tensor("x2_rows", [RESULTS, D], F32, kind="Internal").ap()
        x2 = x2_rows[0:SEQ * L].rearrange("(s l) d -> s l d", l=L)
        rwkv_all_weights, rwkv_weights = weights_side_by_side(nc, ctx, "rwkv")
        loaded = ctx.enter_context(nc.semaphore("later_weights_loaded"))
        load_later_weights, loads = later_weights_loader(io, F, rwkv_all_weights, loaded)
        start_of_program(nc, io, C, F)
        gla_phase(nc, io, C, io["x"], x1, load_later_weights)
        behind_the_first_layer(nc, C, F, loaded, loads)
        ffn_attention(nc, C, F, x1, "att1_")
        ffn_experts(nc, io, C, F, x2_rows, "experts1_")
        rwkv_phase(nc, C, rwkv_weights, x2, x3)
        ffn_attention(nc, C, F, x3, "att2_")
        ffn_experts(nc, io, C, F, out_rows, "experts2_")


def laid_out(inputs):
    a = {k[len("L0_attn_a_"):]: v for k, v in inputs.items() if k.startswith("L0_attn_a_")}
    b = {k[len("L0_attn_b_"):]: v for k, v in inputs.items() if k.startswith("L0_attn_b_")}
    f = {k[len("L0_ffn_"):]: v for k, v in inputs.items() if k.startswith("L0_ffn_")}
    fc = DF // P
    w1b = np.concatenate([f["W1"].transpose(1, 0, 2), f["b1"].reshape(EXPERTS, fc, P).transpose(2, 0, 1),
                          np.broadcast_to(f["b2"][None], (P, EXPERTS, D))], 2).transpose(1, 0, 2)
    rows = ("ln1_g", "ln1_b", "ln2_g", "ln2_b", "mix_k", "mix_v", "mix_r", "cmix_k", "cmix_r", "time_decay",
            "time_first")
    wide = lambda v: np.broadcast_to(v[None], (P, D))
    rows16 = lambda v: np.concatenate([v, np.zeros((P - len(v), v.shape[1]), v.dtype)], 0)
    gla = {"Wqk": np.concatenate([a["Wq"], a["Wk"]], 1), "Wvg": np.concatenate([a["Wv"], a["Wg"]], 1),
           "Wo": a["Wo"].reshape(2, P, D).transpose(1, 0, 2).reshape(P, 2 * D), "gk_w1T": rows16(a["gk_w1"].T),
           "gk_w2": rows16(a["gk_w2"]), "g_norm_col": np.tile(a["g_norm_w"], 2)[:, None], "gk_b2_col": a["gk_b2"][:, None]}
    ffn = {"WqT": f["Wqkv"][0:P].T, "WkT": f["Wqkv"][P:2 * P].T, "WvT": f["Wqkv"][2 * P:3 * P].T, "WoT": f["Wo"].T,
           "WgT": f["Wg"].T, "bq": f["bqkv"][0:P, None], "bk": f["bqkv"][P:2 * P, None],
           "bv": f["bqkv"][2 * P:3 * P, None], **{k: wide(f[k]) for k in ("bo", "g1", "be1", "g2", "be2")}}
    rwkv = {"w_tk": b["w_tk"], "w_tv": b["w_tv"], "w_tr": b["w_tr"], "w_cr": b["w_cr"], "w_ck": b["w_ck"],
            "w_cv": b["w_cv"].reshape(fc, P, D).transpose(1, 0, 2).reshape(P, DF),
            "rwkv_cols": np.stack([b[k].reshape(-1) for k in rows], 1)}
    side_by_side = lambda layer, parts: np.concatenate([parts[k] for k in WEIGHTS[layer]], 1)
    io = {
        "x": a["x"], "consts": const_array(),
        "w1b": w1b, "w2": f["W2"].reshape(EXPERTS, fc, P, D).transpose(2, 0, 1, 3).reshape(P, -1),
        "pads": pad_rows(),
        "gla_weights": side_by_side("gla", gla), "ffn_weights": side_by_side("ffn", ffn), "rwkv_weights": side_by_side("rwkv", rwkv),
    }
    return {k: np.ascontiguousarray(v) for k, v in io.items()}


def kernel(**inputs):
    import concourse.bacc as bacc
    from concourse.bass_utils import run_bass_kernel_spmd

    nc = bacc.Bacc("TRN2", target_bir_lowering=False, num_devices=1)
    arrays, io = {}, {}
    for name, array in laid_out({k: np.asarray(v) for k, v in inputs.items()}).items():
        arrays[f"in_{name}_dram"] = array
        io[name] = nc.dram_tensor(f"in_{name}_dram", array.shape, mybir.dt.from_np(array.dtype),
                                  kind="ExternalInput").ap()
    out = nc.dram_tensor("out_0_dram", [RESULTS, D], F32, kind="ExternalOutput").ap()
    hybrid_layers(nc, io, out)
    result = run_bass_kernel_spmd(nc, [arrays], core_ids=[0])
    return result.results[0]["out_0_dram"][:SEQ * L].reshape(SEQ, L, D)
```
